# Optimizing a Trainium2 kernel written in Bass

```python
import numpy as np
import jax
import jax.numpy as jnp

def _softmax(x, axis=-1):
    return jax.nn.softmax(x, axis=axis)

def _gelu(x):
    return jax.nn.gelu(x, approximate=True)

def _silu(x):
    return jax.nn.silu(x)

def _sigmoid(x):
    return jax.nn.sigmoid(x)

def _layernorm(x, axis=-1, eps=1e-05):
    m = jnp.mean(x, axis=axis, keepdims=True)
    v = jnp.var(x, axis=axis, keepdims=True)
    return (x - m) / jnp.sqrt(v + eps)

def _scatter_add(tgt, idx, src, axis=0):
    return tgt.at[idx].add(src)

def _segment_sum(src, seg, n):
    return jax.ops.segment_sum(src, seg, n)
kernel_name = 'mk_perceiver_d1_seqx_r4_7b1e54'

def setup_inputs(seed: int=0):
    np.random.seed(seed)
    _w = jnp.asarray

    def _rec_inputs():
        import jax
        import jax.numpy as jnp
        _rk = jax.random.key(seed)
        x = 7.22e-05 + 1 * jax.random.normal(jax.random.fold_in(_rk, 1), (32, 32, 256), jnp.float32)
        _lenS = 32 - jax.random.randint(jax.random.fold_in(_rk, 7), (32,), 0, max(1, 32 // 4) + 1, jnp.int32)
        _lenS2 = 257 - jax.random.randint(jax.random.fold_in(_rk, 8), (32,), 0, max(1, 257 // 4) + 1, jnp.int32)
        _ctx_1024P = jax.random.normal(jax.random.fold_in(_rk, 11), (32, 16, 256), jnp.float32)
        _ctx_1024c = jax.random.dirichlet(jax.random.fold_in(_rk, 511), 0.3 * jnp.ones((16,), jnp.float32), (32, 257))
        _ctx_1024t = jnp.einsum('bsk,bkd->bsd', _ctx_1024c, _ctx_1024P)
        _ctx_1024t = _ctx_1024t * jax.lax.rsqrt(jnp.mean(jnp.square(_ctx_1024t)) + 1e-12) * 0.953939
        ctx_1024 = 4.13588e-05 + 0.999923 * (_ctx_1024t + 0.3 * jax.random.normal(jax.random.fold_in(_rk, 611), (32, 257, 256), jnp.float32))
        _validS = jnp.arange(32)[None, :] < _lenS[:, None]
        _validS2 = jnp.arange(257)[None, :] < _lenS2[:, None]
        _causal = jnp.tril(jnp.ones((32, 32), dtype=bool))
        mask_1x1xSxS2_ik1 = jnp.where(jnp.broadcast_to(_validS2[0:1, None, None, :], (1, 1, 32, 257)), 1, 0).astype(jnp.int32)
        return (x, ctx_1024, mask_1x1xSxS2_ik1)
    x, ctx_1024, mask_1x1xSxS2_ik1 = _rec_inputs()

    def _L0_xattn_setup():
        import jax, jax.numpy as jnp
        import numpy as np
        D_MODEL = 256
        NUM_HEADS = 16
        HEAD_DIM = D_MODEL // NUM_HEADS
        B, S = (4, 512)
        key = jax.random.key(seed)
        ks = jax.random.split(key, 12)
        scale = 1.0 / np.sqrt(D_MODEL)
        inp = {'query': jax.random.normal(ks[0], (B, S, D_MODEL), jnp.float32), 'key': jax.random.normal(ks[1], (B, S, D_MODEL), jnp.float32), 'value': jax.random.normal(ks[2], (B, S, D_MODEL), jnp.float32), 'mask': jax.random.randint(ks[3], (1, 1, S, S), 0, 2, jnp.int32), 'Wq': jax.random.normal(ks[4], (D_MODEL, D_MODEL), jnp.float32) * scale, 'bq': jnp.zeros((D_MODEL,), jnp.float32), 'Wk': jax.random.normal(ks[5], (D_MODEL, D_MODEL), jnp.float32) * scale, 'bk': jnp.zeros((D_MODEL,), jnp.float32), 'Wv': jax.random.normal(ks[6], (D_MODEL, D_MODEL), jnp.float32) * scale, 'bv': jnp.zeros((D_MODEL,), jnp.float32), 'Wo': jax.random.normal(ks[7], (D_MODEL, D_MODEL), jnp.float32) * scale, 'bo': jnp.zeros((D_MODEL,), jnp.float32)}
        return inp
    _L0_xattn_all = _L0_xattn_setup()
    _L0_xattn_in = {k: v for k, v in _L0_xattn_all.items() if k in ('Wq', 'bq', 'Wk', 'bk', 'Wv', 'bv', 'Wo', 'bo')}
    del _L0_xattn_all

    def _L0_attn_setup():
        import jax, jax.numpy as jnp
        import numpy as np
        NUM_HEADS = 16
        THETA = 10000.0

        def _rope(x, theta):
            S, d_k = (x.shape[1], x.shape[-1])
            k = jnp.arange(d_k // 2, dtype=jnp.float32)
            inv_freq = theta ** (-2.0 * k / d_k)
            ang = jnp.arange(S, dtype=jnp.float32)[:, None] * inv_freq
            cos = jnp.cos(ang)[None, :, None, :]
            sin = jnp.sin(ang)[None, :, None, :]
            x_even = x[..., 0::2]
            x_odd = x[..., 1::2]
            y_even = cos * x_even - sin * x_odd
            y_odd = sin * x_even + cos * x_odd
            y = jnp.stack([y_even, y_odd], axis=-1)
            return y.reshape(x.shape)
        key = jax.random.key(seed)
        ks = jax.random.split(key, 5)
        B, S, D = (2, 512, 256)
        std = 1.0 / np.sqrt(D)
        return {'in_features': jax.random.normal(ks[0], (B, S, D), dtype=jnp.float32), 'W_Q': jax.random.normal(ks[1], (D, D), dtype=jnp.float32) * std, 'W_K': jax.random.normal(ks[2], (D, D), dtype=jnp.float32) * std, 'W_V': jax.random.normal(ks[3], (D, D), dtype=jnp.float32) * std, 'W_O': jax.random.normal(ks[4], (D, D), dtype=jnp.float32) * std}
    _L0_attn_all = _L0_attn_setup()
    _L0_attn_in = {k: v for k, v in _L0_attn_all.items() if k in ('W_Q', 'W_K', 'W_V', 'W_O')}
    del _L0_attn_all

    def _L0_ffn_setup():
        import jax, jax.numpy as jnp
        import numpy as np
        B, L, M = (4, 512, 256)
        G, E = (8, 8)
        CAP_FACTOR = 2.0

        def _ffn_size(m, widening=8.0):
            f = int(widening * m) * 2 // 3
            return f + (8 - f) % 8
        H = _ffn_size(M)

        def _gating_top2(logits, C):
            Gd, Sd, Ed = logits.shape
            raw = jax.nn.softmax(logits, axis=-1)
            idx1 = jnp.argmax(raw, axis=-1)
            m1 = jax.nn.one_hot(idx1, Ed, dtype=logits.dtype)
            gate1 = jnp.sum(raw * m1, axis=-1)
            rest = raw * (1.0 - m1)
            idx2 = jnp.argmax(rest, axis=-1)
            m2 = jax.nn.one_hot(idx2, Ed, dtype=logits.dtype)
            gate2 = jnp.sum(rest * m2, axis=-1)
            p1 = jnp.cumsum(m1, axis=-2) - m1
            m1 = m1 * (p1 < C).astype(m1.dtype)
            p1 = jnp.sum(p1 * m1, axis=-1)
            m1_flat = jnp.sum(m1, axis=-1)
            m1_count = jnp.sum(m1, axis=-2)
            p2 = jnp.cumsum(m2, axis=-2) - m2 + m1_count[:, None, :]
            m2 = m2 * (p2 < C).astype(m2.dtype)
            p2 = jnp.sum(p2 * m2, axis=-1)
            m2_flat = jnp.sum(m2, axis=-1)
            gate1 = gate1 * m1_flat
            gate2 = gate2 * m2_flat
            c1 = (gate1[..., None] * jax.nn.one_hot(idx1, Ed, dtype=jnp.float32))[..., None] * jax.nn.one_hot(p1.astype(jnp.int32), C, dtype=jnp.float32)[:, :, None, :]
            c2 = (gate2[..., None] * jax.nn.one_hot(idx2, Ed, dtype=jnp.float32))[..., None] * jax.nn.one_hot(p2.astype(jnp.int32), C, dtype=jnp.float32)[:, :, None, :]
            combine = (c1 + c2).astype(logits.dtype)
            dispatch = (combine != 0).astype(logits.dtype)
            return (dispatch, combine)
        key = jax.random.key(seed)
        k0, k1, k2, k3, k4 = jax.random.split(key, 5)
        return {'inputs': jax.random.normal(k0, (B, L, M), jnp.float32), 'router_w': jax.random.normal(k1, (M, E), jnp.float32) * 0.02, 'w0_kernel': jax.random.normal(k2, (E, M, H), jnp.float32) * 0.02, 'w1_kernel': jax.random.normal(k3, (E, M, H), jnp.float32) * 0.02, 'wo_kernel': jax.random.normal(k4, (E, H, M), jnp.float32) * 0.02}
    _L0_ffn_all = _L0_ffn_setup()
    _L0_ffn_in = {k: v for k, v in _L0_ffn_all.items() if k in ('router_w', 'w0_kernel', 'w1_kernel', 'wo_kernel')}
    del _L0_ffn_all
    return {'x': x, 'ctx_1024': ctx_1024, 'mask_1x1xSxS2_ik1': mask_1x1xSxS2_ik1, 'L0_xattn_Wq': _L0_xattn_in['Wq'], 'L0_xattn_bq': _L0_xattn_in['bq'], 'L0_xattn_Wk': _L0_xattn_in['Wk'], 'L0_xattn_bk': _L0_xattn_in['bk'], 'L0_xattn_Wv': _L0_xattn_in['Wv'], 'L0_xattn_bv': _L0_xattn_in['bv'], 'L0_xattn_Wo': _L0_xattn_in['Wo'], 'L0_xattn_bo': _L0_xattn_in['bo'], 'L0_attn_W_Q': _L0_attn_in['W_Q'], 'L0_attn_W_K': _L0_attn_in['W_K'], 'L0_attn_W_V': _L0_attn_in['W_V'], 'L0_attn_W_O': _L0_attn_in['W_O'], 'L0_ffn_router_w': _L0_ffn_in['router_w'], 'L0_ffn_w0_kernel': _L0_ffn_in['w0_kernel'], 'L0_ffn_w1_kernel': _L0_ffn_in['w1_kernel'], 'L0_ffn_wo_kernel': _L0_ffn_in['wo_kernel']}

def reference(x, ctx_1024, mask_1x1xSxS2_ik1, L0_xattn_Wq, L0_xattn_bq, L0_xattn_Wk, L0_xattn_bk, L0_xattn_Wv, L0_xattn_bv, L0_xattn_Wo, L0_xattn_bo, L0_attn_W_Q, L0_attn_W_K, L0_attn_W_V, L0_attn_W_O, L0_ffn_router_w, L0_ffn_w0_kernel, L0_ffn_w1_kernel, L0_ffn_wo_kernel):
    import jax
    import jax.numpy as jnp

    def _L0_xattn_ref(query, key, value, mask, Wq, bq, Wk, bk, Wv, bv, Wo, bo):
        import jax, jax.numpy as jnp
        import numpy as np
        D_MODEL = 256
        NUM_HEADS = 16
        HEAD_DIM = D_MODEL // NUM_HEADS
        B, S = (4, 512)
        b = query.shape[0]
        Q = query @ Wq.T + bq
        K = key @ Wk.T + bk
        V = value @ Wv.T + bv
        Q = Q.reshape(b, -1, NUM_HEADS, HEAD_DIM).transpose(0, 2, 1, 3)
        K = K.reshape(b, -1, NUM_HEADS, HEAD_DIM).transpose(0, 2, 1, 3)
        V = V.reshape(b, -1, NUM_HEADS, HEAD_DIM).transpose(0, 2, 1, 3)
        energy = jnp.einsum('bhqd,bhkd->bhqk', Q, K) / np.sqrt(HEAD_DIM).astype(np.float32)
        energy = jnp.where(mask == 0, jnp.float32(-1e+20), energy)
        attention = jax.nn.softmax(energy, axis=-1)
        x = jnp.einsum('bhqk,bhkd->bhqd', attention, V)
        x = x.transpose(0, 2, 1, 3).reshape(b, -1, D_MODEL)
        return x @ Wo.T + bo

    def _L0_attn_ref(in_features, W_Q, W_K, W_V, W_O):
        import jax, jax.numpy as jnp
        import numpy as np
        NUM_HEADS = 16
        THETA = 10000.0

        def _rope(x, theta):
            S, d_k = (x.shape[1], x.shape[-1])
            k = jnp.arange(d_k // 2, dtype=jnp.float32)
            inv_freq = theta ** (-2.0 * k / d_k)
            ang = jnp.arange(S, dtype=jnp.float32)[:, None] * inv_freq
            cos = jnp.cos(ang)[None, :, None, :]
            sin = jnp.sin(ang)[None, :, None, :]
            x_even = x[..., 0::2]
            x_odd = x[..., 1::2]
            y_even = cos * x_even - sin * x_odd
            y_odd = sin * x_even + cos * x_odd
            y = jnp.stack([y_even, y_odd], axis=-1)
            return y.reshape(x.shape)
        B, S, D = in_features.shape
        H = NUM_HEADS
        d_k = D // H
        scale = 1.0 / np.sqrt(np.float32(d_k))
        q = jnp.einsum('kd,bsd->bsk', W_Q, in_features).reshape(B, S, H, d_k)
        k = jnp.einsum('kd,bsd->bsk', W_K, in_features).reshape(B, S, H, d_k)
        v = jnp.einsum('vd,bsd->bsv', W_V, in_features).reshape(B, S, H, d_k)
        q = _rope(q, THETA)
        k = _rope(k, THETA)
        q = q.transpose(0, 2, 1, 3)
        k = k.transpose(0, 2, 1, 3)
        v = v.transpose(0, 2, 1, 3)
        scores = jnp.einsum('bhqd,bhkd->bhqk', q, k) * scale
        causal = jnp.tril(jnp.ones((S, S), dtype=bool))
        scores = jnp.where(causal[None, None], scores, -jnp.inf)
        attn = jax.nn.softmax(scores, axis=-1)
        out = jnp.einsum('bhqk,bhkd->bhqd', attn, v)
        out = out.transpose(0, 2, 1, 3).reshape(B, S, D)
        return jnp.einsum('dv,bsv->bsd', W_O, out)

    def _L0_ffn_ref(inputs, router_w, w0_kernel, w1_kernel, wo_kernel):
        import jax, jax.numpy as jnp
        import numpy as np
        B, L, M = (4, 512, 256)
        G, E = (8, 8)
        CAP_FACTOR = 2.0

        def _ffn_size(m, widening=8.0):
            f = int(widening * m) * 2 // 3
            return f + (8 - f) % 8
        H = _ffn_size(M)

        def _gating_top2(logits, C):
            Gd, Sd, Ed = logits.shape
            raw = jax.nn.softmax(logits, axis=-1)
            idx1 = jnp.argmax(raw, axis=-1)
            m1 = jax.nn.one_hot(idx1, Ed, dtype=logits.dtype)
            gate1 = jnp.sum(raw * m1, axis=-1)
            rest = raw * (1.0 - m1)
            idx2 = jnp.argmax(rest, axis=-1)
            m2 = jax.nn.one_hot(idx2, Ed, dtype=logits.dtype)
            gate2 = jnp.sum(rest * m2, axis=-1)
            p1 = jnp.cumsum(m1, axis=-2) - m1
            m1 = m1 * (p1 < C).astype(m1.dtype)
            p1 = jnp.sum(p1 * m1, axis=-1)
            m1_flat = jnp.sum(m1, axis=-1)
            m1_count = jnp.sum(m1, axis=-2)
            p2 = jnp.cumsum(m2, axis=-2) - m2 + m1_count[:, None, :]
            m2 = m2 * (p2 < C).astype(m2.dtype)
            p2 = jnp.sum(p2 * m2, axis=-1)
            m2_flat = jnp.sum(m2, axis=-1)
            gate1 = gate1 * m1_flat
            gate2 = gate2 * m2_flat
            c1 = (gate1[..., None] * jax.nn.one_hot(idx1, Ed, dtype=jnp.float32))[..., None] * jax.nn.one_hot(p1.astype(jnp.int32), C, dtype=jnp.float32)[:, :, None, :]
            c2 = (gate2[..., None] * jax.nn.one_hot(idx2, Ed, dtype=jnp.float32))[..., None] * jax.nn.one_hot(p2.astype(jnp.int32), C, dtype=jnp.float32)[:, :, None, :]
            combine = (c1 + c2).astype(logits.dtype)
            dispatch = (combine != 0).astype(logits.dtype)
            return (dispatch, combine)
        Bb, Ll, Mm = inputs.shape
        S = Bb * Ll // G
        x = inputs.reshape(G, S, Mm)
        logits = jnp.einsum('GSM,ME->GSE', x, router_w)
        cap = int(CAP_FACTOR * S / E)
        C = (cap + 3) // 4 * 4
        dispatch, combine = _gating_top2(logits, C)
        expert_inputs = jnp.einsum('GSEC,GSM->EGCM', dispatch, x)
        layer_w0 = jnp.einsum('EGCM,EMH->EGCH', expert_inputs, w0_kernel)
        layer_w1 = jnp.einsum('EGCM,EMH->EGCH', expert_inputs, w1_kernel)
        hidden = jax.nn.gelu(layer_w0, approximate=True) * layer_w1
        expert_outputs = jnp.einsum('EGCH,EHM->EGCM', hidden, wo_kernel)
        out = jnp.einsum('EGCM,GSEC->GSM', expert_outputs, combine)
        return out.reshape(Bb, Ll, Mm)
    x = x + _L0_xattn_ref(_layernorm(x, axis=-1), ctx_1024, ctx_1024, mask_1x1xSxS2_ik1, L0_xattn_Wq, L0_xattn_bq, L0_xattn_Wk, L0_xattn_bk, L0_xattn_Wv, L0_xattn_bv, L0_xattn_Wo, L0_xattn_bo)
    x = x + _L0_attn_ref(_layernorm(x, axis=-1), L0_attn_W_Q, L0_attn_W_K, L0_attn_W_V, L0_attn_W_O)
    x = x + _L0_ffn_ref(_layernorm(x, axis=-1), L0_ffn_router_w, L0_ffn_w0_kernel, L0_ffn_w1_kernel, L0_ffn_wo_kernel)
    return x

_drawn_inputs = setup_inputs


def setup_inputs(seed=0):
    import zlib

    import numpy as np

    out = dict(_drawn_inputs(seed))
    spreads = {'L0_xattn_bq': (0.0, 0.339),
     'L0_xattn_bk': (0.0, 0.8),
     'L0_xattn_bv': (0.0, 0.1),
     'L0_xattn_bo': (0.0, 0.1)}
    factors = {'L0_ffn_router_w': 8.0,
     'L0_ffn_w0_kernel': 7.943,
     'L0_ffn_w1_kernel': 7.736,
     'L0_ffn_wo_kernel': 7.736}
    for name, (base, spread) in spreads.items():
        noise = np.random.default_rng([zlib.crc32(name.encode()), seed]).standard_normal(out[name].shape)
        drawn = base * np.exp(spread * noise) if base else spread * noise
        out[name] = jnp.asarray(drawn.astype(out[name].dtype))
    for name, factor in factors.items():
        out[name] = (out[name] * factor).astype(out[name].dtype)
    return out
```

```python
from contextlib import ExitStack

import concourse.bass as bass
from concourse import mybir

F32 = mybir.dt.float32
F32R = mybir.dt.float32r
I32 = mybir.dt.int32
ALU = mybir.AluOpType
ACT = mybir.ActivationFunctionType
X = mybir.AxisListType.X

P = 128
B, S, D = 32, 32, 256
SC = 257
NH, DH = 16, 16
KH = D // P
BT = P // S
TT = B // BT
HG = P // S
G = NH // HG
E, CAP = 8, 32
HF = 1368
HT = -(-HF // P)
SL = TT * CAP
SP_ = SL // P
EPS = 1e-5
MASKED = -1e20
NC_ = 128 + 128 + 16 + 8 + 8 + 32 + 4 + 8 + 32


def constants():
    import numpy as np

    p = np.arange(P)
    ident = np.eye(P)
    before = (p[:, None] < p[None, :])
    freq = np.float32(10000.0) ** (np.float32(-2.0) * np.arange(DH // 2, dtype=np.float32) / np.float32(DH))
    angle = (p % S).astype(np.float32)[:, None] * freq
    cos, sin = np.cos(angle), np.sin(angle)
    causal = np.where(np.arange(S)[None, :] <= (p % S)[:, None], 0.0, -1e30)
    block = (p % 64)[:, None] // DH == np.arange(HG)
    expert = np.broadcast_to(np.arange(E) - E, (P, E))
    slot = np.broadcast_to(np.arange(CAP), (P, CAP))
    parts = [ident, before, np.repeat(cos, 2, 1), sin, -sin, causal, block, expert, slot]
    table = np.concatenate([np.asarray(t, np.float32) for t in parts], 1)
    assert table.shape == (P, NC_)
    return table


def build(nc, x, ctx_in, mask, weights, xbq, xbk, xbv, xbo, router, w0, w1, wo, table, out):
    with ExitStack() as stack:
        program(nc, stack, x, ctx_in, mask, weights, xbq, xbk, xbv, xbo, router, w0, w1, wo, table, out)


def program(nc, stack, x, ctx_in, mask, weights, xbq, xbk, xbv, xbo, router, w0, w1, wo, table, out):
    def sb(name, shape, dt=F32, scope=stack):
        return scope.enter_context(nc.sbuf_tensor(name, shape, dt))

    def f(ap):
        return ap.bitcast(F32)

    tab = sb("tab", [P, NC_])
    at = [0]

    def column(n):
        at[0] += n
        return tab[:, at[0] - n:at[0]]

    ident, before = column(P), column(P)
    cos16, sin8, nsin8 = column(DH), column(DH // 2), column(DH // 2)
    causal, block, expert_no, slot_no = column(S), column(HG), column(E), column(CAP)
    ones = sb("ones", [P, P])
    half = sb("half", [P, TT])
    WT_hi = sb("WT_hi", [P, 8, KH, D], F32R)
    WT_lo = sb("WT_lo", [P, 8, KH, D], F32R)
    x_sb = sb("x_sb", [P, TT, D])
    O_all = sb("O_all", [P, TT, D])
    stat_all = sb("stat_all", [P, TT, NH, 2])
    VL_all = sb("VL_all", [P, TT, D])
    bias_col = sb("bias_col", [P, 3 * KH])
    bq_col, bk_col, bv_col = (bias_col[:, KH * i:KH * i + KH] for i in range(3))
    bo_row = sb("bo_row", [P, D])
    router_sb = sb("router_sb", [P, KH, E])
    raw01 = sb("raw01", [P, 2, KH, HF])
    raw2 = sb("raw2", [P, HT, D])

    early = ExitStack()
    mask_i = sb("mask_i", [P, SC], I32, early)
    mask_add = sb("mask_add", [P, SC], scope=early)
    QT = sb("QT", [P, KH, TT * P], scope=early)
    KLT = sb("KLT", [P, KH, B], scope=early)
    ctx_raw = sb("ctx_raw", [P, 4, KH, D], scope=early)
    prep = ExitStack()
    w_raw = sb("w_raw", [P, 8, KH, D], scope=prep)
    bias_raw = sb("bias_raw", [3 * KH, P], scope=prep)
    xn = sb("xn", [P, TT, D], scope=prep)
    bn = sb("bn", [P, TT, 6], scope=prep)
    mv = sb("mv", [P, TT, 2], scope=prep)
    rstd = sb("rstd", [P, TT], scope=prep)
    xnT_hi = sb("xnT_hi", [P, KH, TT * P], F32R, prep)
    xnT_lo = sb("xnT_lo", [P, KH, TT * P], F32R, prep)
    last_raw = sb("last_raw", [B, D], scope=prep)
    lastT_hi = sb("lastT_hi", [P, KH, B, S], F32R, prep)
    lastT_lo = sb("lastT_lo", [P, KH, B, S], F32R, prep)
    prep.close()
    ctxT_hi = sb("ctxT_hi", [P, 2, KH, 2 * P], F32R, early)
    ctxT_lo = sb("ctxT_lo", [P, 2, KH, 2 * P], F32R, early)
    KT = sb("KT", [P, 2, KH, SC + 1], scope=early)
    V = sb("V", [P, 4, 2, D], scope=early)
    Qb = sb("Qb", [P, 2, KH, HG, S], scope=early)
    Sc = sb("Sc", [P, 2, G, SC + 1], scope=early)
    Pr = sb("Pr", [P, 2, G, SC + 1], scope=early)
    nmax = sb("nmax", [P, 2, G], scope=early)
    PT = sb("PT", [P, 2, 2, G, P], scope=early)
    early.close()

    late = ExitStack()
    C_all = sb("C_all", [P, E, TT, CAP], scope=stack)
    XT_hi = sb("XT_hi", [P, KH, E, SL], F32R)
    XT_lo = sb("XT_lo", [P, KH, E, SL], F32R)
    rinv = sb("rinv", [P, NH], scope=late)
    Ot = sb("Ot", [P, D], scope=late)
    Ot2 = sb("Ot2", [P, D], scope=late)
    Ot3 = sb("Ot3", [P, D], scope=late)
    OT_hi, OT_lo = sb("OT_hi", [P, KH, P], F32R, late), sb("OT_lo", [P, KH, P], F32R, late)
    OTf = sb("OTf", [P, KH, P], scope=late)
    ln_bn, ln_mv, ln_r = sb("ln_bn", [P, 6], scope=late), sb("ln_mv", [P, 2], scope=late), sb("ln_r", [P, 1], scope=late)
    y = sb("y", [P, D], scope=late)
    yT_hi, yT_lo = sb("yT_hi", [P, KH, P], F32R, late), sb("yT_lo", [P, KH, P], F32R, late)
    qk_c = sb("qk_c", [P, 2 * NH, DH], scope=late)
    qk_s = sb("qk_s", [P, 2 * NH, DH], scope=late)
    qk = sb("qk", [P, 2 * D], scope=late)
    Vb = sb("Vb", [P, G, BT, HG * DH], scope=late)
    kT = sb("kT", [P, KH, P], scope=late)
    qTb = sb("qTb", [P, KH, BT, HG, S], scope=late)
    sc2 = sb("sc2", [P, 2, 2, BT, S], scope=late)
    sc2m = sb("sc2m", [P, 2, 2, BT, S], scope=late)
    pr2 = sb("pr2", [P, 2, 2, BT, S], scope=late)
    pr2n = sb("pr2n", [P, 2, 2, BT, S], scope=late)
    mx2, sum2, inv2 = (sb(n, [P, NH], scope=late) for n in ("mx2", "sum2", "inv2"))
    PT2 = sb("PT2", [P, G, P], scope=late)
    O2 = sb("O2", [P, G, HG, DH], scope=late)
    y_hi, y_lo = sb("y_hi", [P, D], F32R, late), sb("y_lo", [P, D], F32R, late)
    yTf = sb("yTf", [P, KH, P], scope=late)
    rt = sb("rt", [P, 24, E], scope=late)
    eq1, eq2 = sb("eq1", [P, E, CAP], scope=late), sb("eq2", [P, E, CAP], scope=late)
    disp = sb("disp", [P, E * CAP], F32R, late)

    late.close()

    late = stack
    RW = 3
    W01_hi, W01_lo = sb("W01_hi", [P, RW, 2, KH, P], F32R, late), sb("W01_lo", [P, RW, 2, KH, P], F32R, late)
    W2_hi, W2_lo = sb("W2_hi", [P, RW, D], F32R, late), sb("W2_lo", [P, RW, D], F32R, late)
    act = sb("act", [P, 3, SL], scope=late)
    hid = sb("hid", [P, 3, SL], scope=late)
    hid_hi, hid_lo = sb("hid_hi", [P, 3, SL], F32R, late), sb("hid_lo", [P, 3, SL], F32R, late)
    CT = sb("CT", [P, E, SP_, P], scope=late)
    Y = sb("Y", [P, E, SP_, D], scope=late)
    fin = sb("fin", [P, 4, D], scope=late)

    bank = stack.enter_context(nc.psum_tensor("bank", [P, 8, 512], F32))
    bk = [bank[:, i, :] for i in range(8)]

    names = """const_in x_in bias_in last_in router_in mask_in xbo_done
        ones_set maskb_set ln1_stats ln1_var ln1_rstd ln1_done
        first_made first_act first_dve
        ctx_turned ctx_hi ctx_lo k_made v_made k_ready kl_ready v_ready qb_ready s_made s_read
        p_ready sums_ready pt_made pt0_ready pt1_ready o_made o_read stats_moved
        a_inv a_last a_add a_norm a_oT_made a_oT_f a_oT_hi a_oT_lo a_wo_made a_x1
        b_bn b_mv b_var b_r b_y b_yT_made b_yT_hi b_yT_lo b_qkv_made b_cos b_sin b_rope b_v_act b_v_dve
        b_qkT_made b_kT b_qT b_s_made b_scaled b_max b_shift b_exp b_sum b_inv b_p b_pT_made b_pT b_o_made
        b_o_act b_o_dve b_oT_made b_oT_hi b_oT_lo b_wo_made b_x2
        c_bn c_mv c_var c_r c_y c_hi c_lo c_yT_made c_yT c_logits_made c_dve c_exp c_m12 c_pos_made c_c c_disp
        c_x_made c_x_hi c_x_lo vb_zero
        split_act split_dve split_pool h_made gelu_done h_done hhi_done hlo_done y_made y_read
        ct_made ct_read comb_made fin_done out_done hi2 turns_ve turns_po""".split()
    sm = {n: stack.enter_context(nc.semaphore(n)) for n in names}
    w_in = [stack.enter_context(nc.semaphore(f"w_in{i}")) for i in range(8)]
    ctx_in_sem = [stack.enter_context(nc.semaphore(f"ctx_in{i}")) for i in range(4)]
    CH = [(0, 4), (4, 8), (8, HT)]
    raw_in = [stack.enter_context(nc.semaphore(f"raw_in{i}")) for i in range(len(CH))]

    def width(t):
        return min(P, HF - t * P)

    def product3(pe, dst, a_hi, a_lo, b_hi, b_lo, first, last):
        pe.matmul(dst, a_hi, b_lo, start=first, stop=False)
        pe.matmul(dst, a_lo, b_hi, start=False, stop=False)
        return pe.matmul(dst, a_hi, b_hi, start=False, stop=last)

    def over_tiles(eng, tile):
        tile(0, True, False)
        with eng.Fori(1, TT - 1) as j:
            tile(j, False, False)
        tile(TT - 1, False, True)

    slots = [("bias", 0)] + [("w", i) for i in range(8)] + [("xT", c) for c in range(4)] + [("q", c) for c in range(4)]
    slots += [("lastT", 0), ("kl", 0)] + [("vl", c) for c in range(4)]
    by_dve = [k in ("w", "xT", "lastT") for k, _ in slots]

    def free_slot(eng, n):
        if n >= 8:
            eng.wait_ge(sm["first_act"], n - 7)
            if any(by_dve[:n - 7]):
                eng.wait_ge(sm["first_dve"], sum(by_dve[:n - 7]))

    NS = len(slots)

    RAW_DMAS = [3, 3, 4]

    def split_ready(eng, e, t):
        for c, (t0, t1) in enumerate(CH):
            if t == t0:
                eng.wait_ge(raw_in[c], 16 * RAW_DMAS[c] * (e + 1))

    def wait_freed(eng, name, e, t, ring, first):
        if t >= ring:
            eng.wait_ge(sm[name], HT * e + t - ring + 1)
        elif not first:
            before_ = max(z for z in range(HT) if z % ring == t % ring)
            eng.wait_ge(sm[name], HT * (e - 1) + before_ + 1)

    def picked(h, b, half_):
        v = bank[h * S:(h + 1) * S, 1 + half_, :].rearrange("p (g b h d) -> p g b h d", g=2, b=BT, h=HG)
        return v[:, :, b, h, :]

    NCD = 23

    block_ = stack.enter_context(nc.Block())

    @block_.sync
    def _(sp):
        sp.dma_start(tab[:, :], table).then_inc(sm["const_in"], 16)
        for i in range(8):
            sp.dma_start(w_raw[:, i, :, :], weights[i].rearrange("(o p) n -> p o n", p=P)).then_inc(w_in[i], 16)
            if i == 0:
                sp.dma_start(x_sb[:, :, :], x.rearrange("(j b) s d -> (b s) j d", b=BT)).then_inc(sm["x_in"], 16)
        sp.dma_start(last_raw[:, :], ctx_in[:, SC - 1, :]).then_inc(sm["last_in"], 16)
        for h in range(HG):
            sp.dma_start(mask_i[h * S:(h + 1) * S, :], mask[0, 0]).then_inc(sm["mask_in"], 16)
        for i, vec in enumerate((xbq, xbk, xbv)):
            sp.dma_start(bias_raw[KH * i:KH * i + KH, :], vec.rearrange("(k p) -> k p", p=P)).then_inc(sm["bias_in"], 16)
        sp.dma_start(bo_row[:, :], xbo.rearrange("(a n) -> a n", a=1).broadcast_to([P, D])).then_inc(sm["bias_in"], 16)
        sp.dma_start(router_sb[:, :, :], router.rearrange("(k p) e -> p k e", p=P)).then_inc(sm["router_in"], 16)

        def load_ctx(j, first, last):
            for u in range(4):
                b = 4 * j + u
                if not first:
                    sp.wait_ge(sm["ctx_turned"], b - 3)
                src = ctx_in[bass.ds(b, 1), 0:2 * P, :] if not isinstance(b, int) else ctx_in[b:b + 1, 0:2 * P, :]
                sp.dma_start(ctx_raw[:, u, :, :], src.rearrange("a (t p) d -> p (a t) d", p=P)).then_inc(ctx_in_sem[u], 16)

        over_tiles(sp, load_ctx)

        def load_expert(e, first):
            for c, (t0, t1) in enumerate(CH):
                if not first:
                    for s in ("split_act", "split_dve", "split_pool"):
                        sp.wait_ge(sm[s], HT * (e - 1) + t1)
                a, z = t0 * P, min(t1 * P, HF)
                for n, w in enumerate((w0, w1)):
                    src = w[bass.ds(e, 1), :, a:z] if not first else w[e:e + 1, :, a:z]
                    sp.dma_start(raw01[:, n, :, a:z], src.rearrange("a (k p) n -> p (a k) n", p=P)).then_inc(raw_in[c], 16)
                full = z // P * P
                src = wo[bass.ds(e, 1), a:full, :] if not first else wo[e:e + 1, a:full, :]
                sp.dma_start(raw2[:, t0:full // P, :], src.rearrange("a (t p) n -> p (a t) n", p=P)).then_inc(raw_in[c], 16)
                if full < z:
                    src = wo[bass.ds(e, 1), full:z, :] if not first else wo[e:e + 1, full:z, :]
                    sp.dma_start(raw2[0:z - full, HT - 1, :], src.rearrange("a p n -> p (a n)")).then_inc(raw_in[c], 16)

        load_expert(0, True)
        with sp.Fori(1, E) as e:
            load_expert(e, False)

        out_v = out.rearrange("(j b) s d -> (b s) j d", b=BT)
        for j in range(TT):
            sp.wait_ge(sm["fin_done"], j + 1)
            sp.dma_start(out_v[:, j, :], fin[:, j % 4, :]).then_inc(sm["out_done"], 16)
        sp.wait_ge(sm["out_done"], 16 * TT)

    @block_.tensor
    def _(pe):
        pe.wait_ge(sm["const_in"], 16)
        for n, (kind, i) in enumerate(slots):
            dst = bk[n % 8]
            free_slot(pe, n)
            if kind == "bias":
                pe.wait_ge(sm["bias_in"], 64)
                last = pe.transpose(dst[:, 0:3 * KH], bias_raw[:, :], ident[0:3 * KH, 0:3 * KH])
            elif kind == "w":
                pe.wait_ge(w_in[i], 16)
                for k in range(KH):
                    for o in range(KH):
                        last = pe.transpose(dst[:, k * D + o * P:k * D + (o + 1) * P],
                                            w_raw[:, i, o, k * P:(k + 1) * P], ident)
            elif kind == "xT":
                pe.wait_ge(sm["ln1_done"], 2 * i + 2)
                for k in range(KH):
                    for j in range(2):
                        last = pe.transpose(dst[:, k * D + j * P:k * D + (j + 1) * P],
                                            xn[:, 2 * i + j, k * P:(k + 1) * P], ident)
            elif kind == "q":
                t, n0 = i // 2, i % 2 * 512
                if i == 0:
                    pe.wait_ge(sm["first_act"], n)
                    pe.wait_ge(sm["first_dve"], n - 1)
                for k in range(KH):
                    last = product3(pe, dst, WT_hi[:, 0, k, t * P:(t + 1) * P], WT_lo[:, 0, k, t * P:(t + 1) * P],
                                    xnT_hi[:, k, n0:n0 + 512], xnT_lo[:, k, n0:n0 + 512], k == 0, k == KH - 1)
            elif kind == "lastT":
                pe.wait_ge(sm["last_in"], 16)
                for k in range(KH):
                    last = pe.transpose(dst[:, k * B:(k + 1) * B], last_raw[:, k * P:(k + 1) * P], ident[0:B, 0:B])
            elif kind == "kl":
                pe.wait_ge(sm["first_act"], n)
                pe.wait_ge(sm["first_dve"], sum(by_dve))
                for t in range(KH):
                    for k in range(KH):
                        last = product3(pe, dst[:, t * B:(t + 1) * B], WT_hi[:, 1, k, t * P:(t + 1) * P],
                                        WT_lo[:, 1, k, t * P:(t + 1) * P], lastT_hi[:, k, :, 0], lastT_lo[:, k, :, 0],
                                        k == 0, k == KH - 1)
            elif kind == "vl":
                for h in range(2):
                    b = (2 * i + h) * BT
                    for k in range(KH):
                        hi, lo = lastT_hi[:, k, b:b + BT, :], lastT_lo[:, k, b:b + BT, :]
                        last = product3(pe, dst[:, h * D:(h + 1) * D], hi, lo, WT_hi[:, 2, k, :], WT_lo[:, 2, k, :],
                                        k == 0, k == KH - 1)
            last.then_inc(sm["first_made"], 1)
        pe.wait_ge(sm["first_act"], NS)
        pe.wait_ge(sm["first_dve"], sum(by_dve))

        def turn_ctx(b, r, landed, first):
            pe.wait_ge(ctx_in_sem[r], landed)
            if not first:
                pe.wait_ge(sm["ctx_hi"], b)
                pe.wait_ge(sm["ctx_lo"], b)
            for k in range(KH):
                for t in range(2):
                    last = pe.transpose(bk[0][:, k * 2 * P + t * P:k * 2 * P + (t + 1) * P],
                                        ctx_raw[:, r, t, k * P:(k + 1) * P], ident)
            last.then_inc(sm["ctx_turned"], 1)

        def keys(b, r, first):
            pe.wait_ge(sm["ctx_hi"], b + 1)
            pe.wait_ge(sm["ctx_lo"], b + 1)
            if not first:
                pe.wait_ge(sm["k_ready"], b)
            for t in range(KH):
                for k in range(KH):
                    last = product3(pe, bk[1][:, t * D:(t + 1) * D], WT_hi[:, 1, k, t * P:(t + 1) * P],
                                    WT_lo[:, 1, k, t * P:(t + 1) * P], ctxT_hi[:, r % 2, k, :],
                                    ctxT_lo[:, r % 2, k, :], k == 0, k == KH - 1)
            last.then_inc(sm["k_made"], 1)

        def values(b, r, first):
            if not first:
                pe.wait_ge(sm["v_ready"], b)
            for t in range(2):
                for k in range(KH):
                    last = product3(pe, bk[2][:, t * D:(t + 1) * D], ctxT_hi[:, r % 2, k, t * P:(t + 1) * P],
                                    ctxT_lo[:, r % 2, k, t * P:(t + 1) * P], WT_hi[:, 2, k, :], WT_lo[:, 2, k, :],
                                    k == 0, k == KH - 1)
            last.then_inc(sm["v_made"], 1)

        def energies(b, r, pair, first):
            if pair == 0:
                pe.wait_ge(sm["k_ready"], b + 1)
                pe.wait_ge(sm["kl_ready"], b + 1)
                pe.wait_ge(sm["qb_ready"], b + 1)
            if not first or pair:
                pe.wait_ge(sm["s_read"], 4 * b + 2 * pair)
            for g in range(2):
                last = pe.matmul(bk[3 + g][:, 0:SC], Qb[64 * g:64 * g + 64, r % 2, pair, :, :],
                                 KT[64 * g:64 * g + 64, r % 2, pair, 0:SC], start=True, stop=True)
            last.then_inc(sm["s_made"], 1)

        def turn_probs(b, r, t, first):
            if t == 0:
                pe.wait_ge(sm["p_ready"], 4 * b + 4)
            if not first:
                pe.wait_ge(sm[("pt0_ready", "pt1_ready")[t]], b)
            for g in range(G):
                last = pe.transpose(bk[5 + t][:, g * P:(g + 1) * P], Pr[:, r % 2, g, t * P:(t + 1) * P], ident)
            last.then_inc(sm["pt_made"], 1)

        def outputs(b, r, first):
            pe.wait_ge(sm["pt0_ready"], b + 1)
            pe.wait_ge(sm["pt1_ready"], b + 1)
            pe.wait_ge(sm["v_ready"], b + 1)
            if not first:
                pe.wait_ge(sm["o_read"], b)
            for g in range(G):
                for t in range(2):
                    last = pe.matmul(bk[7][:, g * 64:(g + 1) * 64], PT[:, r % 2, t, g, :],
                                     V[:, r % 4, t, g * 64:(g + 1) * 64], start=t == 0, stop=t == 1)
            last.then_inc(sm["o_made"], 1)

        turn_ctx(0, 0, 16, True)
        keys(0, 0, True)
        values(0, 0, True)
        turn_ctx(1, 1, 16, False)

        def cross(j, first, last):
            for u in range(4):
                b = 4 * j + u
                energies(b, u, 0, first and u == 0)
                if not first or u >= 2:
                    outputs(b - 2, (u - 2) % 4, first and u == 2)
                if not last or u < 2:
                    turn_ctx(b + 2, (u + 2) % 4, 16 * (j + 1 + (u + 2) // 4), False)
                energies(b, u, 1, first and u == 0)
                if not last or u < 3:
                    keys(b + 1, (u + 1) % 4, False)
                if not first or u >= 1:
                    turn_probs(b - 1, (u - 1) % 4, 0, first and u == 1)
                if not last or u < 3:
                    values(b + 1, (u + 1) % 4, False)
                if not first or u >= 1:
                    turn_probs(b - 1, (u - 1) % 4, 1, first and u == 1)

        over_tiles(pe, cross)
        outputs(B - 2, (B - 2) % 4, False)
        turn_probs(B - 1, (B - 1) % 4, 0, False)
        turn_probs(B - 1, (B - 1) % 4, 1, False)
        outputs(B - 1, (B - 1) % 4, False)

        with pe.Fori(0, TT) as j:
            pe.wait_ge(sm["a_norm"], j + 1)
            for k in range(KH):
                last = pe.transpose(bk[0][:, k * P:(k + 1) * P], Ot3[:, k * P:(k + 1) * P], ident)
            last.then_inc(sm["a_oT_made"], 1)
            pe.wait_ge(sm["a_oT_lo"], j + 1)
            for k in range(KH):
                last = product3(pe, bk[1][:, 0:D], OT_hi[:, k, :], OT_lo[:, k, :], WT_hi[:, 3, k, :], WT_lo[:, 3, k, :],
                                k == 0, k == KH - 1)
            last.then_inc(sm["a_wo_made"], 1)

            pe.wait_ge(sm["b_y"], j + 1)
            for k in range(KH):
                last = pe.transpose(bk[2][:, k * P:(k + 1) * P], y[:, k * P:(k + 1) * P], ident)
            last.then_inc(sm["b_yT_made"], 1)
            pe.wait_ge(sm["b_yT_lo"], j + 1)
            for i in range(3):
                for k in range(KH):
                    last = product3(pe, bk[3 + i // 2][:, i % 2 * D:i % 2 * D + D], yT_hi[:, k, :], yT_lo[:, k, :],
                                    WT_hi[:, 4 + i, k, :], WT_lo[:, 4 + i, k, :], k == 0, k == KH - 1)
            last.then_inc(sm["b_qkv_made"], 1)
            pe.wait_ge(sm["b_rope"], j + 1)
            for i in range(4):
                last = pe.transpose(bk[5][:, i * P:(i + 1) * P], qk[:, i * P:(i + 1) * P], ident)
            last.then_inc(sm["b_qkT_made"], 1)
            pe.wait_ge(sm["b_kT"], j + 1)
            pe.wait_ge(sm["b_qT"], j + 1)
            for gh in range(2):
                for gp in range(2):
                    for b in range(BT):
                        last = pe.matmul(bk[6 + gp][:, (gh * BT + b) * S:(gh * BT + b + 1) * S],
                                         qTb[64 * gp:64 * gp + 64, gh, b, :, :],
                                         kT[64 * gp:64 * gp + 64, gh, b * S:(b + 1) * S], start=True, stop=True)
            last.then_inc(sm["b_s_made"], 1)
            pe.wait_ge(sm["b_p"], j + 1)
            for g in range(G):
                last = pe.transpose(bk[0][:, g * P:(g + 1) * P], pr2n[:, g % 2, g // 2, :, :], ident)
            last.then_inc(sm["b_pT_made"], 1)
            pe.wait_ge(sm["b_pT"], j + 1)
            pe.wait_ge(sm["b_v_act"], j + 1)
            pe.wait_ge(sm["b_v_dve"], j + 1)
            for g in range(G):
                last = pe.matmul(bk[1 + g // 2][:, g % 2 * D:g % 2 * D + D], PT2[:, g, :], Vb[:, g, :, :],
                                 start=True, stop=True)
            last.then_inc(sm["b_o_made"], 1)
            pe.wait_ge(sm["b_o_act"], j + 1)
            pe.wait_ge(sm["b_o_dve"], j + 1)
            for k in range(KH):
                last = pe.transpose(bk[3][:, k * P:(k + 1) * P], O2[:, 2 * k:2 * k + 2, :, :], ident)
            last.then_inc(sm["b_oT_made"], 1)
            pe.wait_ge(sm["b_oT_lo"], j + 1)
            for k in range(KH):
                last = product3(pe, bk[4][:, 0:D], OT_hi[:, k, :], OT_lo[:, k, :], WT_hi[:, 7, k, :], WT_lo[:, 7, k, :],
                                k == 0, k == KH - 1)
            last.then_inc(sm["b_wo_made"], 1)

            pe.wait_ge(sm["c_y"], j + 1)
            for k in range(KH):
                last = pe.transpose(bk[5][:, k * P:(k + 1) * P], y[:, k * P:(k + 1) * P], ident)
            last.then_inc(sm["c_yT_made"], 1)
            pe.wait_ge(sm["c_yT"], j + 1)
            for k in range(KH):
                last = pe.matmul(bk[6][:, 0:E], yTf[:, k, :], router_sb[:, k, :], start=k == 0, stop=k == KH - 1)
            last.then_inc(sm["c_logits_made"], 1)
            pe.wait_ge(sm["c_m12"], j + 1)
            pe.matmul(bk[7][:, 0:2 * E], before, rt[:, 10:12, :], start=True, stop=True)
            pe.matmul(bk[7][:, 2 * E:3 * E], ones[:, :], rt[:, 10, :], start=True, stop=True)\
              .then_inc(sm["c_pos_made"], 1)
            pe.wait_ge(sm["c_disp"], j + 1)
            pe.wait_ge(sm["c_hi"], j + 1)
            pe.wait_ge(sm["c_lo"], j + 1)
            for part, (i, src) in enumerate(((0, y_hi), (1, y_lo))):
                for m in range(KH):
                    last = pe.matmul(bk[i][:, m * D:(m + 1) * D], src[:, m * P:(m + 1) * P], disp[:, :],
                                     start=True, stop=True)
            last.then_inc(sm["c_x_made"], 1)
            pe.wait_ge(sm["c_x_hi"], j + 1)
            pe.wait_ge(sm["c_x_lo"], j + 1)

        for i in range(4):
            for q in range(4):
                e, h = (4 * i + q) // SP_, (4 * i + q) % SP_
                last = pe.transpose(bk[i][:, q * P:(q + 1) * P], C_all[:, e, 4 * h:4 * h + 4, :], ident)
            last.then_inc(sm["ct_made"], 1)
        pe.wait_ge(sm["ct_read"], 4)

        def up(e, t, first):
            n, w = HT * e + t, width(t)
            pe.wait_ge(sm["split_act"], n + 1)
            pe.wait_ge(sm["split_dve"], n + 1)
            wait_freed(pe, "h_done", e, t, 3, first)
            for i in range(2):
                for k in range(KH):
                    last = product3(pe, bk[3 * i + t % 3][0:w, 0:SL], W01_hi[:, t % RW, i, k, 0:w],
                                    W01_lo[:, t % RW, i, k, 0:w], XT_hi[:, k, at_e(e), :], XT_lo[:, k, at_e(e), :],
                                    k == 0, k == KH - 1)
            last.then_inc(sm["h_made"], 1)

        def at_e(e):
            return e if isinstance(e, int) else bass.ds(e, 1)

        def down(e, t, first):
            n, w = HT * e + t, width(t)
            pe.wait_ge(sm["hhi_done"], n + 1)
            pe.wait_ge(sm["hlo_done"], n + 1)
            pe.wait_ge(sm["split_pool"], n + 1)
            if t == 0 and not first:
                pe.wait_ge(sm["y_read"], 2 * e)
            for h in range(SP_):
                last = product3(pe, bk[6 + h][:, 0:D], hid_hi[0:w, t % 3, h * P:(h + 1) * P],
                                hid_lo[0:w, t % 3, h * P:(h + 1) * P], W2_hi[0:w, t % RW, :], W2_lo[0:w, t % RW, :],
                                t == 0, t == HT - 1)
            last.then_inc(sm["y_made"], 1)

        def expert(e, first):
            for t in range(HT):
                up(e, t, first)
                if t >= 1:
                    down(e, t - 1, first)
            down(e, HT - 1, first)

        expert(0, True)
        with pe.Fori(1, E) as e:
            expert(e, False)

        pe.wait_ge(sm["y_read"], 2 * E)
        for h in range(SP_):
            for e in range(E):
                for q in range(4):
                    last = pe.matmul(bk[4 * h + q][:, 0:D], CT[q * CAP:(q + 1) * CAP, e, h, :],
                                     Y[q * CAP:(q + 1) * CAP, e, h, :], start=e == 0, stop=e == E - 1)
            last.then_inc(sm["comb_made"], 1)

    @block_.scalar
    def _(ac):
        for n, (kind, i) in enumerate(slots):
            src = bk[n % 8]
            ac.wait_ge(sm["first_made"], n + 1)
            if kind == "bias":
                last = ac.activation(bias_col[:, :], src[:, 0:3 * KH], ACT.Copy)
            elif kind == "w":
                last = ac.activation(WT_hi[:, i, :, :], src.rearrange("p (k n) -> p k n", k=KH), ACT.Copy)
            elif kind == "xT":
                last = ac.activation(xnT_hi[:, :, i * D:(i + 1) * D], src.rearrange("p (k n) -> p k n", k=KH), ACT.Copy)
            elif kind == "q":
                t, n0 = i // 2, i % 2 * 512
                last = ac.activation(QT[:, t, n0:n0 + 512], src, ACT.Identity, bias=bq_col[:, t:t + 1])
            elif kind == "lastT":
                last = ac.activation(lastT_hi[:, :, :, :].rearrange("p k b s -> p (k b) s"),
                                     src[:, 0:KH * B].unsqueeze(2).broadcast_to([P, KH * B, S]), ACT.Copy)
            elif kind == "kl":
                for t in range(KH):
                    last = ac.activation(KLT[:, t, :], src[:, t * B:(t + 1) * B], ACT.Identity, bias=bk_col[:, t:t + 1])
            elif kind == "vl":
                last = ac.activation(VL_all[:, 2 * i:2 * i + 2, :], src.rearrange("p (k n) -> p k n", k=2), ACT.Copy)
            last.then_inc(sm["first_act"], 1)

        def split_ctx(b, r, first2):
            ac.wait_ge(sm["ctx_turned"], b + 1)
            if not first2:
                ac.wait_ge(sm["v_made"], b - 1)
            ac.activation(ctxT_hi[:, r % 2, :, :], bk[0].rearrange("p (k n) -> p k n", k=KH), ACT.Copy)\
              .then_inc(sm["ctx_hi"], 1)

        def keep_keys(b, r, first2):
            ac.wait_ge(sm["k_made"], b + 1)
            if not first2:
                ac.wait_ge(sm["s_made"], 2 * b - 2)
            for t in range(KH):
                last = ac.activation(KT[:, r % 2, t, 0:2 * P], bk[1][:, t * D:(t + 1) * D], ACT.Identity,
                                     bias=bk_col[:, t:t + 1])
            last.then_inc(sm["k_ready"], 1)

        def keep_values(b, r, first4):
            ac.wait_ge(sm["v_made"], b + 1)
            if not first4:
                ac.wait_ge(sm["o_made"], b - 3)
            ac.activation(V[:, r % 4, :, :], bk[2].rearrange("p (t n) -> p t n", t=2), ACT.Copy)\
              .then_inc(sm["v_ready"], 1)

        def exps(b, r, first2, gs):
            for g in gs:
                ac.wait_ge(sm["s_read"], 4 * b + g + 1)
                if g == 0 and not first2:
                    ac.wait_ge(sm["pt_made"], 2 * b - 2)
                    ac.wait_ge(sm["stats_moved"], b - 1)
                ac.activation(Pr[:, r % 2, g, 0:SC], Sc[:, r % 2, g, 0:SC], ACT.Exp, bias=nmax[:, r % 2, g:g + 1],
                              scale=-1.0, accum_out=Pr[:, r % 2, g, SC:SC + 1]).then_inc(sm["p_ready"], 1)

        def keep_probs(b, r, first2):
            ac.wait_ge(sm["pt_made"], 2 * b + 1)
            if not first2:
                ac.wait_ge(sm["o_made"], b - 1)
            ac.activation(PT[:, r % 2, 0, :, :], bk[5].rearrange("p (g n) -> p g n", g=G), ACT.Copy)\
              .then_inc(sm["pt0_ready"], 1)

        split_ctx(0, 0, True)
        keep_keys(0, 0, True)
        keep_values(0, 0, True)
        split_ctx(1, 1, True)

        def cross(j, first, last):
            for u in range(4):
                b = 4 * j + u
                exps(b, u, first and u < 2, (0, 1))
                if not last or u < 2:
                    split_ctx(b + 2, u, False)
                exps(b, u, first and u < 2, (2, 3))
                if not last or u < 3:
                    keep_keys(b + 1, (u + 1) % 4, first and u < 1)
                if not first or u >= 1:
                    keep_probs(b - 1, (u - 1) % 4, first and u < 3)
                if not last or u < 3:
                    keep_values(b + 1, (u + 1) % 4, first and u < 3)

        over_tiles(ac, cross)
        keep_probs(B - 1, (B - 1) % 4, False)

        with ac.Fori(0, TT) as j:
            ac.wait_ge(sm["a_oT_made"], j + 1)
            for k in range(KH):
                last = ac.activation(OTf[:, k, :], bk[0][:, k * P:(k + 1) * P], ACT.Identity, bias=bv_col[:, k:k + 1])
            last.then_inc(sm["a_oT_f"], 1)
            ac.wait_ge(sm["a_oT_f"], j + 1)
            ac.activation(OT_hi[:, :, :], OTf[:, :, :], ACT.Copy).then_inc(sm["a_oT_hi"], 1)
            ac.wait_ge(sm["b_yT_made"], j + 1)
            ac.activation(yT_hi[:, :, :], bk[2][:, 0:KH * P].rearrange("p (k n) -> p k n", k=KH), ACT.Copy)\
              .then_inc(sm["b_yT_hi"], 1)
            ac.wait_ge(sm["b_qkv_made"], j + 1)
            ac.wait_ge(sm["vb_zero"], 1)
            for b in range(2):
                last = ac.activation(Vb[b * S:(b + 1) * S, :, b, :],
                                     bk[4][b * S:(b + 1) * S, 0:D].rearrange("p (g n) -> p g n", g=G), ACT.Copy)
            last.then_inc(sm["b_v_act"], 1)
            ac.wait_ge(sm["b_qkT_made"], j + 1)
            ac.activation(kT[:, :, :], bk[5][:, D:2 * D].rearrange("p (k n) -> p k n", k=KH), ACT.Copy)\
              .then_inc(sm["b_kT"], 1)
            ac.wait_ge(sm["b_shift"], j + 1)
            ac.activation(pr2[:, :, :, :, :], sc2m[:, :, :, :, :], ACT.Exp).then_inc(sm["b_exp"], 1)
            ac.wait_ge(sm["b_pT_made"], j + 1)
            ac.activation(PT2[:, :, :], bk[0].rearrange("p (g n) -> p g n", g=G), ACT.Copy).then_inc(sm["b_pT"], 1)
            ac.wait_ge(sm["b_o_made"], j + 1)
            for b in range(BT):
                for h in range(HG):
                    last = ac.activation(O2[b * S:(b + 1) * S, 0:2, h, :], picked(h, b, 0), ACT.Copy)
            last.then_inc(sm["b_o_act"], 1)
            ac.wait_ge(sm["b_oT_made"], j + 1)
            ac.activation(OT_hi[:, :, :], bk[3][:, 0:KH * P].rearrange("p (k n) -> p k n", k=KH), ACT.Copy)\
              .then_inc(sm["b_oT_hi"], 1)
            ac.wait_ge(sm["c_y"], j + 1)
            ac.activation(y_hi[:, :], y[:, :], ACT.Copy).then_inc(sm["c_hi"], 1)
            ac.wait_ge(sm["c_yT_made"], j + 1)
            ac.activation(yTf[:, :, :], bk[5][:, 0:KH * P].rearrange("p (k n) -> p k n", k=KH), ACT.Copy)\
              .then_inc(sm["c_yT"], 1)
            ac.wait_ge(sm["c_dve"], NCD * j + 1)
            ac.activation(rt[:, 1, :], bk[6][:, 0:E], ACT.Exp, bias=rt[:, 0, 0:1], accum_out=rt[:, 0, 1:2])\
              .then_inc(sm["c_exp"], 1)
            ac.wait_ge(sm["c_x_made"], j + 1)
            ac.activation(XT_hi[:, 0:KH, :, bass.ds(j * CAP, CAP)],
                          bk[0].rearrange("p (k e c) -> p k e c", k=KH, e=E), ACT.Copy).then_inc(sm["c_x_hi"], 1)

        for i in range(0, 4, 2):
            ac.wait_ge(sm["ct_made"], i + 2)
            for q in range(2):
                last = ac.activation(CT[:, (4 * (i + q)) // SP_:(4 * (i + q) + 4) // SP_, :, :],
                                     bk[i + q].rearrange("p (e h n) -> p e h n", h=SP_, n=P), ACT.Copy)
                last.then_inc(sm["ct_read"], 1)

        def expert(e, first):
            for t in range(HT + 1):
                if t < HT:
                    n, w = HT * e + t, width(t)
                    split_ready(ac, e, t)
                    wait_freed(ac, "h_made", e, t, RW, first)
                    ac.activation(W01_hi[:, t % RW, :, :, 0:w].rearrange("p i k n -> p (i k) n"),
                                  raw01[:, :, :, t * P:t * P + w].rearrange("p i k n -> p (i k) n"), ACT.Copy)\
                      .then_inc(sm["split_act"], 1)
                if t >= 1:
                    tt = t - 1
                    n, w = HT * e + tt, width(tt)
                    ac.wait_ge(sm["h_made"], n + 1)
                    wait_freed(ac, "h_done", e, tt, 3, first)
                    ac.activation(act[0:w, tt % 3, :], bk[tt % 3][0:w, 0:SL], ACT.Gelu_apprx_tanh)\
                      .then_inc(sm["gelu_done"], 1)
                    ac.wait_ge(sm["h_done"], n + 1)
                    wait_freed(ac, "y_made", e, tt, 3, first)
                    ac.activation(hid_hi[0:w, tt % 3, :], hid[0:w, tt % 3, :], ACT.Copy).then_inc(sm["hhi_done"], 1)

        expert(0, True)
        with ac.Fori(1, E) as e:
            expert(e, False)

    @block_.vector
    def _(ve):
        ve.memset(ones[:, :], 1.0)
        ve.memset(half[:, :], -0.5).then_inc(sm["ones_set"], 1)
        ve.wait_ge(sm["mask_in"], 64)
        ve.tensor_scalar(mask_add[:, :], mask_i[:, :], 0.0, MASKED * 4.0, ALU.is_equal, ALU.mult).then_inc(sm["maskb_set"], 1)
        ve.wait_ge(sm["x_in"], 16)
        for j in range(TT):
            ve.bn_stats(bn[:, j, :], x_sb[:, j, :]).then_inc(sm["ln1_stats"], 1)
        ve.wait_ge(sm["ln1_stats"], TT)
        for j in range(TT):
            ve.bn_aggr(mv[:, j, :], bn[:, j, :]).then_inc(sm["ln1_stats"], 1)
        ve.wait_ge(sm["ln1_stats"], 2 * TT)
        ve.tensor_scalar(mv[:, :, 1], mv[:, :, 1], EPS, None, ALU.add).then_inc(sm["ln1_var"], 1)
        ve.wait_ge(sm["ln1_rstd"], 1)
        for j in range(TT):
            ve.tensor_scalar(xn[:, j, :], x_sb[:, j, :], mv[:, j, 0:1], rstd[:, j:j + 1], ALU.subtract, ALU.mult)\
              .then_inc(sm["ln1_done"], 1)
        ve.wait_ge(sm["bias_in"], 64)
        for n, (kind, i) in enumerate(slots):
            if not by_dve[n]:
                continue
            ve.wait_ge(sm["first_act"], n + 1)
            src = bk[n % 8]
            if kind == "w":
                hi, lo = WT_hi[:, i, :, :], WT_lo[:, i, :, :]
            elif kind == "xT":
                hi, lo = xnT_hi[:, :, i * D:(i + 1) * D], xnT_lo[:, :, i * D:(i + 1) * D]
            if kind == "lastT":
                hi, lo = (z[:, :, :, :].rearrange("p k b s -> p (k b) s") for z in (lastT_hi, lastT_lo))
                src = src[:, 0:KH * B].unsqueeze(2).broadcast_to([P, KH * B, S])
            else:
                src = src.rearrange("p (k n) -> p k n", k=KH)
            ve.tensor_tensor(lo, src, f(hi), ALU.subtract).then_inc(sm["first_dve"], 1)

        def split_ctx(b, r, first2):
            ve.wait_ge(sm["ctx_hi"], b + 1)
            if not first2:
                ve.wait_ge(sm["v_made"], b - 1)
            ve.tensor_tensor(ctxT_lo[:, r % 2, :, :], bk[0].rearrange("p (k n) -> p k n", k=KH),
                             f(ctxT_hi[:, r % 2, :, :]), ALU.subtract).then_inc(sm["ctx_lo"], 1)

        def maxima(b, r, first2, pair):
            ve.wait_ge(sm["s_made"], 2 * b + pair + 1)
            for q in range(2):
                g = 2 * pair + q
                if not first2:
                    ve.wait_ge(sm["p_ready"], 4 * b - 7 + g)
                ve.sem_inc(sm["turns_ve"], 1)
                ve.tensor_tensor_reduce(Sc[:, r % 2, g, 0:SC], bk[3 + q][:, 0:SC], mask_add[:, :], -0.25, 3e38,
                                        ALU.add, ALU.min, nmax[:, r % 2, g:g + 1]).then_inc(sm["s_read"], 1)

        def keep_outputs(b, r):
            ve.wait_ge(sm["o_made"], b + 1)
            for h in range(HG):
                src = bk[7][h * S:(h + 1) * S, 0:D].rearrange("p (g h d) -> p g h d", g=G, h=HG)[:, :, h, :]
                dst = O_tile(b, r).rearrange("p (g h d) -> p g h d", g=G, h=HG)[:, :, h, :]
                last = ve.tensor_copy(dst, src)
            last.then_inc(sm["o_read"], 1)

        def move_stats(b, r):
            ve.wait_ge(sm["p_ready"], 4 * b + 4)
            for h in range(HG):
                rows = stat_all[r * S:(r + 1) * S]
                row = rows[:, b // BT] if isinstance(b, int) else rows[:, bass.ds((b - r) // BT, 1)].rearrange("p a h k -> p (a h) k")
                last = ve.tensor_copy(row.rearrange("p (g h) k -> p g h k", h=HG)[:, :, h, :],
                                      Pr[h * S:(h + 1) * S, r % 2, :, SC - 1:SC + 1])
            last.then_inc(sm["stats_moved"], 1)

        def O_tile(b, r):
            if isinstance(b, int):
                return O_all[r * S:(r + 1) * S, b // BT, :]
            return O_all[r * S:(r + 1) * S, bass.ds((b - r) // BT, 1), :].rearrange("p a n -> p (a n)")

        def keep_probs(b, r, first2):
            ve.wait_ge(sm["pt_made"], 2 * b + 2)
            if not first2:
                ve.wait_ge(sm["o_made"], b - 1)
            ve.tensor_copy(PT[:, r % 2, 1, :, :], bk[6].rearrange("p (g n) -> p g n", g=G)).then_inc(sm["pt1_ready"], 1)

        split_ctx(0, 0, True)
        split_ctx(1, 1, True)
        ve.wait_ge(sm["maskb_set"], 1)

        def cross(j, first, last):
            for u in range(4):
                b = 4 * j + u
                maxima(b, u, first and u < 2, 0)
                if not first or u >= 2:
                    keep_outputs(b - 2, (u - 2) % 4)
                if not last or u < 2:
                    split_ctx(b + 2, u, False)
                maxima(b, u, first and u < 2, 1)
                if not first or u >= 1:
                    move_stats(b - 1, (u - 1) % 4)
                    keep_probs(b - 1, (u - 1) % 4, first and u < 3)

        over_tiles(ve, cross)
        keep_outputs(B - 2, (B - 2) % 4)
        move_stats(B - 1, (B - 1) % 4)
        keep_probs(B - 1, (B - 1) % 4, False)
        keep_outputs(B - 1, (B - 1) % 4)
        ve.wait_ge(sm["stats_moved"], B)
        ve.wait_ge(sm["pt0_ready"], B)
        ve.memset(Vb[:, :, :, :], 0.0).then_inc(sm["vb_zero"], 1)

        def at_j(t, j):
            return t[:, bass.ds(j, 1), :].rearrange("p a n -> p (a n)")

        def norm(j, who, src, dst):
            ve.bn_stats(ln_bn[:, :], src).then_inc(sm[who + "_bn"], 1)
            ve.wait_ge(sm["ones_set"], 1)
            ve.wait_ge(sm[who + "_bn"], j + 1)
            ve.bn_aggr(ln_mv[:, :], ln_bn[:, :]).then_inc(sm[who + "_mv"], 1)
            ve.wait_ge(sm[who + "_mv"], j + 1)
            ve.tensor_scalar(ln_mv[:, 1:2], ln_mv[:, 1:2], EPS, None, ALU.add).then_inc(sm[who + "_var"], 1)
            ve.wait_ge(sm[who + "_r"], j + 1)
            ve.tensor_scalar(dst, src, ln_mv[:, 0:1], ln_r[:, 0:1], ALU.subtract, ALU.mult).then_inc(sm[who + "_y"], 1)

        with ve.Fori(0, TT) as j:
            stat = stat_all[:, bass.ds(j, 1)].rearrange("p a h k -> p (a h) k")
            ve.reciprocal(rinv[:, :], stat[:, :, 1]).then_inc(sm["a_inv"], 1)
            ve.tensor_tensor(Ot[:, :].rearrange("p (h d) -> p h d", d=DH),
                             at_j(VL_all, j).rearrange("p (h d) -> p h d", d=DH),
                             stat[:, :, 0].unsqueeze(2).broadcast_to([P, NH, DH]), ALU.mult).then_inc(sm["a_last"], 1)
            ve.wait_ge(sm["a_last"], j + 1)
            ve.tensor_tensor(Ot2[:, :], Ot[:, :], at_j(O_all, j), ALU.add).then_inc(sm["a_add"], 1)
            ve.wait_ge(sm["a_add"], j + 1)
            ve.tensor_tensor(Ot3[:, :].rearrange("p (h d) -> p h d", d=DH), Ot2[:, :].rearrange("p (h d) -> p h d", d=DH),
                             rinv[:, :].unsqueeze(2).broadcast_to([P, NH, DH]), ALU.mult).then_inc(sm["a_norm"], 1)
            ve.wait_ge(sm["a_oT_hi"], j + 1)
            ve.tensor_tensor(OT_lo[:, :, :], OTf[:, :, :], f(OT_hi[:, :, :]), ALU.subtract).then_inc(sm["a_oT_lo"], 1)
            ve.wait_ge(sm["a_wo_made"], j + 1)
            ve.tensor_tensor(at_j(x_sb, j), bk[1][:, 0:D], at_j(x_sb, j), ALU.add).then_inc(sm["a_x1"], 1)
            ve.wait_ge(sm["ones_set"], 1)
            ve.wait_ge(sm["a_x1"], j + 1)
            norm(j, "b", at_j(x_sb, j), y[:, :])
            ve.wait_ge(sm["b_yT_hi"], j + 1)
            ve.tensor_tensor(yT_lo[:, :, :], bk[2][:, 0:KH * P].rearrange("p (k n) -> p k n", k=KH), f(yT_hi[:, :, :]),
                             ALU.subtract).then_inc(sm["b_yT_lo"], 1)
            ve.wait_ge(sm["b_qkv_made"], j + 1)
            pq = bk[3].rearrange("p (h d) -> p h d", d=DH)
            ve.tensor_tensor(qk_c[:, :, :], pq, cos16.unsqueeze(1).broadcast_to([P, 2 * NH, DH]), ALU.mult)\
              .then_inc(sm["b_cos"], 1)
            ve.tensor_tensor(qk_s[:, :, 0::2], pq[:, :, 1::2], nsin8.unsqueeze(1).broadcast_to([P, 2 * NH, DH // 2]),
                             ALU.mult)
            ve.tensor_tensor(qk_s[:, :, 1::2], pq[:, :, 0::2], sin8.unsqueeze(1).broadcast_to([P, 2 * NH, DH // 2]),
                             ALU.mult).then_inc(sm["b_sin"], 1)
            ve.wait_ge(sm["b_cos"], j + 1)
            ve.wait_ge(sm["b_sin"], j + 1)
            ve.tensor_tensor(qk[:, :].rearrange("p (h d) -> p h d", d=DH), qk_c[:, :, :], qk_s[:, :, :], ALU.add)\
              .then_inc(sm["b_rope"], 1)
            ve.wait_ge(sm["b_v_act"], j + 1)
            for b in range(2, BT):
                last = ve.tensor_copy(Vb[b * S:(b + 1) * S, :, b, :],
                                      bk[4][b * S:(b + 1) * S, 0:D].rearrange("p (g n) -> p g n", g=G))
            last.then_inc(sm["b_v_dve"], 1)
            ve.wait_ge(sm["b_kT"], j + 1)
            ve.tensor_tensor(qTb[:, :, :, :, :].rearrange("p k b h s -> p (k b) h s"),
                             bk[5][:, 0:D].rearrange("p (kb s) -> p kb s", s=S).unsqueeze(2).broadcast_to([P, KH * BT, HG, S]),
                             block.unsqueeze(1).unsqueeze(3).broadcast_to([P, KH * BT, HG, S]), ALU.mult)\
              .then_inc(sm["b_qT"], 1)
            ve.wait_ge(sm["b_s_made"], j + 1)
            for gp in range(2):
                last = ve.scalar_tensor_tensor(
                    out=sc2[:, gp, :, :, :].rearrange("p g b s -> p (g b) s"),
                    in0=bk[6 + gp][:, 0:2 * BT * S].rearrange("p (q s) -> p q s", s=S), scalar=0.25,
                    in1=causal.unsqueeze(1).broadcast_to([P, 2 * BT, S]), op0=ALU.mult, op1=ALU.add)
            last.then_inc(sm["b_scaled"], 1)
            flat = lambda t: t[:, :, :, :, :].rearrange("p a g b s -> p (a g b) s")
            ve.wait_ge(sm["b_scaled"], j + 1)
            ve.tensor_reduce(mx2[:, :], flat(sc2), X, ALU.max).then_inc(sm["b_max"], 1)
            ve.wait_ge(sm["b_max"], j + 1)
            ve.tensor_tensor(flat(sc2m), flat(sc2), mx2[:, :].unsqueeze(2).broadcast_to([P, NH, S]), ALU.subtract)\
              .then_inc(sm["b_shift"], 1)
            ve.wait_ge(sm["b_exp"], j + 1)
            ve.tensor_reduce(sum2[:, :], flat(pr2), X, ALU.add).then_inc(sm["b_sum"], 1)
            ve.wait_ge(sm["b_sum"], j + 1)
            ve.reciprocal(inv2[:, :], sum2[:, :]).then_inc(sm["b_inv"], 1)
            ve.wait_ge(sm["b_inv"], j + 1)
            ve.tensor_tensor(flat(pr2n), flat(pr2), inv2[:, :].unsqueeze(2).broadcast_to([P, NH, S]), ALU.mult)\
              .then_inc(sm["b_p"], 1)
            ve.wait_ge(sm["b_o_made"], j + 1)
            for b in range(BT):
                for h in range(HG):
                    last = ve.tensor_copy(O2[b * S:(b + 1) * S, 2:4, h, :], picked(h, b, 1))
            last.then_inc(sm["b_o_dve"], 1)
            ve.wait_ge(sm["b_oT_hi"], j + 1)
            ve.tensor_tensor(OT_lo[:, :, :], bk[3][:, 0:KH * P].rearrange("p (k n) -> p k n", k=KH), f(OT_hi[:, :, :]),
                             ALU.subtract).then_inc(sm["b_oT_lo"], 1)
            ve.wait_ge(sm["b_wo_made"], j + 1)
            ve.tensor_tensor(at_j(x_sb, j), bk[4][:, 0:D], at_j(x_sb, j), ALU.add).then_inc(sm["b_x2"], 1)
            ve.wait_ge(sm["ones_set"], 1)
            ve.wait_ge(sm["b_x2"], j + 1)
            norm(j, "c", at_j(x_sb, j), y[:, :])
            ve.wait_ge(sm["c_hi"], j + 1)
            ve.tensor_tensor(y_lo[:, :], y[:, :], f(y_hi[:, :]), ALU.subtract).then_inc(sm["c_lo"], 1)

            count = [0]

            def chain(ins):
                ins.then_inc(sm["c_dve"], 1)
                count[0] += 1
                ve.wait_ge(sm["c_dve"], NCD * j + count[0])

            ve.wait_ge(sm["c_logits_made"], j + 1)
            chain(ve.tensor_reduce(rt[:, 0, 0:1], bk[6][:, 0:E], X, ALU.max, negate=True))
            ve.wait_ge(sm["c_exp"], j + 1)
            chain(ve.reciprocal(rt[:, 0, 2:3], rt[:, 0, 1:2]))
            chain(ve.tensor_scalar(rt[:, 2, :], rt[:, 1, :], rt[:, 0, 2:3], None, ALU.mult))
            for k, (src, one_hot, gate) in enumerate(((2, 10, 3), (7, 11, 4))):
                chain(ve.tensor_reduce(rt[:, 0, gate:gate + 1], rt[:, src, :], X, ALU.max))
                chain(ve.tensor_scalar(rt[:, 5, :], rt[:, src, :], rt[:, 0, gate:gate + 1], None, ALU.is_equal))
                chain(ve.tensor_tensor(rt[:, 6, :], rt[:, 5, :], expert_no, ALU.mult))
                chain(ve.tensor_reduce(rt[:, 0, 5:6], rt[:, 6, :], X, ALU.min))
                chain(ve.tensor_scalar(rt[:, one_hot, :], expert_no, rt[:, 0, 5:6], None, ALU.is_equal))
                if k == 0:
                    chain(ve.tensor_scalar(rt[:, 8, :], rt[:, 10, :], -1.0, 1.0, ALU.mult, ALU.add))
                    chain(ve.tensor_tensor(rt[:, 7, :], rt[:, 2, :], rt[:, 8, :], ALU.mult))
            chain(ve.tensor_scalar(rt[:, 12, :], rt[:, 10, :], rt[:, 0, 3:4], None, ALU.mult))
            ve.tensor_scalar(rt[:, 13, :], rt[:, 11, :], rt[:, 0, 4:5], None, ALU.mult).then_inc(sm["c_m12"], 1)
            ve.wait_ge(sm["c_m12"], j + 1)
            ve.wait_ge(sm["c_pos_made"], j + 1)
            chain(ve.tensor_scalar(rt[:, 14, :], bk[7][:, 2 * E:3 * E], float(CAP), None, ALU.min))
            chain(ve.tensor_tensor(rt[:, 15, :], bk[7][:, E:2 * E], rt[:, 14, :], ALU.add))
            slot_b = slot_no.unsqueeze(1).broadcast_to([P, E, CAP])
            wide = lambda a: a.unsqueeze(2).broadcast_to([P, E, CAP])
            chain(ve.tensor_tensor(eq1[:, :, :], slot_b, wide(bk[7][:, 0:E]), ALU.is_equal))
            chain(ve.tensor_tensor(eq1[:, :, :], eq1[:, :, :], wide(rt[:, 12, :]), ALU.mult))
            chain(ve.tensor_tensor(eq2[:, :, :], slot_b, wide(rt[:, 15, :]), ALU.is_equal))
            chain(ve.tensor_tensor(eq2[:, :, :], eq2[:, :, :], wide(rt[:, 13, :]), ALU.mult))
            chain(ve.tensor_tensor(eq1[:, :, :], eq1[:, :, :], eq2[:, :, :], ALU.add))
            assert count[0] == NCD, count[0]
            ve.tensor_copy(C_all[:, :, bass.ds(j, 1), :].rearrange("p e a c -> p (e a) c"), eq1[:, :, :])\
              .then_inc(sm["c_c"], 1)
            ve.tensor_scalar(disp[:, :], eq1[:, :, :].rearrange("p e c -> p (e c)"), 0.0, None, ALU.not_equal)\
              .then_inc(sm["c_disp"], 1)
            ve.wait_ge(sm["c_x_made"], j + 1)
            ve.tensor_copy(XT_lo[:, 0:KH, :, bass.ds(j * CAP, CAP)],
                           bk[1].rearrange("p (k e c) -> p k e c", k=KH, e=E)).then_inc(sm["c_x_lo"], 1)

        def expert(e, first):
            for t in range(HT + 1):
                if t < HT:
                    n, w = HT * e + t, width(t)
                    split_ready(ve, e, t)
                    ve.wait_ge(sm["split_act"], n + 1)
                    wait_freed(ve, "h_made", e, t, RW, first)
                    ve.tensor_tensor(W01_lo[:, t % RW, :, :, 0:w].rearrange("p i k n -> p (i k) n"),
                                     raw01[:, :, :, t * P:t * P + w].rearrange("p i k n -> p (i k) n"),
                                     f(W01_hi[:, t % RW, :, :, 0:w]).rearrange("p i k n -> p (i k) n"), ALU.subtract)\
                      .then_inc(sm["split_dve"], 1)
                if t >= 1:
                    tt = t - 1
                    n, w = HT * e + tt, width(tt)
                    ve.wait_ge(sm["gelu_done"], n + 1)
                    wait_freed(ve, "hhi_done", e, tt, 3, first)
                    wait_freed(ve, "hlo_done", e, tt, 3, first)
                    ve.tensor_tensor(hid[0:w, tt % 3, :], bk[3 + tt % 3][0:w, 0:SL], act[0:w, tt % 3, :], ALU.mult)\
                      .then_inc(sm["h_done"], 1)
                    ve.wait_ge(sm["hhi_done"], n + 1)
                    wait_freed(ve, "y_made", e, tt, 3, first)
                    ve.tensor_tensor(hid_lo[0:w, tt % 3, :], hid[0:w, tt % 3, :], f(hid_hi[0:w, tt % 3, :]), ALU.subtract)\
                      .then_inc(sm["hlo_done"], 1)
            ve.wait_ge(sm["y_made"], HT * (e + 1))
            for h in range(SP_):
                dst = Y[:, e, h, :] if isinstance(e, int) else Y[:, bass.ds(e, 1), h, :].rearrange("p a n -> p (a n)")
                ve.tensor_copy(dst, bk[6 + h][:, 0:D]).then_inc(sm["y_read"], 1)

        ve.wait_ge(sm["ct_read"], 4)
        expert(0, True)
        with ve.Fori(1, E) as e:
            expert(e, False)

        for j in range(TT):
            h, q = j // 4, j % 4
            ve.wait_ge(sm["comb_made"], h + 1)
            if j >= 4:
                ve.wait_ge(sm["out_done"], 16 * 4)
            ve.tensor_tensor(fin[:, j % 4, :], bk[4 * h + q][:, 0:D], x_sb[:, j, :], ALU.add).then_inc(sm["fin_done"], 1)

    @block_.gpsimd
    def _(po):
        po.wait_ge(sm["ones_set"], 1)
        po.wait_ge(sm["ln1_var"], 1)
        po.tensor_tensor(rstd[:, :], mv[:, :, 1], half[:, :], ALU.pow).then_inc(sm["ln1_rstd"], 1)
        po.wait_ge(sm["const_in"], 16)
        po.wait_ge(sm["bias_in"], 64)
        po.wait_ge(sm["ln1_done"], TT)
        for j in range(TT):
            po.tensor_tensor(x_sb[:, j, :], x_sb[:, j, :], bo_row[:, :], ALU.add).then_inc(sm["xbo_done"], 1)
        po.wait_ge(sm["first_act"], NS)

        def spread(b, r, first2):
            if not first2:
                po.wait_ge(sm["s_made"], 2 * b - 2)
            for_b = slice(b * S, (b + 1) * S) if isinstance(b, int) else bass.ds(b * S, S)
            po.tensor_tensor(Qb[:, r % 2, :, :, :], QT[:, :, for_b].unsqueeze(2).broadcast_to([P, KH, HG, S]),
                             block.unsqueeze(1).unsqueeze(3).broadcast_to([P, KH, HG, S]), ALU.mult)\
              .then_inc(sm["qb_ready"], 1)
            one = slice(b, b + 1) if isinstance(b, int) else bass.ds(b, 1)
            po.tensor_copy(KT[:, r % 2, :, 2 * P:SC], KLT[:, :, one]).then_inc(sm["kl_ready"], 1)

        spread(0, 0, True)

        def cross(j, first, last):
            for u in range(4):
                b = 4 * j + u
                if not last or u < 3:
                    spread(b + 1, (u + 1) % 4, first and u < 1)

        over_tiles(po, cross)

        po.wait_ge(sm["xbo_done"], TT)
        with po.Fori(0, TT) as j:
            for who in ("b", "c"):
                po.wait_ge(sm[who + "_var"], j + 1)
                po.tensor_tensor(ln_r[:, :], ln_mv[:, 1:2], half[:, 0:1], ALU.pow).then_inc(sm[who + "_r"], 1)

        po.wait_ge(sm["ct_made"], 4)

        def expert(e, first):
            for t in range(HT):
                n, w = HT * e + t, width(t)
                split_ready(po, e, t)
                wait_freed(po, "y_made", e, t, RW, first)
                po.sem_inc(sm["turns_po"], 1)
                po.tensor_copy(W2_hi[0:w, t % RW, :], raw2[0:w, t, :]).then_inc(sm["hi2"], 1)
                po.wait_ge(sm["hi2"], n + 1)
                po.tensor_tensor(W2_lo[0:w, t % RW, :], raw2[0:w, t, :], f(W2_hi[0:w, t % RW, :]), ALU.subtract)\
                  .then_inc(sm["split_pool"], 1)

        expert(0, True)
        with po.Fori(1, E) as e:
            expert(e, False)


_SQUARE = ["L0_xattn_Wq", "L0_xattn_Wk", "L0_xattn_Wv", "L0_xattn_Wo", "L0_attn_W_Q", "L0_attn_W_K", "L0_attn_W_V",
           "L0_attn_W_O"]
_INS = ["x", "ctx_1024", "mask_1x1xSxS2_ik1", *_SQUARE, "L0_xattn_bq", "L0_xattn_bk", "L0_xattn_bv", "L0_xattn_bo",
        "L0_ffn_router_w", "L0_ffn_w0_kernel", "L0_ffn_w1_kernel", "L0_ffn_wo_kernel"]


def make(nc, arrays):
    ap = {n: nc.dram_tensor(f"in_{n}", a.shape, mybir.dt.from_np(a.dtype), kind="ExternalInput").ap()
          for n, a in arrays.items()}
    out = nc.dram_tensor("out", (B, S, D), F32, kind="ExternalOutput").ap()
    build(nc, ap["x"], ap["ctx_1024"], ap["mask_1x1xSxS2_ik1"], [ap[n] for n in _SQUARE], ap["L0_xattn_bq"],
          ap["L0_xattn_bk"], ap["L0_xattn_bv"], ap["L0_xattn_bo"], ap["L0_ffn_router_w"], ap["L0_ffn_w0_kernel"],
          ap["L0_ffn_w1_kernel"], ap["L0_ffn_wo_kernel"], ap["table"], out)


def kernel(**inputs):
    import numpy as _np
    import concourse.bacc as _bacc
    from concourse.bass_utils import run_bass_kernel_spmd as _run

    nc = _bacc.Bacc("TRN2", target_bir_lowering=False, num_devices=1)
    arrays = {n: _np.ascontiguousarray(inputs[n]) for n in _INS}
    arrays["table"] = constants()
    make(nc, arrays)
    r = _run(nc, [{f"in_{n}": a for n, a in arrays.items()}], core_ids=[0])
    return r.results[0]["out"]
```

```python
from contextlib import ExitStack

import concourse.bass as bass
from concourse import mybir

F32 = mybir.dt.float32
F32R = mybir.dt.float32r
I32 = mybir.dt.int32
ALU = mybir.AluOpType
ACT = mybir.ActivationFunctionType
X = mybir.AxisListType.X

P = 128
B, S, D = 32, 32, 256
SC = 257
NH, DH = 16, 16
KH = D // P
BT = P // S
TT = B // BT
HG = P // S
G = NH // HG
E, CAP = 8, 32
HF = 1368
HT = -(-HF // P)
SL = TT * CAP
SP_ = SL // P
EPS = 1e-5
MASKED = -1e20
NC_ = 128 + 128 + 16 + 8 + 8 + 32 + 4 + 8 + 32


def constants():
    import numpy as np

    p = np.arange(P)
    ident = np.eye(P)
    before = (p[:, None] < p[None, :])
    freq = np.float32(10000.0) ** (np.float32(-2.0) * np.arange(DH // 2, dtype=np.float32) / np.float32(DH))
    angle = (p % S).astype(np.float32)[:, None] * freq
    cos, sin = np.cos(angle), np.sin(angle)
    causal = np.where(np.arange(S)[None, :] <= (p % S)[:, None], 0.0, -1e30)
    block = (p % 64)[:, None] // DH == np.arange(HG)
    expert = np.broadcast_to(np.arange(E) - E, (P, E))
    slot = np.broadcast_to(np.arange(CAP), (P, CAP))
    parts = [ident, before, np.repeat(cos, 2, 1), sin, -sin, causal, block, expert, slot]
    table = np.concatenate([np.asarray(t, np.float32) for t in parts], 1)
    assert table.shape == (P, NC_)
    return table


def build(nc, x, ctx_in, mask, weights, xbq, xbk, xbv, xbo, router, w0, w1, wo, table, out):
    with ExitStack() as stack:
        program(nc, stack, x, ctx_in, mask, weights, xbq, xbk, xbv, xbo, router, w0, w1, wo, table, out)


def program(nc, stack, x, ctx_in, mask, weights, xbq, xbk, xbv, xbo, router, w0, w1, wo, table, out):
    def sb(name, shape, dt=F32, scope=stack):
        return scope.enter_context(nc.sbuf_tensor(name, shape, dt))

    def f(ap):
        return ap.bitcast(F32)

    tab = sb("tab", [P, NC_])
    at = [0]

    def column(n):
        at[0] += n
        return tab[:, at[0] - n:at[0]]

    ident, before = column(P), column(P)
    cos16, sin8, nsin8 = column(DH), column(DH // 2), column(DH // 2)
    causal, block, expert_no, slot_no = column(S), column(HG), column(E), column(CAP)
    ones = sb("ones", [P, P])
    half = sb("half", [P, TT])
    WT_hi = sb("WT_hi", [P, 8, KH, D], F32R)
    WT_lo = sb("WT_lo", [P, 8, KH, D], F32R)
    x_sb = sb("x_sb", [P, TT, D])
    O_all = sb("O_all", [P, TT, D])
    stat_all = sb("stat_all", [P, TT, NH, 2])
    VL_all = sb("VL_all", [P, TT, D])
    bias_col = sb("bias_col", [P, 3 * KH])
    bq_col, bk_col, bv_col = (bias_col[:, KH * i:KH * i + KH] for i in range(3))
    bo_row = sb("bo_row", [P, D])
    router_sb = sb("router_sb", [P, KH, E])
    C_all = sb("C_all", [P, TT, E * CAP])
    XT_hi = sb("XT_hi", [P, KH, E, SL], F32R)
    XT_lo = sb("XT_lo", [P, KH, E, SL], F32R)

    early = ExitStack()
    mask_i = sb("mask_i", [P, SC], I32, early)
    mask_add = sb("mask_add", [P, SC], scope=early)
    QT = sb("QT", [P, KH, TT * P], scope=early)
    KLT = sb("KLT", [P, KH, B], scope=early)
    ctx_raw = sb("ctx_raw", [P, 4, KH, D], scope=early)
    prep = ExitStack()
    w_raw = sb("w_raw", [P, 8, KH, D], scope=prep)
    bias_raw = sb("bias_raw", [3 * KH, P], scope=prep)
    xn = sb("xn", [P, TT, D], scope=prep)
    bn = sb("bn", [P, TT, 6], scope=prep)
    mv = sb("mv", [P, TT, 2], scope=prep)
    rstd = sb("rstd", [P, TT], scope=prep)
    xnT_hi = sb("xnT_hi", [P, KH, TT * P], F32R, prep)
    xnT_lo = sb("xnT_lo", [P, KH, TT * P], F32R, prep)
    last_raw = sb("last_raw", [B, D], scope=prep)
    lastT_hi = sb("lastT_hi", [P, KH, B, S], F32R, prep)
    lastT_lo = sb("lastT_lo", [P, KH, B, S], F32R, prep)
    prep.close()
    ctxT_hi = sb("ctxT_hi", [P, 2, KH, 2 * P], F32R, early)
    ctxT_lo = sb("ctxT_lo", [P, 2, KH, 2 * P], F32R, early)
    KT = sb("KT", [P, 2, KH, SC + 1], scope=early)
    V = sb("V", [P, 4, 2, D], scope=early)
    Qb = sb("Qb", [P, 2, KH, HG, S], scope=early)
    Sc = sb("Sc", [P, 2, G, SC + 1], scope=early)
    Pr = sb("Pr", [P, 2, G, SC + 1], scope=early)
    nmax = sb("nmax", [P, 2, G], scope=early)
    PT = sb("PT", [P, 2, 2, G, P], scope=early)
    rinv = sb("rinv", [P, NH], scope=early)
    Ot = sb("Ot", [P, D], scope=early)
    OT_hi, OT_lo = sb("OT_hi", [P, KH, P], F32R, early), sb("OT_lo", [P, KH, P], F32R, early)
    ln_bn = {w: sb("ln_bn" + w, [P, 6], scope=early) for w in "bc"}
    ln_mv = {w: sb("ln_mv" + w, [P, 2], scope=early) for w in "bc"}
    ln_r = {w: sb("ln_r" + w, [P, 1], scope=early) for w in "bc"}
    y1, y2 = sb("y1", [P, D], scope=early), sb("y2", [P, D], scope=early)
    yT_hi, yT_lo = sb("yT_hi", [P, KH, P], F32R, early), sb("yT_lo", [P, KH, P], F32R, early)
    qk_s = sb("qk_s", [P, 2 * NH, DH], scope=early)
    qk = sb("qk", [P, 2 * D], scope=early)
    Vs = sb("Vs", [P, D], scope=early)
    kT = sb("kT", [P, KH, P], scope=early)
    qTb = sb("qTb", [P, KH, BT, HG, S], scope=early)
    sc2 = sb("sc2", [P, 2, 2, BT, S], scope=early)
    pr2 = sb("pr2", [P, 2, 2, BT, S], scope=early)
    mx2, sum2, inv2 = (sb(n, [P, NH], scope=early) for n in ("mx2", "sum2", "inv2"))
    PTd = sb("PTd", [P, G, HG, BT, S], scope=early)
    O2 = sb("O2", [P, D], scope=early)
    O2T_hi, O2T_lo = sb("O2T_hi", [P, KH, P], F32R, early), sb("O2T_lo", [P, KH, P], F32R, early)
    yTf = sb("yTf", [P, KH, P], scope=early)
    rt = sb("rt", [P, 16, E], scope=early)
    eq1, eq2 = sb("eq1", [P, E, CAP], scope=early), sb("eq2", [P, E, CAP], scope=early)
    disp = sb("disp", [P, E * CAP], scope=early)
    early.close()

    raw01 = sb("raw01", [P, 2, KH, HF])
    raw2 = sb("raw2", [P, HT, D])
    RW = 3
    W01_hi, W01_lo = sb("W01_hi", [P, RW, 2, KH, P], F32R), sb("W01_lo", [P, RW, 2, KH, P], F32R)
    act = sb("act", [P, 3, SL])
    W2_hi, W2_lo = sb("W2_hi", [P, RW, D], F32R), sb("W2_lo", [P, RW, D], F32R)
    hid = sb("hid", [P, 3, SL])
    hid_hi, hid_lo = sb("hid_hi", [P, 3, SL], F32R), sb("hid_lo", [P, 3, SL], F32R)
    CT = sb("CT", [P, TT, 2, P])
    Y = sb("Y", [P, TT, 2, D])
    fin = sb("fin", [P, 4, D])

    bank = stack.enter_context(nc.psum_tensor("bank", [P, 8, 512], F32))
    bk = [bank[:, i, :] for i in range(8)]

    names = """const_in x_in bias_in last_in router_in mask_in xbo_done
        ones_set maskb_set ln1_stats ln1_var ln1_rstd ln1_done
        first_made first_act first_dve
        ctx_turned ctx_hi ctx_lo k_made v_made k_ready kl_ready v_ready qb_ready s_made s_read
        p_ready sums_ready pt_made pt0_ready pt1_ready o_made o_read stats_moved
        a_inv a_last a_add a_norm a_oT_made a_oT_hi a_oT_lo a_wo_made a_x1
        b_bn b_mv b_var b_r b_y b_yT_made b_yT_hi b_yT_lo b_qk_made b_v_made b_cos b_sin b_rope b_v
        b_qkT_made b_kT b_qT b_s0_made b_s_made b_scaled b_max b_shift b_exp b_sum b_inv b_p b_pT_made b_pT_act b_pT_dve b_o_made b_o
        b_oT_made b_oT_hi b_oT_lo b_wo_made b_x2
        c_bn c_mv c_var c_r c_y c_yT_made c_yT c_logits_made c_dve c_exp c_m12 c_pos_made c_c c_disp
        c_x_made c_x_hi c_x_lo diag_zero
        split_act split_dve split_pool h_made gelu_done h_done hhi_done hlo_done y_made y_read
        y_read_act ct_made ct_read comb_made fin_done out_done hi2 turns_ve turns_po""".split()
    sm = {n: stack.enter_context(nc.semaphore(n)) for n in names}
    w_in = [stack.enter_context(nc.semaphore(f"w_in{i}")) for i in range(8)]
    ctx_in_sem = [stack.enter_context(nc.semaphore(f"ctx_in{i}")) for i in range(4)]
    CH = [(0, 4), (4, 8), (8, HT)]
    raw_in = [stack.enter_context(nc.semaphore(f"raw_in{i}")) for i in range(len(CH))]

    def width(t):
        return min(P, HF - t * P)

    def product3(pe, dst, a_hi, a_lo, b_hi, b_lo, first, last):
        pe.matmul(dst, a_hi, b_lo, start=first, stop=False)
        pe.matmul(dst, a_lo, b_hi, start=False, stop=False)
        return pe.matmul(dst, a_hi, b_hi, start=False, stop=last)

    def over_tiles(eng, tile):
        tile(0, True, False)
        with eng.Fori(1, TT - 1) as j:
            tile(j, False, False)
        tile(TT - 1, False, True)

    slots = [("bias", 0)] + [("w", i) for i in range(8)] + [("xT", c) for c in range(4)] + [("q", c) for c in range(4)]
    slots += [("lastT", 0), ("kl", 0)] + [("vl", c) for c in range(4)]
    by_dve = [k in ("w", "xT", "lastT") for k, _ in slots]

    def free_slot(eng, n):
        if n >= 8:
            eng.wait_ge(sm["first_act"], n - 7)
            if any(by_dve[:n - 7]):
                eng.wait_ge(sm["first_dve"], sum(by_dve[:n - 7]))

    NS = len(slots)

    RAW_DMAS = [3, 3, 4]

    def split_ready(eng, e, t):
        for c, (t0, t1) in enumerate(CH):
            if t == t0:
                eng.wait_ge(raw_in[c], 16 * RAW_DMAS[c] * (e + 1))

    def exists(n, count):
        return not isinstance(n, int) or 0 <= n < count

    def beyond(n, least):
        return not isinstance(n, int) or n >= least

    def one(n):
        return slice(n, n + 1) if isinstance(n, int) else bass.ds(n, 1)

    def tile_of(array, t):
        return array[:, one(t), :].rearrange("p a n -> p (a n)")

    def halves(ap):
        return ap.rearrange("p (k n) -> p k n", k=KH)

    def pipeline(step):
        def run(eng):
            for j in range(3):
                step(j)
            with eng.Fori(3, TT - 1) as j:
                step(j)
            for j in range(TT - 1, TT + 3):
                step(j)
        return run

    def wait_freed(eng, name, e, t, ring):
        if t >= ring:
            eng.wait_ge(sm[name], HT * (e + 1) + t - ring + 1)
        else:
            before_ = max(z for z in range(HT) if z % ring == t % ring)
            eng.wait_ge(sm[name], HT * e + before_ + 1)

    def done(e, t):
        return HT * (e + 1) + t + 1

    NCD = 23

    block_ = stack.enter_context(nc.Block())

    @block_.sync
    def _(sp):
        sp.dma_start(tab[:, :], table).then_inc(sm["const_in"], 16)
        for i in range(8):
            sp.dma_start(w_raw[:, i, :, :], weights[i].rearrange("(o p) n -> p o n", p=P)).then_inc(w_in[i], 16)
            if i == 0:
                sp.dma_start(x_sb[:, :, :], x.rearrange("(j b) s d -> (b s) j d", b=BT)).then_inc(sm["x_in"], 16)
        sp.dma_start(last_raw[:, :], ctx_in[:, SC - 1, :]).then_inc(sm["last_in"], 16)
        for h in range(HG):
            sp.dma_start(mask_i[h * S:(h + 1) * S, :], mask[0, 0]).then_inc(sm["mask_in"], 16)
        for i, vec in enumerate((xbq, xbk, xbv)):
            sp.dma_start(bias_raw[KH * i:KH * i + KH, :], vec.rearrange("(k p) -> k p", p=P)).then_inc(sm["bias_in"], 16)
        sp.dma_start(bo_row[:, :], xbo.rearrange("(a n) -> a n", a=1).broadcast_to([P, D])).then_inc(sm["bias_in"], 16)
        sp.dma_start(router_sb[:, :, :], router.rearrange("(k p) e -> p k e", p=P)).then_inc(sm["router_in"], 16)

        def load_ctx(j, first, last):
            for u in range(4):
                b = 4 * j + u
                if not first:
                    sp.wait_ge(sm["ctx_turned"], b - 3)
                src = ctx_in[bass.ds(b, 1), 0:2 * P, :] if not isinstance(b, int) else ctx_in[b:b + 1, 0:2 * P, :]
                sp.dma_start(ctx_raw[:, u, :, :], src.rearrange("a (t p) d -> p (a t) d", p=P)).then_inc(ctx_in_sem[u], 16)

        over_tiles(sp, load_ctx)

        def load_expert(e, first):
            for c, (t0, t1) in enumerate(CH):
                if not first:
                    for s in ("split_act", "split_dve", "split_pool"):
                        sp.wait_ge(sm[s], HT * e + t1)
                a, z = t0 * P, min(t1 * P, HF)
                for n, w in enumerate((w0, w1)):
                    src = w[bass.ds(e, 1), :, a:z] if not first else w[e:e + 1, :, a:z]
                    sp.dma_start(raw01[:, n, :, a:z], src.rearrange("a (k p) n -> p (a k) n", p=P)).then_inc(raw_in[c], 16)
                full = z // P * P
                src = wo[bass.ds(e, 1), a:full, :] if not first else wo[e:e + 1, a:full, :]
                sp.dma_start(raw2[:, t0:full // P, :], src.rearrange("a (t p) n -> p (a t) n", p=P)).then_inc(raw_in[c], 16)
                if full < z:
                    src = wo[bass.ds(e, 1), full:z, :] if not first else wo[e:e + 1, full:z, :]
                    sp.dma_start(raw2[0:z - full, HT - 1, :], src.rearrange("a p n -> p (a n)")).then_inc(raw_in[c], 16)

        sp.wait_ge(sm["o_read"], B)
        sp.wait_ge(sm["stats_moved"], B)
        load_expert(0, True)
        with sp.Fori(1, E) as e:
            load_expert(e, False)

        out_v = out.rearrange("(j b) s d -> (b s) j d", b=BT)
        for j in range(TT):
            sp.wait_ge(sm["fin_done"], j + 1)
            sp.dma_start(out_v[:, j, :], fin[:, j % 4, :]).then_inc(sm["out_done"], 16)
        sp.wait_ge(sm["out_done"], 16 * TT)

    @block_.tensor
    def _(pe):
        pe.wait_ge(sm["const_in"], 16)
        for n, (kind, i) in enumerate(slots):
            dst = bk[n % 8]
            free_slot(pe, n)
            if kind == "bias":
                pe.wait_ge(sm["bias_in"], 64)
                last = pe.transpose(dst[:, 0:3 * KH], bias_raw[:, :], ident[0:3 * KH, 0:3 * KH])
            elif kind == "w":
                pe.wait_ge(w_in[i], 16)
                for k in range(KH):
                    for o in range(KH):
                        last = pe.transpose(dst[:, k * D + o * P:k * D + (o + 1) * P],
                                            w_raw[:, i, o, k * P:(k + 1) * P], ident)
            elif kind == "xT":
                pe.wait_ge(sm["ln1_done"], 2 * i + 2)
                for k in range(KH):
                    for j in range(2):
                        last = pe.transpose(dst[:, k * D + j * P:k * D + (j + 1) * P],
                                            xn[:, 2 * i + j, k * P:(k + 1) * P], ident)
            elif kind == "q":
                t, n0 = i // 2, i % 2 * 512
                if i == 0:
                    pe.wait_ge(sm["first_act"], n)
                    pe.wait_ge(sm["first_dve"], n - 1)
                for k in range(KH):
                    last = product3(pe, dst, WT_hi[:, 0, k, t * P:(t + 1) * P], WT_lo[:, 0, k, t * P:(t + 1) * P],
                                    xnT_hi[:, k, n0:n0 + 512], xnT_lo[:, k, n0:n0 + 512], k == 0, k == KH - 1)
            elif kind == "lastT":
                pe.wait_ge(sm["last_in"], 16)
                for k in range(KH):
                    last = pe.transpose(dst[:, k * B:(k + 1) * B], last_raw[:, k * P:(k + 1) * P], ident[0:B, 0:B])
            elif kind == "kl":
                pe.wait_ge(sm["first_act"], n)
                pe.wait_ge(sm["first_dve"], sum(by_dve))
                for t in range(KH):
                    for k in range(KH):
                        last = product3(pe, dst[:, t * B:(t + 1) * B], WT_hi[:, 1, k, t * P:(t + 1) * P],
                                        WT_lo[:, 1, k, t * P:(t + 1) * P], lastT_hi[:, k, :, 0], lastT_lo[:, k, :, 0],
                                        k == 0, k == KH - 1)
            elif kind == "vl":
                for h in range(2):
                    b = (2 * i + h) * BT
                    for k in range(KH):
                        hi, lo = lastT_hi[:, k, b:b + BT, :], lastT_lo[:, k, b:b + BT, :]
                        last = product3(pe, dst[:, h * D:(h + 1) * D], hi, lo, WT_hi[:, 2, k, :], WT_lo[:, 2, k, :],
                                        k == 0, k == KH - 1)
            last.then_inc(sm["first_made"], 1)
        pe.wait_ge(sm["first_act"], NS)
        pe.wait_ge(sm["first_dve"], sum(by_dve))

        def turn_ctx(b, r, landed):
            if not exists(b, B):
                return
            pe.wait_ge(ctx_in_sem[r], landed)
            if beyond(b, 4):
                pe.wait_ge(sm["pt1_ready"], b - 3)
            elif b > 0:
                pe.wait_ge(sm["ctx_hi"], b)
                pe.wait_ge(sm["ctx_lo"], b)
            for k in range(KH):
                for t in range(2):
                    last = pe.transpose(bk[0][:, k * 2 * P + t * P:k * 2 * P + (t + 1) * P],
                                        ctx_raw[:, r, t, k * P:(k + 1) * P], ident)
            last.then_inc(sm["ctx_turned"], 1)

        def keys(b, r):
            if not exists(b, B):
                return
            pe.wait_ge(sm["ctx_hi"], b + 1)
            pe.wait_ge(sm["ctx_lo"], b + 1)
            if beyond(b, 1):
                pe.wait_ge(sm["k_ready"], b)
            for t in range(KH):
                for k in range(KH):
                    last = product3(pe, bk[1][:, t * D:(t + 1) * D], WT_hi[:, 1, k, t * P:(t + 1) * P],
                                    WT_lo[:, 1, k, t * P:(t + 1) * P], ctxT_hi[:, r % 2, k, :],
                                    ctxT_lo[:, r % 2, k, :], k == 0, k == KH - 1)
            last.then_inc(sm["k_made"], 1)

        def values(b, r):
            if not exists(b, B):
                return
            if beyond(b, 3):
                pe.wait_ge(sm["o_read"], b - 2)
            elif b > 0:
                pe.wait_ge(sm["v_ready"], b)
            for t in range(2):
                for k in range(KH):
                    last = product3(pe, bk[7][:, t * D:(t + 1) * D], ctxT_hi[:, r % 2, k, t * P:(t + 1) * P],
                                    ctxT_lo[:, r % 2, k, t * P:(t + 1) * P], WT_hi[:, 2, k, :], WT_lo[:, 2, k, :],
                                    k == 0, k == KH - 1)
            last.then_inc(sm["v_made"], 1)

        def energies(b, r, pair):
            if not exists(b, B):
                return
            if pair == 0:
                pe.wait_ge(sm["k_ready"], b + 1)
                pe.wait_ge(sm["kl_ready"], b + 1)
                pe.wait_ge(sm["qb_ready"], b + 1)
            if beyond(b, 1) or pair:
                pe.wait_ge(sm["s_read"], 4 * b + 2 * pair)
            for g in range(2):
                last = pe.matmul(bk[3 + g][:, 0:SC], Qb[64 * g:64 * g + 64, r % 2, pair, :, :],
                                 KT[64 * g:64 * g + 64, r % 2, pair, 0:SC], start=True, stop=True)
            last.then_inc(sm["s_made"], 1)

        def turn_probs(b, r, t):
            if not exists(b, B):
                return
            if t == 0:
                pe.wait_ge(sm["p_ready"], 4 * b + 4)
                if beyond(b, 1):
                    pe.wait_ge(sm["pt0_ready"], b)
            else:
                turned = min(b + 4, B) if isinstance(b, int) else b + 4
                pe.wait_ge(sm["ctx_hi"], turned)
                pe.wait_ge(sm["ctx_lo"], turned)
                if isinstance(b, int) and b > B - 4:
                    pe.wait_ge(sm["pt1_ready"], b)
            for g in range(G):
                last = pe.transpose(bk[5 - 5 * t][:, g * P:(g + 1) * P], Pr[:, r % 2, g, t * P:(t + 1) * P], ident)
            last.then_inc(sm["pt_made"], 1)

        def outputs(b, r):
            if not exists(b, B):
                return
            pe.wait_ge(sm["pt0_ready"], b + 1)
            pe.wait_ge(sm["pt1_ready"], b + 1)
            made = min(b + 3, B) if isinstance(b, int) else b + 3
            pe.wait_ge(sm["v_ready"], made)
            if isinstance(b, int) and b > B - 3:
                pe.wait_ge(sm["o_read"], b)
            for g in range(G):
                for t in range(2):
                    last = pe.matmul(bk[7][:, g * 64:(g + 1) * 64], PT[:, r % 2, t, g, :],
                                     V[:, r % 4, t, g * 64:(g + 1) * 64], start=t == 0, stop=t == 1)
            last.then_inc(sm["o_made"], 1)

        def turn_cross(t):
            if not exists(t, TT):
                return
            pe.wait_ge(sm["a_norm"], t + 1)
            if beyond(t, 1):
                pe.wait_ge(sm["b_scaled"], t)
            for k in range(KH):
                last = pe.transpose(bk[2][:, k * P:(k + 1) * P], Ot[:, k * P:(k + 1) * P], ident)
            last.then_inc(sm["a_oT_made"], 1)

        def project_cross(t):
            if not exists(t, TT):
                return
            pe.wait_ge(sm["a_oT_hi"], t + 1)
            pe.wait_ge(sm["a_oT_lo"], t + 1)
            for k in range(KH):
                last = product3(pe, bk[2][:, 0:D], OT_hi[:, k, :], OT_lo[:, k, :], WT_hi[:, 3, k, :], WT_lo[:, 3, k, :],
                                k == 0, k == KH - 1)
            last.then_inc(sm["a_wo_made"], 1)

        def turn_norm(t):
            if not exists(t, TT):
                return
            pe.wait_ge(sm["b_y"], t + 1)
            for k in range(KH):
                last = pe.transpose(bk[2][:, k * P:(k + 1) * P], y1[:, k * P:(k + 1) * P], ident)
            last.then_inc(sm["b_yT_made"], 1)

        def project_self(t, of_values):
            if not exists(t, TT):
                return
            if of_values:
                pe.wait_ge(sm["b_cos"], t + 1)
                pe.wait_ge(sm["b_sin"], t + 1)
            else:
                pe.wait_ge(sm["b_yT_hi"], t + 1)
                pe.wait_ge(sm["b_yT_lo"], t + 1)
            for n, i in enumerate((6,) if of_values else (4, 5)):
                for k in range(KH):
                    last = product3(pe, bk[2][:, n * D:n * D + D], yT_hi[:, k, :], yT_lo[:, k, :],
                                    WT_hi[:, i, k, :], WT_lo[:, i, k, :], k == 0, k == KH - 1)
            last.then_inc(sm["b_v_made" if of_values else "b_qk_made"], 1)

        def turn_qk(t):
            if not exists(t, TT):
                return
            pe.wait_ge(sm["b_rope"], t + 1)
            pe.wait_ge(sm["b_v"], t + 1)
            for i in range(4):
                last = pe.transpose(bk[2][:, i * P:(i + 1) * P], qk[:, i * P:(i + 1) * P], ident)
            last.then_inc(sm["b_qkT_made"], 1)

        def scores(t, gp):
            if not exists(t, TT):
                return
            if gp == 0:
                pe.wait_ge(sm["b_kT"], t + 1)
                pe.wait_ge(sm["b_qT"], t + 1)
            else:
                pe.wait_ge(sm["b_s0_made"], t + 1)
            for gh in range(2):
                for b in range(BT):
                    at_ = ((gp * 2 + gh) * BT + b) * S
                    last = pe.matmul(bk[2][:, at_:at_ + S], qTb[64 * gp:64 * gp + 64, gh, b, :, :],
                                     kT[64 * gp:64 * gp + 64, gh, b * S:(b + 1) * S], start=True, stop=True)
            last.then_inc(sm[("b_s0_made", "b_s_made")[gp]], 1)

        def turn_self_probs(t):
            if not exists(t, TT):
                return
            pe.wait_ge(sm["b_p"], t + 1)
            if beyond(t, 1):
                pe.wait_ge(sm["c_x_lo"], t)
            for g in range(G):
                last = pe.transpose(bk[6][:, g * P:(g + 1) * P], pr2[:, g % 2, g // 2, :, :], ident)
            last.then_inc(sm["b_pT_made"], 1)

        def self_outputs(t):
            if not exists(t, TT):
                return
            pe.wait_ge(sm["b_pT_act"], t + 1)
            pe.wait_ge(sm["b_pT_dve"], t + 1)
            for g in range(G):
                for h in range(HG):
                    c = (g * HG + h) * DH
                    last = pe.matmul(bk[6][:, c:c + DH], PTd[:, g, h, :, :], Vs[:, c:c + DH], start=True, stop=True)
            last.then_inc(sm["b_o_made"], 1)

        def turn_self(t):
            if not exists(t, TT):
                return
            pe.wait_ge(sm["b_o"], t + 1)
            for k in range(KH):
                last = pe.transpose(bk[6][:, k * P:(k + 1) * P], O2[:, k * P:(k + 1) * P], ident)
            last.then_inc(sm["b_oT_made"], 1)

        def project_out(t):
            if not exists(t, TT):
                return
            pe.wait_ge(sm["b_oT_hi"], t + 1)
            pe.wait_ge(sm["b_oT_lo"], t + 1)
            for k in range(KH):
                last = product3(pe, bk[6][:, 0:D], O2T_hi[:, k, :], O2T_lo[:, k, :], WT_hi[:, 7, k, :], WT_lo[:, 7, k, :],
                                k == 0, k == KH - 1)
            last.then_inc(sm["b_wo_made"], 1)

        def turn_router(t):
            if not exists(t, TT):
                return
            pe.wait_ge(sm["c_y"], t + 1)
            for k in range(KH):
                last = pe.transpose(bk[6][:, k * P:(k + 1) * P], y2[:, k * P:(k + 1) * P], ident)
            last.then_inc(sm["c_yT_made"], 1)

        def logits(t):
            if not exists(t, TT):
                return
            pe.wait_ge(sm["c_yT"], t + 1)
            for k in range(KH):
                last = pe.matmul(bk[6][:, 0:E], yTf[:, k, :], router_sb[:, k, :], start=k == 0, stop=k == KH - 1)
            last.then_inc(sm["c_logits_made"], 1)

        def positions(t):
            if not exists(t, TT):
                return
            pe.wait_ge(sm["c_m12"], t + 1)
            pe.matmul(bk[6][:, 0:2 * E], before, rt[:, 10:12, :], start=True, stop=True)
            pe.matmul(bk[6][:, 2 * E:3 * E], ones[:, :], rt[:, 10, :], start=True, stop=True)\
              .then_inc(sm["c_pos_made"], 1)

        def dispatch(t):
            if not exists(t, TT):
                return
            pe.wait_ge(sm["c_disp"], t + 1)
            for m in range(KH):
                last = pe.matmul(bk[6][:, m * D:(m + 1) * D], y2[:, m * P:(m + 1) * P], disp[:, :], start=True, stop=True)
            last.then_inc(sm["c_x_made"], 1)

        turn_ctx(0, 0, 16)
        keys(0, 0)
        values(0, 0)
        turn_ctx(1, 1, 16)

        def step(j):
            for u in range(4):
                b = 4 * j + u
                energies(b, u, 0)
                outputs(b - 2, (u - 2) % 4)
                if u == 0:
                    project_self(j - 2, True)
                    turn_router(j - 3)
                elif u == 1:
                    scores(j - 2, 0)
                    positions(j - 3)
                elif u == 2:
                    turn_cross(j - 1)
                    turn_self_probs(j - 2)
                else:
                    turn_norm(j - 1)
                    turn_self(j - 2)
                turn_ctx(b + 2, (u + 2) % 4, 16 * (j + 1 + (u + 2) // 4))
                energies(b, u, 1)
                if u == 0:
                    turn_qk(j - 2)
                    logits(j - 3)
                elif u == 1:
                    scores(j - 2, 1)
                elif u == 2:
                    project_cross(j - 1)
                    self_outputs(j - 2)
                else:
                    project_self(j - 1, False)
                    project_out(j - 2)
                keys(b + 1, (u + 1) % 4)
                turn_probs(b - 1, (u - 1) % 4, 0)
                if u == 1:
                    dispatch(j - 3)
                values(b + 1, (u + 1) % 4)
                turn_probs(b - 1, (u - 1) % 4, 1)

        pipeline(step)(pe)
        pe.wait_ge(sm["c_x_lo"], TT)

        for i in range(4):
            for q in range(4):
                t, k = 2 * i + q // 2, q % 2
                last = pe.transpose(bk[i][:, q * P:(q + 1) * P], C_all[:, t, k * P:(k + 1) * P], ident)
            last.then_inc(sm["ct_made"], 1)
        pe.wait_ge(sm["ct_read"], 4)

        def up(e, t):
            w = width(t)
            pe.wait_ge(sm["split_act"], done(e, t))
            pe.wait_ge(sm["split_dve"], done(e, t))
            wait_freed(pe, "h_done", e, t, 3)
            for i in range(2):
                for k in range(KH):
                    last = product3(pe, bk[3 * i + t % 3][0:w, 0:SL], W01_hi[:, t % RW, i, k, 0:w],
                                    W01_lo[:, t % RW, i, k, 0:w], XT_hi[:, k, one(e), :], XT_lo[:, k, one(e), :],
                                    k == 0, k == KH - 1)
            last.then_inc(sm["h_made"], 1)

        def down(e, t):
            w = width(t)
            pe.wait_ge(sm["hhi_done"], done(e, t))
            pe.wait_ge(sm["hlo_done"], done(e, t))
            pe.wait_ge(sm["split_pool"], done(e, t))
            if t == 0:
                pe.wait_ge(sm["y_read"], e + 1)
                pe.wait_ge(sm["y_read_act"], e + 1)
            for h in range(SP_):
                last = product3(pe, bk[6 + h][:, 0:D], hid_hi[0:w, t % 3, h * P:(h + 1) * P],
                                hid_lo[0:w, t % 3, h * P:(h + 1) * P], W2_hi[0:w, t % RW, :], W2_lo[0:w, t % RW, :],
                                t == 0, t == HT - 1)
            last.then_inc(sm["y_made"], 1)

        pe.sem_inc(sm["h_made"], HT)
        pe.sem_inc(sm["y_made"], HT)
        with pe.Fori(0, 2) as half_:
            for q in range(4):
                e = 4 * half_ + q
                for t in range(HT):
                    up(e, t)
                    if t >= 1:
                        down(e, t - 1)
                down(e, HT - 1)

        pe.wait_ge(sm["y_read"], E + 1)
        pe.wait_ge(sm["y_read_act"], E + 1)
        for t in range(TT):
            for k in range(2):
                last = pe.matmul(bk[t][:, 0:D], CT[:, t, k, :], Y[:, t, k, :], start=k == 0, stop=k == 1)
            last.then_inc(sm["comb_made"], 1)

    @block_.scalar
    def _(ac):
        for n, (kind, i) in enumerate(slots):
            src = bk[n % 8]
            ac.wait_ge(sm["first_made"], n + 1)
            if kind == "bias":
                last = ac.activation(bias_col[:, :], src[:, 0:3 * KH], ACT.Copy)
            elif kind == "w":
                last = ac.activation(WT_hi[:, i, :, :], src.rearrange("p (k n) -> p k n", k=KH), ACT.Copy)
            elif kind == "xT":
                last = ac.activation(xnT_hi[:, :, i * D:(i + 1) * D], src.rearrange("p (k n) -> p k n", k=KH), ACT.Copy)
            elif kind == "q":
                t, n0 = i // 2, i % 2 * 512
                last = ac.activation(QT[:, t, n0:n0 + 512], src, ACT.Identity, bias=bq_col[:, t:t + 1])
            elif kind == "lastT":
                last = ac.activation(lastT_hi[:, :, :, :].rearrange("p k b s -> p (k b) s"),
                                     src[:, 0:KH * B].unsqueeze(2).broadcast_to([P, KH * B, S]), ACT.Copy)
            elif kind == "kl":
                for t in range(KH):
                    last = ac.activation(KLT[:, t, :], src[:, t * B:(t + 1) * B], ACT.Identity, bias=bk_col[:, t:t + 1])
            elif kind == "vl":
                last = ac.activation(VL_all[:, 2 * i:2 * i + 2, :], src.rearrange("p (k n) -> p k n", k=2), ACT.Copy)
            last.then_inc(sm["first_act"], 1)

        def split_ctx(b, r):
            if not exists(b, B):
                return
            ac.wait_ge(sm["ctx_turned"], b + 1)
            if beyond(b, 2):
                ac.wait_ge(sm["v_made"], b - 1)
            ac.activation(ctxT_hi[:, r % 2, :, :], halves(bk[0]), ACT.Copy).then_inc(sm["ctx_hi"], 1)

        def keep_keys(b, r):
            if not exists(b, B):
                return
            ac.wait_ge(sm["k_made"], b + 1)
            if beyond(b, 2):
                ac.wait_ge(sm["s_made"], 2 * b - 2)
            for t in range(KH):
                last = ac.activation(KT[:, r % 2, t, 0:2 * P], bk[1][:, t * D:(t + 1) * D], ACT.Identity,
                                     bias=bk_col[:, t:t + 1])
            last.then_inc(sm["k_ready"], 1)

        def keep_values(b, r):
            if not exists(b, B):
                return
            ac.wait_ge(sm["v_made"], b + 1)
            if beyond(b, 4):
                ac.wait_ge(sm["o_made"], b - 3)
            ac.activation(V[:, r % 4, :, :], bk[7].rearrange("p (t n) -> p t n", t=2), ACT.Copy)\
              .then_inc(sm["v_ready"], 1)

        def exps(b, r, gs):
            if not exists(b, B):
                return
            for g in gs:
                ac.wait_ge(sm["s_read"], 4 * b + g + 1)
                if g == 0 and beyond(b, 2):
                    ac.wait_ge(sm["pt_made"], 2 * b - 2)
                    ac.wait_ge(sm["stats_moved"], b - 1)
                ac.activation(Pr[:, r % 2, g, 0:SC], Sc[:, r % 2, g, 0:SC], ACT.Exp, bias=nmax[:, r % 2, g:g + 1],
                              scale=-1.0, accum_out=Pr[:, r % 2, g, SC:SC + 1]).then_inc(sm["p_ready"], 1)

        def keep_probs(b, r):
            if not exists(b, B):
                return
            ac.wait_ge(sm["pt_made"], 2 * b + 1)
            if beyond(b, 2):
                ac.wait_ge(sm["o_made"], b - 1)
            ac.activation(PT[:, r % 2, 0, :, :], bk[5].rearrange("p (g n) -> p g n", g=G), ACT.Copy)\
              .then_inc(sm["pt0_ready"], 1)

        def keep(t, made, dst, src, ready):
            if not exists(t, TT):
                return
            ac.wait_ge(sm[made], t + 1)
            ac.activation(dst, src, ACT.Copy).then_inc(sm[ready], 1)

        def split_cross(t):
            if not exists(t, TT):
                return
            ac.wait_ge(sm["a_oT_made"], t + 1)
            for k in range(KH):
                last = ac.activation(OT_hi[:, k, :], bk[2][:, k * P:(k + 1) * P], ACT.Identity, bias=bv_col[:, k:k + 1])
            last.then_inc(sm["a_oT_hi"], 1)

        def self_exp(t):
            if not exists(t, TT):
                return
            ac.wait_ge(sm["b_shift"], t + 1)
            if beyond(t, 1):
                ac.wait_ge(sm["b_pT_made"], t)
            ac.activation(pr2[:, :, :, :, :], sc2[:, :, :, :, :], ACT.Exp).then_inc(sm["b_exp"], 1)

        def spread_probs(t):
            if not exists(t, TT):
                return
            ac.wait_ge(sm["diag_zero"], 1)
            ac.wait_ge(sm["b_pT_made"], t + 1)
            if beyond(t, 1):
                ac.wait_ge(sm["b_o_made"], t)
            for b in range(2):
                last = ac.activation(PTd[b * S:(b + 1) * S, :, :, b, :].rearrange("p g h s -> p (g h) s"),
                                     bk[6][b * S:(b + 1) * S, :].rearrange("p (gh s) -> p gh s", s=S), ACT.Copy)
            last.then_inc(sm["b_pT_act"], 1)

        def router_exp(t):
            if not exists(t, TT):
                return
            ac.wait_ge(sm["c_dve"], NCD * t + 1)
            ac.activation(rt[:, 1, :], bk[6][:, 0:E], ACT.Exp, bias=rt[:, 0, 0:1], accum_out=rt[:, 0, 1:2])\
              .then_inc(sm["c_exp"], 1)

        def keep_inputs(t):
            if not exists(t, TT):
                return
            ac.wait_ge(sm["c_x_made"], t + 1)
            cols = slice(t * CAP, (t + 1) * CAP) if isinstance(t, int) else bass.ds(t * CAP, CAP)
            ac.activation(XT_hi[:, :, :, cols], bk[6].rearrange("p (k e c) -> p k e c", k=KH, e=E), ACT.Copy)\
              .then_inc(sm["c_x_hi"], 1)

        split_ctx(0, 0)
        keep_keys(0, 0)
        keep_values(0, 0)
        split_ctx(1, 1)

        def step(j):
            for u in range(4):
                b = 4 * j + u
                exps(b, u, (0, 1))
                if u == 0:
                    keep(j - 2, "b_v_made", Vs[:, :], bk[2][:, 0:D], "b_v")
                    keep(j - 3, "c_yT_made", yTf[:, :, :], halves(bk[6][:, 0:D]), "c_yT")
                elif u == 2:
                    split_cross(j - 1)
                    spread_probs(j - 2)
                elif u == 3:
                    keep(j - 1, "b_yT_made", yT_hi[:, :, :], halves(bk[2][:, 0:D]), "b_yT_hi")
                    keep(j - 2, "b_oT_made", O2T_hi[:, :, :], halves(bk[6][:, 0:D]), "b_oT_hi")
                split_ctx(b + 2, u)
                exps(b, u, (2, 3))
                if u == 0:
                    keep(j - 2, "b_qkT_made", kT[:, :, :], halves(bk[2][:, D:2 * D]), "b_kT")
                    router_exp(j - 3)
                elif u == 1:
                    self_exp(j - 2)
                elif u == 2:
                    keep(j - 2, "b_o_made", O2[:, :], bk[6][:, 0:D], "b_o")
                keep_keys(b + 1, (u + 1) % 4)
                keep_probs(b - 1, (u - 1) % 4)
                if u == 1:
                    keep_inputs(j - 3)
                keep_values(b + 1, (u + 1) % 4)

        pipeline(step)(ac)

        for i in range(0, 4, 2):
            ac.wait_ge(sm["ct_made"], i + 2)
            for q in range(2):
                ac.activation(CT[:, 2 * (i + q):2 * (i + q) + 2, :, :],
                              bk[i + q].rearrange("p (t k n) -> p t k n", t=2, k=2), ACT.Copy).then_inc(sm["ct_read"], 1)

        ac.sem_inc(sm["split_act"], HT)
        ac.sem_inc(sm["gelu_done"], HT)
        ac.sem_inc(sm["hhi_done"], HT)
        ac.sem_inc(sm["y_read_act"], 1)
        with ac.Fori(0, 2) as half_:
            for q in range(4):
                e = 4 * half_ + q
                for t in range(HT + 1):
                    if t < HT:
                        w = width(t)
                        split_ready(ac, e, t)
                        wait_freed(ac, "h_made", e, t, RW)
                        ac.activation(W01_hi[:, t % RW, :, :, 0:w].rearrange("p i k n -> p (i k) n"),
                                      raw01[:, :, :, t * P:t * P + w].rearrange("p i k n -> p (i k) n"), ACT.Copy)\
                          .then_inc(sm["split_act"], 1)
                    if t >= 1:
                        tt = t - 1
                        w = width(tt)
                        ac.wait_ge(sm["h_made"], done(e, tt))
                        wait_freed(ac, "h_done", e, tt, 3)
                        ac.activation(act[0:w, tt % 3, :], bk[tt % 3][0:w, 0:SL], ACT.Gelu_apprx_tanh)\
                          .then_inc(sm["gelu_done"], 1)
                        ac.wait_ge(sm["h_done"], done(e, tt))
                        wait_freed(ac, "y_made", e, tt, 3)
                        ac.activation(hid_hi[0:w, tt % 3, :], hid[0:w, tt % 3, :], ACT.Copy).then_inc(sm["hhi_done"], 1)
                ac.wait_ge(sm["y_made"], done(e, HT - 1))
                for g in range(4):
                    dst = Y[q * CAP:(q + 1) * CAP, g, one(half_), :].rearrange("p a n -> p (a n)")
                    last = ac.activation(dst, bk[6][g * CAP:(g + 1) * CAP, 0:D], ACT.Copy)
                last.then_inc(sm["y_read_act"], 1)

    @block_.vector
    def _(ve):
        ve.memset(ones[:, :], 1.0)
        ve.memset(half[:, :], -0.5).then_inc(sm["ones_set"], 1)
        ve.wait_ge(sm["mask_in"], 64)
        ve.tensor_scalar(mask_add[:, :], mask_i[:, :], 0.0, MASKED * 4.0, ALU.is_equal, ALU.mult).then_inc(sm["maskb_set"], 1)
        ve.wait_ge(sm["x_in"], 16)
        for j in range(TT):
            ve.bn_stats(bn[:, j, :], x_sb[:, j, :]).then_inc(sm["ln1_stats"], 1)
        ve.wait_ge(sm["ln1_stats"], TT)
        for j in range(TT):
            ve.bn_aggr(mv[:, j, :], bn[:, j, :]).then_inc(sm["ln1_stats"], 1)
        ve.wait_ge(sm["ln1_stats"], 2 * TT)
        ve.tensor_scalar(mv[:, :, 1], mv[:, :, 1], EPS, None, ALU.add).then_inc(sm["ln1_var"], 1)
        ve.wait_ge(sm["ln1_rstd"], 1)
        for j in range(TT):
            ve.tensor_scalar(xn[:, j, :], x_sb[:, j, :], mv[:, j, 0:1], rstd[:, j:j + 1], ALU.subtract, ALU.mult)\
              .then_inc(sm["ln1_done"], 1)
        ve.wait_ge(sm["bias_in"], 64)
        for n, (kind, i) in enumerate(slots):
            if not by_dve[n]:
                continue
            ve.wait_ge(sm["first_act"], n + 1)
            src = bk[n % 8]
            if kind == "w":
                hi, lo = WT_hi[:, i, :, :], WT_lo[:, i, :, :]
            elif kind == "xT":
                hi, lo = xnT_hi[:, :, i * D:(i + 1) * D], xnT_lo[:, :, i * D:(i + 1) * D]
            if kind == "lastT":
                hi, lo = (z[:, :, :, :].rearrange("p k b s -> p (k b) s") for z in (lastT_hi, lastT_lo))
                src = src[:, 0:KH * B].unsqueeze(2).broadcast_to([P, KH * B, S])
            else:
                src = src.rearrange("p (k n) -> p k n", k=KH)
            ve.tensor_tensor(lo, src, f(hi), ALU.subtract).then_inc(sm["first_dve"], 1)

        def split_ctx(b, r):
            if not exists(b, B):
                return
            ve.wait_ge(sm["ctx_hi"], b + 1)
            if beyond(b, 2):
                ve.wait_ge(sm["v_made"], b - 1)
            ve.tensor_tensor(ctxT_lo[:, r % 2, :, :], halves(bk[0]), f(ctxT_hi[:, r % 2, :, :]), ALU.subtract)\
              .then_inc(sm["ctx_lo"], 1)

        def maxima(b, r, pair):
            if not exists(b, B):
                return
            ve.wait_ge(sm["s_made"], 2 * b + pair + 1)
            for q in range(2):
                g = 2 * pair + q
                if beyond(b, 2):
                    ve.wait_ge(sm["p_ready"], 4 * b - 7 + g)
                ve.sem_inc(sm["turns_ve"], 1)
                ve.tensor_tensor_reduce(Sc[:, r % 2, g, 0:SC], bk[3 + q][:, 0:SC], mask_add[:, :], -0.25, 3e38,
                                        ALU.add, ALU.min, nmax[:, r % 2, g:g + 1]).then_inc(sm["s_read"], 1)

        def rows_of(array, b, r):
            t = b // BT if isinstance(b, int) else (b - r) // BT
            return array[r * S:(r + 1) * S, one(t)]

        def keep_outputs(b, r):
            if not exists(b, B):
                return
            ve.wait_ge(sm["o_made"], b + 1)
            rows = rows_of(O_all, b, r).rearrange("p a n -> p (a n)").rearrange("p (g h d) -> p g h d", g=G, h=HG)
            for h in range(HG):
                src = bk[7][h * S:(h + 1) * S, 0:D].rearrange("p (g h d) -> p g h d", g=G, h=HG)[:, :, h, :]
                last = ve.tensor_copy(rows[:, :, h, :], src)
            last.then_inc(sm["o_read"], 1)

        def move_stats(b, r):
            ve.wait_ge(sm["p_ready"], 4 * b + 4)
            rows = rows_of(stat_all, b, r).rearrange("p a h k -> p (a h) k").rearrange("p (g h) k -> p g h k", h=HG)
            for h in range(HG):
                last = ve.tensor_copy(rows[:, :, h, :], Pr[h * S:(h + 1) * S, r % 2, :, SC - 1:SC + 1])
            last.then_inc(sm["stats_moved"], 1)

        def keep_probs(b, r):
            if not exists(b, B):
                return
            move_stats(b, r)
            ve.wait_ge(sm["pt_made"], 2 * b + 2)
            if beyond(b, 2):
                ve.wait_ge(sm["o_made"], b - 1)
            ve.tensor_copy(PT[:, r % 2, 1, :, :], bk[0].rearrange("p (g n) -> p g n", g=G)).then_inc(sm["pt1_ready"], 1)

        def invert_sums(t):
            if not exists(t, TT):
                return
            ve.wait_ge(sm["stats_moved"], BT * t + BT)
            if beyond(t, 1):
                ve.wait_ge(sm["a_norm"], t)
            ve.sem_inc(sm["turns_ve"], 1)
            ve.reciprocal(rinv[:, :], stat_all[:, one(t), :, 1].rearrange("p a h -> p (a h)")).then_inc(sm["a_inv"], 1)

        def split_cross(t):
            if not exists(t, TT):
                return
            ve.wait_ge(sm["a_oT_hi"], t + 1)
            for k in range(KH):
                last = ve.scalar_tensor_tensor(out=OT_lo[:, k, :], in0=bk[2][:, k * P:(k + 1) * P], scalar=bv_col[:, k:k + 1],
                                               in1=f(OT_hi[:, k, :]), op0=ALU.add, op1=ALU.subtract)
            last.then_inc(sm["a_oT_lo"], 1)

        def add_and_norm(t, made, src, who, dst):
            if not exists(t, TT):
                return
            ve.wait_ge(sm[made], t + 1)
            added = ("a_x1", "b_x2")[who == "c"]
            ve.tensor_tensor(tile_of(x_sb, t), src, tile_of(x_sb, t), ALU.add).then_inc(sm[added], 1)
            ve.wait_ge(sm[added], t + 1)
            if beyond(t, 1):
                ve.wait_ge(sm[who + "_y"], t)
            ve.sem_inc(sm["turns_ve"], 1)
            ve.bn_stats(ln_bn[who][:, :], tile_of(x_sb, t)).then_inc(sm[who + "_bn"], 1)
            ve.wait_ge(sm[who + "_bn"], t + 1)
            ve.sem_inc(sm["turns_ve"], 1)
            ve.bn_aggr(ln_mv[who][:, :], ln_bn[who][:, :]).then_inc(sm[who + "_mv"], 1)
            ve.wait_ge(sm[who + "_mv"], t + 1)
            ve.tensor_scalar(ln_mv[who][:, 1:2], ln_mv[who][:, 1:2], EPS, None, ALU.add).then_inc(sm[who + "_var"], 1)
            ve.wait_ge(sm[who + "_r"], t + 1)
            if beyond(t, 1):
                ve.wait_ge(sm["b_yT_made" if who == "b" else "c_x_made"], t)
            ve.tensor_scalar(dst, tile_of(x_sb, t), ln_mv[who][:, 0:1], ln_r[who][:, 0:1], ALU.subtract, ALU.mult)\
              .then_inc(sm[who + "_y"], 1)

        def low_parts(t, hi_done, lo, src, hi, ready):
            if not exists(t, TT):
                return
            ve.wait_ge(sm[hi_done], t + 1)
            ve.tensor_tensor(lo, src, f(hi), ALU.subtract).then_inc(sm[ready], 1)

        def rotate(t):
            if not exists(t, TT):
                return
            ve.wait_ge(sm["b_qk_made"], t + 1)
            if beyond(t, 1):
                ve.wait_ge(sm["b_qkT_made"], t)
            pq = bk[2].rearrange("p (h d) -> p h d", d=DH)
            turned = qk[:, :].rearrange("p (h d) -> p h d", d=DH)
            ve.tensor_tensor(turned, pq, cos16.unsqueeze(1).broadcast_to([P, 2 * NH, DH]), ALU.mult).then_inc(sm["b_cos"], 1)
            ve.tensor_tensor(qk_s[:, :, 0::2], pq[:, :, 1::2], nsin8.unsqueeze(1).broadcast_to([P, 2 * NH, DH // 2]),
                             ALU.mult)
            ve.tensor_tensor(qk_s[:, :, 1::2], pq[:, :, 0::2], sin8.unsqueeze(1).broadcast_to([P, 2 * NH, DH // 2]),
                             ALU.mult).then_inc(sm["b_sin"], 1)

        def spread_queries(t):
            if not exists(t, TT):
                return
            ve.wait_ge(sm["b_kT"], t + 1)
            if beyond(t, 1):
                ve.wait_ge(sm["b_s_made"], t)
            ve.tensor_tensor(qTb[:, :, :, :, :].rearrange("p k b h s -> p (k b) h s"),
                             bk[2][:, 0:D].rearrange("p (kb s) -> p kb s", s=S).unsqueeze(2).broadcast_to([P, KH * BT, HG, S]),
                             block.unsqueeze(1).unsqueeze(3).broadcast_to([P, KH * BT, HG, S]), ALU.mult)\
              .then_inc(sm["b_qT"], 1)

        flat = lambda t: t[:, :, :, :, :].rearrange("p a g b s -> p (a g b) s")

        def shift_scores(t):
            if not exists(t, TT):
                return
            ve.wait_ge(sm["b_s_made"], t + 1)
            if beyond(t, 1):
                ve.wait_ge(sm["b_exp"], t)
            ve.scalar_tensor_tensor(out=flat(sc2), in0=bk[2].rearrange("p (q s) -> p q s", s=S), scalar=0.25,
                                    in1=causal.unsqueeze(1).broadcast_to([P, NH, S]), op0=ALU.mult, op1=ALU.add)\
              .then_inc(sm["b_scaled"], 1)
            ve.wait_ge(sm["b_scaled"], t + 1)
            ve.tensor_reduce(mx2[:, :], flat(sc2), X, ALU.max).then_inc(sm["b_max"], 1)
            ve.wait_ge(sm["b_max"], t + 1)
            ve.tensor_tensor(flat(sc2), flat(sc2), mx2[:, :].unsqueeze(2).broadcast_to([P, NH, S]), ALU.subtract)\
              .then_inc(sm["b_shift"], 1)

        def normalise(t):
            if not exists(t, TT):
                return
            ve.wait_ge(sm["b_exp"], t + 1)
            ve.tensor_reduce(sum2[:, :], flat(pr2), X, ALU.add).then_inc(sm["b_sum"], 1)
            ve.wait_ge(sm["b_sum"], t + 1)
            ve.reciprocal(inv2[:, :], sum2[:, :]).then_inc(sm["b_inv"], 1)
            ve.wait_ge(sm["b_inv"], t + 1)
            ve.tensor_tensor(flat(pr2), flat(pr2), inv2[:, :].unsqueeze(2).broadcast_to([P, NH, S]), ALU.mult)\
              .then_inc(sm["b_p"], 1)

        def spread_probs(t):
            if not exists(t, TT):
                return
            ve.wait_ge(sm["diag_zero"], 1)
            ve.wait_ge(sm["b_pT_made"], t + 1)
            if beyond(t, 1):
                ve.wait_ge(sm["b_o_made"], t)
            for b in range(2, BT):
                last = ve.tensor_copy(PTd[b * S:(b + 1) * S, :, :, b, :].rearrange("p g h s -> p (g h) s"),
                                      bk[6][b * S:(b + 1) * S, :].rearrange("p (gh s) -> p gh s", s=S))
            last.then_inc(sm["b_pT_dve"], 1)

        count = [0]

        def chain(t, ins):
            ins.then_inc(sm["c_dve"], 1)
            count[0] += 1
            ve.wait_ge(sm["c_dve"], NCD * t + count[0])

        def choose(t):
            if not exists(t, TT):
                return
            count[0] = 0
            ve.wait_ge(sm["c_logits_made"], t + 1)
            chain(t, ve.tensor_reduce(rt[:, 0, 0:1], bk[6][:, 0:E], X, ALU.max, negate=True))
            ve.wait_ge(sm["c_exp"], t + 1)
            chain(t, ve.reciprocal(rt[:, 0, 2:3], rt[:, 0, 1:2]))
            chain(t, ve.tensor_scalar(rt[:, 2, :], rt[:, 1, :], rt[:, 0, 2:3], None, ALU.mult))
            for k, (src, one_hot, gate) in enumerate(((2, 10, 3), (7, 11, 4))):
                chain(t, ve.tensor_reduce(rt[:, 0, gate:gate + 1], rt[:, src, :], X, ALU.max))
                chain(t, ve.tensor_scalar(rt[:, 5, :], rt[:, src, :], rt[:, 0, gate:gate + 1], None, ALU.is_equal))
                chain(t, ve.tensor_tensor(rt[:, 6, :], rt[:, 5, :], expert_no, ALU.mult))
                chain(t, ve.tensor_reduce(rt[:, 0, 5:6], rt[:, 6, :], X, ALU.min))
                chain(t, ve.tensor_scalar(rt[:, one_hot, :], expert_no, rt[:, 0, 5:6], None, ALU.is_equal))
                if k == 0:
                    chain(t, ve.tensor_scalar(rt[:, 8, :], rt[:, 10, :], -1.0, 1.0, ALU.mult, ALU.add))
                    chain(t, ve.tensor_tensor(rt[:, 7, :], rt[:, 2, :], rt[:, 8, :], ALU.mult))
            chain(t, ve.tensor_scalar(rt[:, 12, :], rt[:, 10, :], rt[:, 0, 3:4], None, ALU.mult))
            ve.tensor_scalar(rt[:, 13, :], rt[:, 11, :], rt[:, 0, 4:5], None, ALU.mult).then_inc(sm["c_m12"], 1)
            ve.wait_ge(sm["c_m12"], t + 1)

        def combine_weights(t):
            if not exists(t, TT):
                return
            ve.wait_ge(sm["c_pos_made"], t + 1)
            chain(t, ve.tensor_scalar(rt[:, 14, :], bk[6][:, 2 * E:3 * E], float(CAP), None, ALU.min))
            chain(t, ve.tensor_tensor(rt[:, 15, :], bk[6][:, E:2 * E], rt[:, 14, :], ALU.add))
            slot_b = slot_no.unsqueeze(1).broadcast_to([P, E, CAP])
            wide = lambda a: a.unsqueeze(2).broadcast_to([P, E, CAP])
            chain(t, ve.tensor_tensor(eq1[:, :, :], slot_b, wide(bk[6][:, 0:E]), ALU.is_equal))
            chain(t, ve.tensor_tensor(eq1[:, :, :], eq1[:, :, :], wide(rt[:, 12, :]), ALU.mult))
            chain(t, ve.tensor_tensor(eq2[:, :, :], slot_b, wide(rt[:, 15, :]), ALU.is_equal))
            chain(t, ve.tensor_tensor(eq2[:, :, :], eq2[:, :, :], wide(rt[:, 13, :]), ALU.mult))
            chain(t, ve.tensor_tensor(tile_of(C_all, t), eq1[:, :, :].rearrange("p e c -> p (e c)"),
                                      eq2[:, :, :].rearrange("p e c -> p (e c)"), ALU.add))
            assert count[0] == NCD, count[0]
            if beyond(t, 1):
                ve.wait_ge(sm["c_x_made"], t)
            ve.tensor_scalar(disp[:, :], tile_of(C_all, t), 0.0, None, ALU.not_equal).then_inc(sm["c_disp"], 1)

        def keep_inputs(t):
            if not exists(t, TT):
                return
            ve.wait_ge(sm["c_x_hi"], t + 1)
            cols = slice(t * CAP, (t + 1) * CAP) if isinstance(t, int) else bass.ds(t * CAP, CAP)
            for k in range(KH):
                last = ve.tensor_tensor(XT_lo[:, k, :, cols], bk[6][:, k * D:(k + 1) * D].rearrange("p (e c) -> p e c", e=E),
                                        f(XT_hi[:, k, :, cols]), ALU.subtract)
            last.then_inc(sm["c_x_lo"], 1)

        split_ctx(0, 0)
        split_ctx(1, 1)
        ve.wait_ge(sm["maskb_set"], 1)

        def step(j):
            for u in range(4):
                b = 4 * j + u
                maxima(b, u, 0)
                keep_outputs(b - 2, (u - 2) % 4)
                if u == 1:
                    invert_sums(j - 1)
                    combine_weights(j - 3)
                elif u == 2:
                    split_cross(j - 1)
                    spread_probs(j - 2)
                elif u == 3:
                    low_parts(j - 1, "b_yT_hi", yT_lo[:, :, :], halves(bk[2][:, 0:D]), yT_hi[:, :, :], "b_yT_lo")
                    low_parts(j - 2, "b_oT_hi", O2T_lo[:, :, :], halves(bk[6][:, 0:D]), O2T_hi[:, :, :], "b_oT_lo")
                split_ctx(b + 2, u)
                maxima(b, u, 1)
                if u == 0:
                    spread_queries(j - 2)
                    choose(j - 3)
                elif u == 1:
                    shift_scores(j - 2)
                    keep_inputs(j - 3)
                elif u == 2:
                    add_and_norm(j - 1, "a_wo_made", bk[2][:, 0:D], "b", y1[:, :])
                else:
                    rotate(j - 1)
                    add_and_norm(j - 2, "b_wo_made", bk[6][:, 0:D], "c", y2[:, :])
                keep_probs(b - 1, (u - 1) % 4)
                if u == 1:
                    normalise(j - 2)

        pipeline(step)(ve)

        ve.wait_ge(sm["ct_read"], 4)
        ve.sem_inc(sm["split_dve"], HT)
        ve.sem_inc(sm["h_done"], HT)
        ve.sem_inc(sm["hlo_done"], HT)
        ve.sem_inc(sm["y_read"], 1)
        with ve.Fori(0, 2) as half_:
            for q in range(4):
                e = 4 * half_ + q
                for t in range(HT + 1):
                    if t < HT:
                        w = width(t)
                        split_ready(ve, e, t)
                        ve.wait_ge(sm["split_act"], done(e, t))
                        wait_freed(ve, "h_made", e, t, RW)
                        ve.tensor_tensor(W01_lo[:, t % RW, :, :, 0:w].rearrange("p i k n -> p (i k) n"),
                                         raw01[:, :, :, t * P:t * P + w].rearrange("p i k n -> p (i k) n"),
                                         f(W01_hi[:, t % RW, :, :, 0:w]).rearrange("p i k n -> p (i k) n"), ALU.subtract)\
                          .then_inc(sm["split_dve"], 1)
                    if t >= 1:
                        tt = t - 1
                        w = width(tt)
                        ve.wait_ge(sm["gelu_done"], done(e, tt))
                        wait_freed(ve, "hhi_done", e, tt, 3)
                        wait_freed(ve, "hlo_done", e, tt, 3)
                        ve.tensor_tensor(hid[0:w, tt % 3, :], bk[3 + tt % 3][0:w, 0:SL], act[0:w, tt % 3, :], ALU.mult)\
                          .then_inc(sm["h_done"], 1)
                        ve.wait_ge(sm["hhi_done"], done(e, tt))
                        wait_freed(ve, "y_made", e, tt, 3)
                        ve.tensor_tensor(hid_lo[0:w, tt % 3, :], hid[0:w, tt % 3, :], f(hid_hi[0:w, tt % 3, :]), ALU.subtract)\
                          .then_inc(sm["hlo_done"], 1)
                ve.wait_ge(sm["y_made"], done(e, HT - 1))
                for g in range(4):
                    dst = Y[q * CAP:(q + 1) * CAP, 4 + g, one(half_), :].rearrange("p a n -> p (a n)")
                    last = ve.tensor_copy(dst, bk[7][g * CAP:(g + 1) * CAP, 0:D])
                last.then_inc(sm["y_read"], 1)

        for j in range(TT):
            ve.wait_ge(sm["comb_made"], j + 1)
            if j >= 4:
                ve.wait_ge(sm["out_done"], 16 * 4)
            ve.tensor_tensor(fin[:, j % 4, :], bk[j][:, 0:D], x_sb[:, j, :], ALU.add).then_inc(sm["fin_done"], 1)

    @block_.gpsimd
    def _(po):
        po.wait_ge(sm["ones_set"], 1)
        po.wait_ge(sm["ln1_var"], 1)
        po.tensor_tensor(rstd[:, :], mv[:, :, 1], half[:, :], ALU.pow).then_inc(sm["ln1_rstd"], 1)
        po.wait_ge(sm["const_in"], 16)
        po.wait_ge(sm["bias_in"], 64)
        po.wait_ge(sm["ln1_done"], TT)
        for j in range(TT):
            po.tensor_tensor(x_sb[:, j, :], x_sb[:, j, :], bo_row[:, :], ALU.add).then_inc(sm["xbo_done"], 1)
        po.wait_ge(sm["first_act"], NS)
        po.wait_ge(sm["first_dve"], sum(by_dve))
        po.memset(PTd[:, :, :, :, :], 0.0).then_inc(sm["diag_zero"], 1)

        def spread(b, r):
            if not exists(b, B):
                return
            if beyond(b, 2):
                po.wait_ge(sm["s_made"], 2 * b - 2)
            for_b = slice(b * S, (b + 1) * S) if isinstance(b, int) else bass.ds(b * S, S)
            po.tensor_tensor(Qb[:, r % 2, :, :, :], QT[:, :, for_b].unsqueeze(2).broadcast_to([P, KH, HG, S]),
                             block.unsqueeze(1).unsqueeze(3).broadcast_to([P, KH, HG, S]), ALU.mult)\
              .then_inc(sm["qb_ready"], 1)
            po.tensor_copy(KT[:, r % 2, :, 2 * P:SC], KLT[:, :, one(b)]).then_inc(sm["kl_ready"], 1)

        def by_head(ap):
            return ap.rearrange("p (h d) -> p h d", d=DH)

        def finish_cross(t):
            if not exists(t, TT):
                return
            if beyond(t, 1):
                po.wait_ge(sm["a_oT_made"], t)
            po.wait_ge(sm["a_inv"], t + 1)
            prob = stat_all[:, one(t), :, 0].rearrange("p a h -> p (a h)")
            po.tensor_tensor(by_head(Ot[:, :]), by_head(tile_of(VL_all, t)), prob.unsqueeze(2).broadcast_to([P, NH, DH]),
                             ALU.mult).then_inc(sm["a_last"], 1)
            po.wait_ge(sm["o_read"], BT * t + BT)
            po.wait_ge(sm["a_last"], t + 1)
            po.tensor_tensor(Ot[:, :], Ot[:, :], tile_of(O_all, t), ALU.add).then_inc(sm["a_add"], 1)
            po.wait_ge(sm["a_add"], t + 1)
            po.tensor_tensor(by_head(Ot[:, :]), by_head(Ot[:, :]), rinv[:, :].unsqueeze(2).broadcast_to([P, NH, DH]),
                             ALU.mult).then_inc(sm["a_norm"], 1)

        def rotate(t):
            if not exists(t, TT):
                return
            po.wait_ge(sm["b_cos"], t + 1)
            po.wait_ge(sm["b_sin"], t + 1)
            po.tensor_tensor(qk[:, :], qk[:, :], qk_s[:, :, :].rearrange("p h d -> p (h d)"), ALU.add).then_inc(sm["b_rope"], 1)

        def power(t, who):
            if not exists(t, TT):
                return
            po.wait_ge(sm[who + "_var"], t + 1)
            po.tensor_tensor(ln_r[who][:, :], ln_mv[who][:, 1:2], half[:, 0:1], ALU.pow).then_inc(sm[who + "_r"], 1)

        spread(0, 0)
        po.wait_ge(sm["xbo_done"], TT)

        def step(j):
            for u in range(4):
                spread(4 * j + u + 1, (u + 1) % 4)
                if u == 1:
                    finish_cross(j - 1)
                elif u == 2:
                    power(j - 1, "b")
                elif u == 3:
                    rotate(j - 1)
                    power(j - 2, "c")

        pipeline(step)(po)

        po.wait_ge(sm["ct_made"], 4)
        po.sem_inc(sm["split_pool"], HT)
        with po.Fori(0, 2) as half_:
            for q in range(4):
                e = 4 * half_ + q
                for t in range(HT):
                    w = width(t)
                    split_ready(po, e, t)
                    wait_freed(po, "y_made", e, t, RW)
                    po.sem_inc(sm["turns_po"], 1)
                    po.tensor_copy(W2_hi[0:w, t % RW, :], raw2[0:w, t, :]).then_inc(sm["hi2"], 1)
                    po.wait_ge(sm["hi2"], HT * e + t + 1)
                    po.tensor_tensor(W2_lo[0:w, t % RW, :], raw2[0:w, t, :], f(W2_hi[0:w, t % RW, :]), ALU.subtract)\
                      .then_inc(sm["split_pool"], 1)


_SQUARE = ["L0_xattn_Wq", "L0_xattn_Wk", "L0_xattn_Wv", "L0_xattn_Wo", "L0_attn_W_Q", "L0_attn_W_K", "L0_attn_W_V",
           "L0_attn_W_O"]
_INS = ["x", "ctx_1024", "mask_1x1xSxS2_ik1", *_SQUARE, "L0_xattn_bq", "L0_xattn_bk", "L0_xattn_bv", "L0_xattn_bo",
        "L0_ffn_router_w", "L0_ffn_w0_kernel", "L0_ffn_w1_kernel", "L0_ffn_wo_kernel"]


def make(nc, arrays):
    ap = {n: nc.dram_tensor(f"in_{n}", a.shape, mybir.dt.from_np(a.dtype), kind="ExternalInput").ap()
          for n, a in arrays.items()}
    out = nc.dram_tensor("out", (B, S, D), F32, kind="ExternalOutput").ap()
    build(nc, ap["x"], ap["ctx_1024"], ap["mask_1x1xSxS2_ik1"], [ap[n] for n in _SQUARE], ap["L0_xattn_bq"],
          ap["L0_xattn_bk"], ap["L0_xattn_bv"], ap["L0_xattn_bo"], ap["L0_ffn_router_w"], ap["L0_ffn_w0_kernel"],
          ap["L0_ffn_w1_kernel"], ap["L0_ffn_wo_kernel"], ap["table"], out)


def kernel(**inputs):
    import numpy as _np
    import concourse.bacc as _bacc
    from concourse.bass_utils import run_bass_kernel_spmd as _run

    nc = _bacc.Bacc("TRN2", target_bir_lowering=False, num_devices=1)
    arrays = {n: _np.ascontiguousarray(inputs[n]) for n in _INS}
    arrays["table"] = constants()
    make(nc, arrays)
    r = _run(nc, [{f"in_{n}": a for n, a in arrays.items()}], core_ids=[0])
    return r.results[0]["out"]
```

```python
from contextlib import ExitStack

import concourse.bass as bass
from concourse import mybir

F32 = mybir.dt.float32
F32R = mybir.dt.float32r
I32 = mybir.dt.int32
ALU = mybir.AluOpType
ACT = mybir.ActivationFunctionType
X = mybir.AxisListType.X

P = 128
B, S, D = 32, 32, 256
SC = 257
NH, DH = 16, 16
KH = D // P
BT = P // S
TT = B // BT
HG = P // S
G = NH // HG
E, CAP = 8, 32
HF = 1368
HT = -(-HF // P)
SL = TT * CAP
WF = 3
SP_ = SL // P
EPS = 1e-5
RW, RH = 4, 3
EQ = 4
NT = EQ * HT
MASKED = -1e20
NC_ = 128 + 128 + 16 + 8 + 8 + 32 + 4 + 8 + 8 + 256


def constants():
    import numpy as np

    p = np.arange(P)
    ident = np.eye(P)
    before = (p[:, None] < p[None, :])
    freq = np.float32(10000.0) ** (np.float32(-2.0) * np.arange(DH // 2, dtype=np.float32) / np.float32(DH))
    angle = (p % S).astype(np.float32)[:, None] * freq
    cos, sin = np.cos(angle), np.sin(angle)
    causal = np.where(np.arange(S)[None, :] <= (p % S)[:, None], 0.0, -1e30)
    block = (p % 64)[:, None] // DH == np.arange(HG)
    expert = np.broadcast_to(np.arange(E) - E, (P, E))
    first_slot = np.broadcast_to(CAP * np.arange(E), (P, E))
    slot = np.broadcast_to(np.arange(E * CAP), (P, E * CAP))
    parts = [ident, before, np.repeat(cos, 2, 1), sin, -sin, causal, block, expert, first_slot, slot]
    table = np.concatenate([np.asarray(t, np.float32) for t in parts], 1)
    assert table.shape == (P, NC_)
    return table


def build(nc, x, ctx_in, mask, weights, xbq, xbk, xbv, xbo, router, w0, w1, wo, table, out):
    with ExitStack() as stack:
        program(nc, stack, x, ctx_in, mask, weights, xbq, xbk, xbv, xbo, router, w0, w1, wo, table, out)


def program(nc, stack, x, ctx_in, mask, weights, xbq, xbk, xbv, xbo, router, w0, w1, wo, table, out):
    def sb(name, shape, dt=F32, scope=stack):
        return scope.enter_context(nc.sbuf_tensor(name, shape, dt))

    def f(ap):
        return ap.bitcast(F32)

    tab = sb("tab", [P, NC_])
    at = [0]

    def column(n):
        at[0] += n
        return tab[:, at[0] - n:at[0]]

    ident, before = column(P), column(P)
    cos16, sin8, nsin8 = column(DH), column(DH // 2), column(DH // 2)
    causal, block, expert_no, first_slot, slot_no = column(S), column(HG), column(E), column(E), column(E * CAP)
    ones = sb("ones", [P, P])
    half = sb("half", [P, TT])
    WT_hi = sb("WT_hi", [P, 8, KH, D], F32R)
    WT_lo = sb("WT_lo", [P, 8, KH, D], F32R)
    x_sb = sb("x_sb", [P, TT, D])
    stat_all = sb("stat_all", [P, TT, NH, 2])
    crossed = ExitStack()
    O_all = sb("O_all", [P, TT, D], scope=crossed)
    VL_all = sb("VL_all", [P, TT, D], scope=crossed)
    crossed.close()
    y_hi, y_lo = sb("y_hi", [P, TT, D], F32R), sb("y_lo", [P, TT, D], F32R)
    bias_col = sb("bias_col", [P, 3 * KH])
    bq_col, bk_col, bv_col = (bias_col[:, KH * i:KH * i + KH] for i in range(3))
    bo_row = sb("bo_row", [P, D])
    router_sb = sb("router_sb", [P, KH, E])
    C_all = sb("C_all", [P, TT, E * CAP])
    XT_hi = sb("XT_hi", [P, KH, E, SL], F32R)
    XT_lo = sb("XT_lo", [P, KH, E, SL], F32R)

    early = ExitStack()
    mask_i = sb("mask_i", [P, SC], I32, early)
    mask_add = sb("mask_add", [P, SC], scope=early)
    QT = sb("QT", [P, KH, TT * P], scope=early)
    KLT = sb("KLT", [P, KH, B], scope=early)
    ctx_raw = sb("ctx_raw", [P, 4, KH, D], scope=early)
    prep = ExitStack()
    bias_raw = sb("bias_raw", [3 * KH, P], scope=prep)
    xn = sb("xn", [P, TT, D], scope=prep)
    bn = sb("bn", [P, TT, 6], scope=prep)
    mv = sb("mv", [P, TT, 2], scope=prep)
    rstd = sb("rstd", [P, TT], scope=prep)
    xnT_hi = sb("xnT_hi", [P, KH, TT * P], F32R, prep)
    xnT_lo = sb("xnT_lo", [P, KH, TT * P], F32R, prep)
    last_raw = sb("last_raw", [B, D], scope=prep)
    lastT_hi = sb("lastT_hi", [P, KH, B, S], F32R, prep)
    lastT_lo = sb("lastT_lo", [P, KH, B, S], F32R, prep)
    w_raw = sb("w_raw", [P, 8, KH, D], scope=prep)
    prep.close()
    ctxT_hi = sb("ctxT_hi", [P, 2, KH, 2 * P], F32R, early)
    ctxT_lo = sb("ctxT_lo", [P, 2, KH, 2 * P], F32R, early)
    KT = sb("KT", [P, 2, KH, SC + 1], scope=early)
    V = sb("V", [P, 4, 2, D], scope=early)
    Qb = sb("Qb", [P, 2, KH, HG, S], scope=early)
    Sc = sb("Sc", [P, 2, G, SC + 1], scope=early)
    Pr = sb("Pr", [P, 2, G, SC + 1], scope=early)
    nmax = sb("nmax", [P, 2, G], scope=early)
    PT = sb("PT", [P, 2, 2, G, P], scope=early)
    rinv = sb("rinv", [P, NH], scope=early)
    Ot = sb("Ot", [P, D], scope=early)
    OT_hi, OT_lo = sb("OT_hi", [P, KH, P], F32R, early), sb("OT_lo", [P, KH, P], F32R, early)
    ln_bn = {w: sb("ln_bn" + w, [P, 6], scope=early) for w in "bc"}
    ln_mv = {w: sb("ln_mv" + w, [P, 2], scope=early) for w in "bc"}
    ln_r = {w: sb("ln_r" + w, [P, 1], scope=early) for w in "bc"}
    y1, y2 = sb("y1", [P, D], scope=early), sb("y2", [P, D], scope=early)
    yT_hi, yT_lo = sb("yT_hi", [P, KH, P], F32R, early), sb("yT_lo", [P, KH, P], F32R, early)
    qk_s = sb("qk_s", [P, 2 * NH, DH], scope=early)
    qk = sb("qk", [P, 2 * D], scope=early)
    Vs = sb("Vs", [P, 2, NH, DH + 1], scope=early)
    kT = sb("kT", [P, KH, P], scope=early)
    qTb = sb("qTb", [P, KH, BT, HG, S], scope=early)
    sc2 = sb("sc2", [P, 2, 2, BT, S], scope=early)
    pr2 = sb("pr2", [P, 2, 2, BT, S], scope=early)
    mx2, inv2 = (sb(n, [P, NH], scope=early) for n in ("mx2", "inv2"))
    PTd = sb("PTd", [P, G, HG, BT, S], scope=early)
    O2 = sb("O2", [P, D], scope=early)
    O2T_hi, O2T_lo = sb("O2T_hi", [P, KH, P], F32R, early), sb("O2T_lo", [P, KH, P], F32R, early)
    yTf = sb("yTf", [P, KH, P], scope=early)
    lg, gates, eq_, pick, rest = (sb(n, [P, TT, E], scope=early) for n in ("lg", "gates", "eq", "pick", "rest"))
    chosen = sb("chosen", [P, 2, TT, E], scope=early)
    weighted = sb("weighted", [P, TT, E], scope=early)
    counted = sb("counted", [P, TT, E], scope=early)
    pos = sb("pos", [P, 2, TT, E], scope=early)
    over = sb("over", [P, 2, TT, E], scope=early)
    rmax, rsum, rinv_, lowest = (sb(n, [P, TT], scope=early) for n in ("rmax", "rsum", "rinv_", "lowest"))
    gate = sb("gate", [P, 2, TT], scope=early)
    slot_of = sb("slot_of", [P, 2, TT], scope=early)
    second = sb("second", [P, 2, E * CAP], scope=early)
    disp = sb("disp", [P, 2, E * CAP], F32R, early)
    early.close()

    raw01 = sb("raw01", [P, 2, KH, HF])
    raw2 = sb("raw2", [P, HT, D])
    W01_hi, W01_lo = sb("W01_hi", [P, RW, 2, KH, P], F32R), sb("W01_lo", [P, RW, 2, KH, P], F32R)
    CT = sb("CT", [P, TT, 2, P])
    act = sb("act", [P, RH, SL])
    W2_hi, W2_lo = sb("W2_hi", [P, RW, D], F32R), sb("W2_lo", [P, RW, D], F32R)
    hid = sb("hid", [P, RH, SL])
    hid_hi, hid_lo = sb("hid_hi", [P, RW, SL], F32R), sb("hid_lo", [P, RW, SL], F32R)
    Y = sb("Y", [P, TT, 2, D])
    fin = sb("fin", [P, 4, D])

    bank = stack.enter_context(nc.psum_tensor("bank", [P, 8, 512], F32))
    bk = [bank[:, i, :] for i in range(8)]

    names = """const_in x_in bias_in bo_in last_in w_made w_hi w_lo router_in mask_in xbo_done
        ones_set maskb_set ln1_stats ln1_var ln1_rstd ln1_done
        first_made first_act first_dve
        ctx_turned ctx_hi ctx_lo k_made v_made k_ready kl_ready v_ready qb_ready s_made s_read
        p_ready sums_ready pt_made pt0_ready pt1_ready o_made o_read stats_moved
        a_inv a_last a_add a_norm a_oT_made a_oT_hi a_oT_lo a_wo_made a_x1
        b_bn b_mv b_var b_r b_y b_yT_made b_yT_hi b_yT_lo b_qk_made b_v_made b_cos b_sin b_rope b_v
        b_qkT_made b_kT b_qT b_s0_made b_s_made b_scaled b_max b_shift b_exp b_inv b_pT_made b_pT_act b_pT_dve b_o_made b_o
        b_oT_made b_oT_hi b_oT_lo b_wo_made b_x2
        c_bn c_mv c_var c_r c_y c_yT_made c_yT c_logits_made c_lg c_rounded c_kept r_dve r_shifted r_exp r_chosen r_pos_made r_slots r_first r_both r_disp
        r_x_made r_x_kept diag_zero
        split_act split_dve split_pool h_made gelu_done h_done hhi_done hlo_done y_made
        y_read_act y_read_dve ct_made ct_read comb_made fin_done out_done hi2 turns_ve turns_po""".split()
    sm = {n: stack.enter_context(nc.semaphore(n)) for n in names}
    w_in = [stack.enter_context(nc.semaphore(f"w_in{i}")) for i in range(8)]
    ctx_in_sem = [stack.enter_context(nc.semaphore(f"ctx_in{i}")) for i in range(4)]
    CH = [(0, 4), (4, 8), (8, HT)]
    raw_in = [stack.enter_context(nc.semaphore(f"raw_in{i}")) for i in range(len(CH))]

    def width(t):
        return min(P, HF - t * P)

    def product3(pe, dst, a_hi, a_lo, b_hi, b_lo, first, last):
        pe.matmul(dst, a_hi, b_lo, start=first, stop=False)
        pe.matmul(dst, a_lo, b_hi, start=False, stop=False)
        return pe.matmul(dst, a_hi, b_hi, start=False, stop=last)

    slots = [("bias", 0)] + [("w", i) for i in range(WF)] + [("lastT", 0), ("kl", 0)] + [("vl", c) for c in range(4)]
    slots += [("xT", c) for c in range(4)] + [("q", c) for c in range(4)]
    by_dve = [k in ("w", "xT", "lastT") for k, _ in slots]

    def free_slot(eng, n):
        if n >= 8:
            eng.wait_ge(sm["first_act"], n - 7)
            if any(by_dve[:n - 7]):
                eng.wait_ge(sm["first_dve"], sum(by_dve[:n - 7]))

    NS = len(slots)

    RAW_DMAS = [3, 3, 4]

    def split_ready(eng, e, t):
        for c, (t0, t1) in enumerate(CH):
            if t == t0:
                eng.wait_ge(raw_in[c], 16 * RAW_DMAS[c] * (e + 1))

    def exists(n, count):
        return not isinstance(n, int) or 0 <= n < count

    def beyond(n, least):
        return not isinstance(n, int) or n >= least

    def one(n):
        return slice(n, n + 1) if isinstance(n, int) else bass.ds(n, 1)

    def tile_of(array, t):
        return array[:, one(t), :].rearrange("p a n -> p (a n)")

    def halves(ap):
        return ap.rearrange("p (k n) -> p k n", k=KH)

    def front(t):
        return bk[1] if isinstance(t, int) and t == TT - 1 else bk[2]

    def back(t):
        return bk[5] if isinstance(t, int) and t == TT - 1 else bk[6]

    def values_of(t):
        return Vs[:, int(isinstance(t, int) and t == TT - 1)]

    BATCHES = [(0, TT - 2), (TT - 2, TT)]

    def late_weights(j, u):
        return {0: (3, 4), 1: (5, 6), 2: (7,)}.get(u, ()) if isinstance(j, int) and j == 0 else ()

    def pipeline(step):
        def run(eng):
            for j in range(3):
                step(j)
            with eng.Fori(3, TT - 1) as j:
                step(j)
            step(TT - 1)
        return run

    def wait_freed(eng, name, half_, n, ring):
        eng.wait_ge(sm[name], NT * half_ + max(n - ring + 1, 0) + 1)

    def done(half_, n):
        return NT * half_ + n + 2

    block_ = stack.enter_context(nc.Block())

    @block_.sync
    def _(sp):
        def load_weight(i):
            sp.dma_start(w_raw[:, i, :, :], weights[i].rearrange("(o p) n -> p o n", p=P)).then_inc(w_in[i], 16)

        sp.dma_start(tab[:, :], table).then_inc(sm["const_in"], 16)
        for i in range(WF):
            load_weight(i)
        sp.dma_start(last_raw[:, :], ctx_in[:, SC - 1, :]).then_inc(sm["last_in"], 16)
        for i, vec in enumerate((xbq, xbk, xbv)):
            sp.dma_start(bias_raw[KH * i:KH * i + KH, :], vec.rearrange("(k p) -> k p", p=P)).then_inc(sm["bias_in"], 16)
        sp.dma_start(x_sb[:, :, :], x.rearrange("(j b) s d -> (b s) j d", b=BT)).then_inc(sm["x_in"], 16)
        sp.dma_start(bo_row[:, :], xbo.rearrange("(a n) -> a n", a=1).broadcast_to([P, D])).then_inc(sm["bo_in"], 16)
        for h in range(HG):
            sp.dma_start(mask_i[h * S:(h + 1) * S, :], mask[0, 0]).then_inc(sm["mask_in"], 16)

        def load_ctx(j, first):
            for u in range(4):
                b = 4 * j + u
                if not first:
                    sp.wait_ge(sm["ctx_turned"], b - 3)
                src = ctx_in[bass.ds(b, 1), 0:2 * P, :] if not isinstance(b, int) else ctx_in[b:b + 1, 0:2 * P, :]
                sp.dma_start(ctx_raw[:, u, :, :], src.rearrange("a (t p) d -> p (a t) d", p=P)).then_inc(ctx_in_sem[u], 16)

        load_ctx(0, True)
        for i in range(WF, 8):
            load_weight(i)
        sp.dma_start(router_sb[:, :, :], router.rearrange("(k p) e -> p k e", p=P)).then_inc(sm["router_in"], 16)
        with sp.Fori(1, TT) as j:
            load_ctx(j, False)

        def load_expert(e, first):
            for c, (t0, t1) in enumerate(CH):
                if not first:
                    for s in ("split_act", "split_dve", "split_pool"):
                        sp.wait_ge(sm[s], HT * (e - 1) + t1 + 1)
                a, z = t0 * P, min(t1 * P, HF)
                for n, w in enumerate((w0, w1)):
                    src = w[bass.ds(e, 1), :, a:z] if not first else w[e:e + 1, :, a:z]
                    sp.dma_start(raw01[:, n, :, a:z], src.rearrange("a (k p) n -> p (a k) n", p=P)).then_inc(raw_in[c], 16)
                full = z // P * P
                src = wo[bass.ds(e, 1), a:full, :] if not first else wo[e:e + 1, a:full, :]
                sp.dma_start(raw2[:, t0:full // P, :], src.rearrange("a (t p) n -> p (a t) n", p=P)).then_inc(raw_in[c], 16)
                if full < z:
                    src = wo[bass.ds(e, 1), full:z, :] if not first else wo[e:e + 1, full:z, :]
                    sp.dma_start(raw2[0:z - full, HT - 1, :], src.rearrange("a p n -> p (a n)")).then_inc(raw_in[c], 16)

        sp.wait_ge(sm["o_read"], B)
        sp.wait_ge(sm["stats_moved"], B)
        load_expert(0, True)
        with sp.Fori(1, E) as e:
            load_expert(e, False)
        sp.wait_ge(raw_in[0], 16 * RAW_DMAS[0] * E)
        sp.sem_inc(raw_in[0], 16 * RAW_DMAS[0])

        out_v = out.rearrange("(j b) s d -> (b s) j d", b=BT)
        for j in range(TT):
            sp.wait_ge(sm["fin_done"], j + 1)
            sp.dma_start(out_v[:, j, :], fin[:, j % 4, :]).then_inc(sm["out_done"], 16)
        sp.wait_ge(sm["out_done"], 16 * TT)

    @block_.tensor
    def _(pe):
        pe.wait_ge(sm["const_in"], 16)
        for n, (kind, i) in enumerate(slots):
            dst = bk[n % 8]
            free_slot(pe, n)
            if kind == "bias":
                pe.wait_ge(sm["bias_in"], 48)
                last = pe.transpose(dst[:, 0:3 * KH], bias_raw[:, :], ident[0:3 * KH, 0:3 * KH])
            elif kind == "w":
                pe.wait_ge(w_in[i], 16)
                for k in range(KH):
                    for o in range(KH):
                        last = pe.transpose(dst[:, k * D + o * P:k * D + (o + 1) * P],
                                            w_raw[:, i, o, k * P:(k + 1) * P], ident)
            elif kind == "xT":
                pe.wait_ge(sm["ln1_done"], 2 * i + 2)
                for k in range(KH):
                    for j in range(2):
                        last = pe.transpose(dst[:, k * D + j * P:k * D + (j + 1) * P],
                                            xn[:, 2 * i + j, k * P:(k + 1) * P], ident)
            elif kind == "q":
                t, n0 = i // 2, i % 2 * 512
                if i == 0:
                    pe.wait_ge(sm["first_act"], n)
                    pe.wait_ge(sm["first_dve"], sum(by_dve[:n]))
                for k in range(KH):
                    last = product3(pe, dst, WT_hi[:, 0, k, t * P:(t + 1) * P], WT_lo[:, 0, k, t * P:(t + 1) * P],
                                    xnT_hi[:, k, n0:n0 + 512], xnT_lo[:, k, n0:n0 + 512], k == 0, k == KH - 1)
            elif kind == "lastT":
                pe.wait_ge(sm["last_in"], 16)
                for k in range(KH):
                    last = pe.transpose(dst[:, k * B:(k + 1) * B], last_raw[:, k * P:(k + 1) * P], ident[0:B, 0:B])
            elif kind == "kl":
                pe.wait_ge(sm["first_act"], n)
                pe.wait_ge(sm["first_dve"], sum(by_dve[:n]))
                for t in range(KH):
                    for k in range(KH):
                        last = product3(pe, dst[:, t * B:(t + 1) * B], WT_hi[:, 1, k, t * P:(t + 1) * P],
                                        WT_lo[:, 1, k, t * P:(t + 1) * P], lastT_hi[:, k, :, 0], lastT_lo[:, k, :, 0],
                                        k == 0, k == KH - 1)
            elif kind == "vl":
                for h in range(2):
                    b = (2 * i + h) * BT
                    for k in range(KH):
                        hi, lo = lastT_hi[:, k, b:b + BT, :], lastT_lo[:, k, b:b + BT, :]
                        last = product3(pe, dst[:, h * D:(h + 1) * D], hi, lo, WT_hi[:, 2, k, :], WT_lo[:, 2, k, :],
                                        k == 0, k == KH - 1)
            last.then_inc(sm["first_made"], 1)
        pe.wait_ge(sm["first_act"], NS)
        pe.wait_ge(sm["first_dve"], sum(by_dve))

        def turn_ctx(b, r, landed):
            if not exists(b, B):
                return
            pe.wait_ge(ctx_in_sem[r], landed)
            if beyond(b, 4):
                pe.wait_ge(sm["pt1_ready"], b - 3)
            elif b > 0:
                pe.wait_ge(sm["ctx_hi"], b)
                pe.wait_ge(sm["ctx_lo"], b)
            for k in range(KH):
                for t in range(2):
                    last = pe.transpose(bk[0][:, k * 2 * P + t * P:k * 2 * P + (t + 1) * P],
                                        ctx_raw[:, r, t, k * P:(k + 1) * P], ident)
            last.then_inc(sm["ctx_turned"], 1)

        def keys(b, r):
            if not exists(b, B):
                return
            pe.wait_ge(sm["ctx_hi"], b + 1)
            pe.wait_ge(sm["ctx_lo"], b + 1)
            if beyond(b, 1):
                pe.wait_ge(sm["k_ready"], b)
            for t in range(KH):
                for k in range(KH):
                    last = product3(pe, bk[1][:, t * D:(t + 1) * D], WT_hi[:, 1, k, t * P:(t + 1) * P],
                                    WT_lo[:, 1, k, t * P:(t + 1) * P], ctxT_hi[:, r % 2, k, :],
                                    ctxT_lo[:, r % 2, k, :], k == 0, k == KH - 1)
            last.then_inc(sm["k_made"], 1)

        def values(b, r):
            if not exists(b, B):
                return
            if beyond(b, 3):
                pe.wait_ge(sm["o_read"], b - 2)
            elif b > 0:
                pe.wait_ge(sm["v_ready"], b)
            for t in range(2):
                for k in range(KH):
                    last = product3(pe, bk[7][:, t * D:(t + 1) * D], ctxT_hi[:, r % 2, k, t * P:(t + 1) * P],
                                    ctxT_lo[:, r % 2, k, t * P:(t + 1) * P], WT_hi[:, 2, k, :], WT_lo[:, 2, k, :],
                                    k == 0, k == KH - 1)
            last.then_inc(sm["v_made"], 1)

        def energies(b, r, pair):
            if not exists(b, B):
                return
            if pair == 0:
                pe.wait_ge(sm["k_ready"], b + 1)
                pe.wait_ge(sm["kl_ready"], b + 1)
                pe.wait_ge(sm["qb_ready"], b + 1)
            if beyond(b, 1) or pair:
                pe.wait_ge(sm["s_read"], 4 * b + 2 * pair)
            for g in range(2):
                last = pe.matmul(bk[3 + g][:, 0:SC], Qb[64 * g:64 * g + 64, r % 2, pair, :, :],
                                 KT[64 * g:64 * g + 64, r % 2, pair, 0:SC], start=True, stop=True)
            last.then_inc(sm["s_made"], 1)

        def turn_probs(b, r, t):
            if not exists(b, B):
                return
            if t == 0:
                pe.wait_ge(sm["p_ready"], 4 * b + 4)
                if beyond(b, 1):
                    pe.wait_ge(sm["pt0_ready"], b)
            else:
                turned = min(b + 4, B) if isinstance(b, int) else b + 4
                pe.wait_ge(sm["ctx_hi"], turned)
                pe.wait_ge(sm["ctx_lo"], turned)
                if isinstance(b, int) and b > B - 4:
                    pe.wait_ge(sm["pt1_ready"], b)
            for g in range(G):
                last = pe.transpose(bk[5 - 5 * t][:, g * P:(g + 1) * P], Pr[:, r % 2, g, t * P:(t + 1) * P], ident)
            last.then_inc(sm["pt_made"], 1)

        def outputs(b, r):
            if not exists(b, B):
                return
            pe.wait_ge(sm["pt0_ready"], b + 1)
            pe.wait_ge(sm["pt1_ready"], b + 1)
            made = min(b + 3, B) if isinstance(b, int) else b + 3
            pe.wait_ge(sm["v_ready"], made)
            if isinstance(b, int) and b > B - 3:
                pe.wait_ge(sm["o_read"], b)
            for g in range(G):
                for t in range(2):
                    last = pe.matmul(bk[7][:, g * 64:(g + 1) * 64], PT[:, r % 2, t, g, :],
                                     V[:, r % 4, t, g * 64:(g + 1) * 64], start=t == 0, stop=t == 1)
            last.then_inc(sm["o_made"], 1)

        def turn_weight(i):
            pe.wait_ge(w_in[i], 16)
            if i >= WF + 2:
                pe.wait_ge(sm["w_lo"], i - WF - 1)
            for k in range(KH):
                for o in range(KH):
                    last = pe.transpose(bk[(2, 6)[(i - WF) % 2]][:, k * D + o * P:k * D + (o + 1) * P],
                                        w_raw[:, i, o, k * P:(k + 1) * P], ident)
            last.then_inc(sm["w_made"], 1)

        def turn_cross(t):
            if not exists(t, TT):
                return
            pe.wait_ge(sm["a_norm"], t + 1)
            if isinstance(t, int) and t == 0:
                pe.wait_ge(sm["w_lo"], 8 - WF)
            if beyond(t, 1) and front(t) is bk[2]:
                pe.wait_ge(sm["b_scaled"], t)
            for k in range(KH):
                last = pe.transpose(front(t)[:, k * P:(k + 1) * P], Ot[:, k * P:(k + 1) * P], ident)
            last.then_inc(sm["a_oT_made"], 1)

        def project_cross(t):
            if not exists(t, TT):
                return
            pe.wait_ge(sm["a_oT_hi"], t + 1)
            pe.wait_ge(sm["a_oT_lo"], t + 1)
            for k in range(KH):
                last = product3(pe, front(t)[:, 0:D], OT_hi[:, k, :], OT_lo[:, k, :], WT_hi[:, 3, k, :], WT_lo[:, 3, k, :],
                                k == 0, k == KH - 1)
            last.then_inc(sm["a_wo_made"], 1)

        def turn_norm(t):
            if not exists(t, TT):
                return
            pe.wait_ge(sm["b_y"], t + 1)
            for k in range(KH):
                last = pe.transpose(front(t)[:, k * P:(k + 1) * P], y1[:, k * P:(k + 1) * P], ident)
            last.then_inc(sm["b_yT_made"], 1)

        def project_self(t, of_values):
            if not exists(t, TT):
                return
            if of_values:
                pe.wait_ge(sm["b_cos"], t + 1)
                pe.wait_ge(sm["b_sin"], t + 1)
            else:
                pe.wait_ge(sm["b_yT_hi"], t + 1)
                pe.wait_ge(sm["b_yT_lo"], t + 1)
            for n, i in enumerate((6,) if of_values else (4, 5)):
                for k in range(KH):
                    last = product3(pe, front(t)[:, n * D:n * D + D], yT_hi[:, k, :], yT_lo[:, k, :],
                                    WT_hi[:, i, k, :], WT_lo[:, i, k, :], k == 0, k == KH - 1)
            last.then_inc(sm["b_v_made" if of_values else "b_qk_made"], 1)

        def turn_qk(t):
            if not exists(t, TT):
                return
            pe.wait_ge(sm["b_rope"], t + 1)
            pe.wait_ge(sm["b_v"], t + 1)
            for i in range(4):
                last = pe.transpose(front(t)[:, i * P:(i + 1) * P], qk[:, i * P:(i + 1) * P], ident)
            last.then_inc(sm["b_qkT_made"], 1)

        def scores(t, gp, gh):
            if not exists(t, TT):
                return
            if (gp, gh) == (0, 0):
                pe.wait_ge(sm["b_kT"], t + 1)
                pe.wait_ge(sm["b_qT"], t + 1)
            elif (gp, gh) == (1, 0):
                pe.wait_ge(sm["b_s0_made"], t + 1)
            for b in range(BT):
                at_ = ((gp * 2 + gh) * BT + b) * S
                last = pe.matmul(front(t)[:, at_:at_ + S], qTb[64 * gp:64 * gp + 64, gh, b, :, :],
                                 kT[64 * gp:64 * gp + 64, gh, b * S:(b + 1) * S], start=True, stop=True)
            if gh == 1:
                last.then_inc(sm[("b_s0_made", "b_s_made")[gp]], 1)

        def turn_self_probs(t):
            if not exists(t, TT):
                return
            pe.wait_ge(sm["b_exp"], t + 1)
            for g in range(G):
                last = pe.transpose(back(t)[:, g * P:(g + 1) * P], pr2[:, g % 2, g // 2, :, :], ident)
            last.then_inc(sm["b_pT_made"], 1)

        def self_outputs(t, g):
            if not exists(t, TT):
                return
            if g == 0:
                pe.wait_ge(sm["b_pT_act"], t + 1)
                pe.wait_ge(sm["b_pT_dve"], t + 1)
            for h in range(HG):
                c = (g * HG + h) * (DH + 1)
                last = pe.matmul(back(t)[:, c:c + DH + 1], PTd[:, g, h, :, :], values_of(t)[:, g * HG + h, :], start=True, stop=True)
            if g == G - 1:
                last.then_inc(sm["b_o_made"], 1)

        def turn_self(t):
            if not exists(t, TT):
                return
            pe.wait_ge(sm["b_o"], t + 1)
            for k in range(KH):
                last = pe.transpose(back(t)[:, k * P:(k + 1) * P], O2[:, k * P:(k + 1) * P], ident)
            last.then_inc(sm["b_oT_made"], 1)

        def project_out(t):
            if not exists(t, TT):
                return
            pe.wait_ge(sm["b_oT_hi"], t + 1)
            pe.wait_ge(sm["b_oT_lo"], t + 1)
            for k in range(KH):
                last = product3(pe, back(t)[:, 0:D], O2T_hi[:, k, :], O2T_lo[:, k, :], WT_hi[:, 7, k, :], WT_lo[:, 7, k, :],
                                k == 0, k == KH - 1)
            last.then_inc(sm["b_wo_made"], 1)

        def turn_router(t):
            if not exists(t, TT):
                return
            pe.wait_ge(sm["c_y"], t + 1)
            for k in range(KH):
                last = pe.transpose(back(t)[:, k * P:(k + 1) * P], y2[:, k * P:(k + 1) * P], ident)
            last.then_inc(sm["c_yT_made"], 1)

        def logits(t):
            if not exists(t, TT):
                return
            pe.wait_ge(sm["c_yT"], t + 1)
            for k in range(KH):
                last = pe.matmul(back(t)[:, 0:E], yTf[:, k, :], router_sb[:, k, :], start=k == 0, stop=k == KH - 1)
            last.then_inc(sm["c_logits_made"], 1)

        turn_ctx(0, 0, 16)
        keys(0, 0)
        values(0, 0)
        turn_ctx(1, 1, 16)

        def step(j):
            for u in range(4):
                b = 4 * j + u
                energies(b, u, 0)
                if u == 0:
                    project_self(j - 2, True)
                    project_out(j - 3)
                elif u == 2:
                    turn_cross(j - 1)
                elif u == 3:
                    turn_norm(j - 1)
                turn_ctx(b + 2, (u + 2) % 4, 16 * (j + 1 + (u + 2) // 4))
                outputs(b - 2, (u - 2) % 4)
                if u == 0:
                    turn_qk(j - 2)
                elif u == 1:
                    scores(j - 2, 0, 1)
                elif u == 2:
                    turn_self_probs(j - 2)
                energies(b, u, 1)
                if u == 1:
                    logits(j - 3)
                elif u == 2:
                    project_cross(j - 1)
                elif u == 3:
                    project_self(j - 1, False)
                    turn_self(j - 2)
                keys(b + 1, (u + 1) % 4)
                if u == 0:
                    turn_router(j - 3)
                elif u == 1:
                    scores(j - 2, 1, 0)
                elif u == 2:
                    self_outputs(j - 2, 0)
                turn_probs(b - 1, (u - 1) % 4, 0)
                if u == 2:
                    self_outputs(j - 2, 1)
                turn_probs(b - 1, (u - 1) % 4, 1)
                if u == 1:
                    scores(j - 2, 1, 1)
                elif u == 2:
                    self_outputs(j - 2, 2)
                values(b + 1, (u + 1) % 4)
                if u == 0:
                    scores(j - 2, 0, 0)
                elif u == 2:
                    self_outputs(j - 2, 3)
                for i in late_weights(j, u):
                    turn_weight(i)

        pipeline(step)(pe)

        pe.sem_inc(sm["h_made"], 1)
        def positions(k):
            t0, t1 = BATCHES[k]
            n = (t1 - t0) * E
            pe.wait_ge(sm["r_chosen"], k + 1)
            pe.matmul(bk[0][:, 0:2 * n], before, chosen[:, :, t0:t1, :], start=True, stop=True)
            pe.matmul(bk[0][:, 2 * n:3 * n], ones[:, :], chosen[:, 0, t0:t1, :], start=True, stop=True)\
              .then_inc(sm["r_pos_made"], 1)

        def dispatch(t):
            pe.wait_ge(sm["c_kept"], t + 1)
            pe.wait_ge(sm["r_disp"], t + 1)
            if t >= 1:
                pe.wait_ge(sm["r_x_kept"], t)
            for i, src in enumerate((y_hi, y_lo)):
                for m in range(KH):
                    last = pe.matmul(bk[3 + i][:, m * D:(m + 1) * D], src[:, t, m * P:(m + 1) * P], disp[:, t % 2, :],
                                     start=True, stop=True)
            last.then_inc(sm["r_x_made"], 1)

        def turn_weights_of(i):
            if i >= 1:
                pe.wait_ge(sm["ct_read"], i)
            for q in range(4):
                t, k = 2 * i + q // 2, q % 2
                last = pe.transpose(bk[7][:, q * P:(q + 1) * P], C_all[:, t, k * P:(k + 1) * P], ident)
            last.then_inc(sm["ct_made"], 1)

        y_, z = TT - 2, TT - 1
        turn_probs(B - 1, (B - 1) % 4, 0)
        project_self(y_, True)
        project_out(y_ - 1)
        turn_probs(B - 1, (B - 1) % 4, 1)
        outputs(B - 2, (B - 2) % 4)
        turn_qk(y_)
        outputs(B - 1, (B - 1) % 4)
        turn_router(y_ - 1)
        scores(y_, 0, 0)
        scores(y_, 0, 1)
        turn_cross(z)
        scores(y_, 1, 0)
        project_cross(z)
        scores(y_, 1, 1)
        logits(y_ - 1)
        turn_norm(z)
        project_self(z, False)
        turn_self_probs(y_)
        project_self(z, True)
        turn_qk(z)
        self_outputs(y_, 0)
        self_outputs(y_, 1)
        scores(z, 0, 0)
        positions(0)
        scores(z, 0, 1)
        scores(z, 1, 0)
        scores(z, 1, 1)
        self_outputs(y_, 2)
        self_outputs(y_, 3)
        turn_self(y_)
        dispatch(0)
        turn_self_probs(z)
        project_out(y_)
        dispatch(1)
        for g in range(G):
            self_outputs(z, g)
        turn_router(y_)
        turn_self(z)
        logits(y_)
        dispatch(2)
        project_out(z)
        dispatch(3)
        turn_router(z)
        logits(z)
        dispatch(4)
        turn_weights_of(0)
        turn_weights_of(1)
        dispatch(5)
        turn_weights_of(2)
        positions(1)
        dispatch(y_)
        dispatch(z)
        turn_weights_of(3)
        pe.wait_ge(sm["r_x_kept"], TT)
        pe.wait_ge(sm["ct_read"], 4)

        def up(half_, n):
            if n >= NT:
                return
            e, t = EQ * half_ + n // HT, n % HT
            w = width(t)
            pe.wait_ge(sm["split_act"], done(half_, n))
            pe.wait_ge(sm["split_dve"], done(half_, n))
            wait_freed(pe, "h_done", half_, n, RH)
            for i in range(2):
                for k in range(KH):
                    last = product3(pe, bk[3 * i + n % RH][0:w, 0:SL], W01_hi[:, n % RW, i, k, 0:w],
                                    W01_lo[:, n % RW, i, k, 0:w], XT_hi[:, k, one(e), :], XT_lo[:, k, one(e), :],
                                    k == 0, k == KH - 1)
            last.then_inc(sm["h_made"], 1)

        def down(half_, n):
            q, t = n // HT, n % HT
            w = width(t)
            pe.wait_ge(sm["hhi_done"], done(half_, n))
            pe.wait_ge(sm["hlo_done"], done(half_, n))
            pe.wait_ge(sm["split_pool"], done(half_, n))
            if t == 0:
                for by in ("y_read_act", "y_read_dve"):
                    pe.wait_ge(sm[by], EQ * half_ + max(q - 1, 0) + 1)
            for h in range(SP_):
                last = product3(pe, bk[6 + q % 2][:, h * D:(h + 1) * D], hid_hi[0:w, n % RW, h * P:(h + 1) * P],
                                hid_lo[0:w, n % RW, h * P:(h + 1) * P], W2_hi[0:w, n % RW, :], W2_lo[0:w, n % RW, :],
                                t == 0 and h == 0, t == HT - 1 and h == SP_ - 1)
            last.then_inc(sm["y_made"], 1)

        pe.sem_inc(sm["y_made"], 1)
        with pe.Fori(0, E // EQ) as half_:
            up(half_, 0)
            up(half_, 1)
            for n in range(NT):
                up(half_, n + 2)
                down(half_, n)

        pe.wait_ge(sm["y_read_dve"], E + 1)
        pe.wait_ge(sm["y_read_act"], E + 1)
        for t in range(TT):
            for k in range(2):
                last = pe.matmul(bk[t][:, 0:D], CT[:, t, k, :], Y[:, t, k, :], start=k == 0, stop=k == 1)
            last.then_inc(sm["comb_made"], 1)

    @block_.scalar
    def _(ac):
        for n, (kind, i) in enumerate(slots):
            src = bk[n % 8]
            ac.wait_ge(sm["first_made"], n + 1)
            if kind == "bias":
                last = ac.activation(bias_col[:, :], src[:, 0:3 * KH], ACT.Copy)
            elif kind == "w":
                last = ac.activation(WT_hi[:, i, :, :], src.rearrange("p (k n) -> p k n", k=KH), ACT.Copy)
            elif kind == "xT":
                last = ac.activation(xnT_hi[:, :, i * D:(i + 1) * D], src.rearrange("p (k n) -> p k n", k=KH), ACT.Copy)
            elif kind == "q":
                t, n0 = i // 2, i % 2 * 512
                last = ac.activation(QT[:, t, n0:n0 + 512], src, ACT.Identity, bias=bq_col[:, t:t + 1])
            elif kind == "lastT":
                last = ac.activation(lastT_hi[:, :, :, :].rearrange("p k b s -> p (k b) s"),
                                     src[:, 0:KH * B].unsqueeze(2).broadcast_to([P, KH * B, S]), ACT.Copy)
            elif kind == "kl":
                for t in range(KH):
                    last = ac.activation(KLT[:, t, :], src[:, t * B:(t + 1) * B], ACT.Identity, bias=bk_col[:, t:t + 1])
            elif kind == "vl":
                last = ac.activation(VL_all[:, 2 * i:2 * i + 2, :], src.rearrange("p (k n) -> p k n", k=2), ACT.Copy)
            last.then_inc(sm["first_act"], 1)

        def split_weight(i):
            ac.wait_ge(sm["w_made"], i - WF + 1)
            ac.activation(WT_hi[:, i, :, :], halves(bk[(2, 6)[(i - WF) % 2]]), ACT.Copy).then_inc(sm["w_hi"], 1)

        def split_ctx(b, r):
            if not exists(b, B):
                return
            ac.wait_ge(sm["ctx_turned"], b + 1)
            if beyond(b, 2):
                ac.wait_ge(sm["v_made"], b - 1)
            ac.activation(ctxT_hi[:, r % 2, :, :], halves(bk[0]), ACT.Copy).then_inc(sm["ctx_hi"], 1)

        def keep_keys(b, r):
            if not exists(b, B):
                return
            ac.wait_ge(sm["k_made"], b + 1)
            if beyond(b, 2):
                ac.wait_ge(sm["s_made"], 2 * b - 2)
            for t in range(KH):
                last = ac.activation(KT[:, r % 2, t, 0:2 * P], bk[1][:, t * D:(t + 1) * D], ACT.Identity,
                                     bias=bk_col[:, t:t + 1])
            last.then_inc(sm["k_ready"], 1)

        def keep_values(b, r):
            if not exists(b, B):
                return
            ac.wait_ge(sm["v_made"], b + 1)
            if beyond(b, 4):
                ac.wait_ge(sm["o_made"], b - 3)
            ac.activation(V[:, r % 4, :, :], bk[7].rearrange("p (t n) -> p t n", t=2), ACT.Copy)\
              .then_inc(sm["v_ready"], 1)

        def exps(b, r, gs):
            if not exists(b, B):
                return
            for g in gs:
                ac.wait_ge(sm["s_read"], 4 * b + g + 1)
                if g == 0 and beyond(b, 2):
                    ac.wait_ge(sm["pt_made"], 2 * b - 2)
                    ac.wait_ge(sm["stats_moved"], b - 1)
                ac.activation(Pr[:, r % 2, g, 0:SC], Sc[:, r % 2, g, 0:SC], ACT.Exp, bias=nmax[:, r % 2, g:g + 1],
                              scale=-1.0, accum_out=Pr[:, r % 2, g, SC:SC + 1]).then_inc(sm["p_ready"], 1)

        def keep_probs(b, r):
            if not exists(b, B):
                return
            ac.wait_ge(sm["pt_made"], 2 * b + 1)
            if beyond(b, 2):
                ac.wait_ge(sm["o_made"], b - 1)
            ac.activation(PT[:, r % 2, 0, :, :], bk[5].rearrange("p (g n) -> p g n", g=G), ACT.Copy)\
              .then_inc(sm["pt0_ready"], 1)

        def keep(t, made, dst, src, ready):
            if not exists(t, TT):
                return
            ac.wait_ge(sm[made], t + 1)
            if made == "b_v_made" and beyond(t, 1) and front(t) is bk[2]:
                ac.wait_ge(sm["b_o_made"], t)
            ac.activation(dst, src, ACT.Copy).then_inc(sm[ready], 1)

        def split_cross(t):
            if not exists(t, TT):
                return
            ac.wait_ge(sm["a_oT_made"], t + 1)
            for k in range(KH):
                last = ac.activation(OT_hi[:, k, :], front(t)[:, k * P:(k + 1) * P], ACT.Identity, bias=bv_col[:, k:k + 1])
            last.then_inc(sm["a_oT_hi"], 1)

        def keep_self_values(t):
            keep(t, "b_v_made", values_of(t)[:, :, 0:DH], front(t)[:, 0:D].rearrange("p (h d) -> p h d", d=DH), "b_v")

        def split_norm(t):
            keep(t, "b_yT_made", yT_hi[:, :, :], halves(front(t)[:, 0:D]), "b_yT_hi")

        def keep_self_keys(t):
            keep(t, "b_qkT_made", kT[:, :, :], halves(front(t)[:, D:2 * D]), "b_kT")

        def split_self(t):
            keep(t, "b_oT_made", O2T_hi[:, :, :], halves(back(t)[:, 0:D]), "b_oT_hi")

        def keep_router(t):
            keep(t, "c_yT_made", yTf[:, :, :], halves(back(t)[:, 0:D]), "c_yT")

        def keep_logits(t):
            if exists(t, TT):
                keep(t, "c_logits_made", tile_of(lg, t), back(t)[:, 0:E], "c_lg")

        def self_exp(t):
            if not exists(t, TT):
                return
            ac.wait_ge(sm["b_shift"], t + 1)
            if beyond(t, 1):
                ac.wait_ge(sm["b_pT_made"], t)
            ac.activation(pr2[:, :, :, :, :], sc2[:, :, :, :, :], ACT.Exp).then_inc(sm["b_exp"], 1)

        def spread_probs(t):
            if not exists(t, TT):
                return
            ac.wait_ge(sm["diag_zero"], 1)
            ac.wait_ge(sm["b_pT_made"], t + 1)
            if beyond(t, 1):
                ac.wait_ge(sm["b_o_made"], t)
            for b in range(2):
                last = ac.activation(PTd[b * S:(b + 1) * S, :, :, b, :].rearrange("p g h s -> p (g h) s"),
                                     back(t)[b * S:(b + 1) * S, :].rearrange("p (gh s) -> p gh s", s=S), ACT.Copy)
            last.then_inc(sm["b_pT_act"], 1)

        split_ctx(0, 0)
        keep_keys(0, 0)
        keep_values(0, 0)
        split_ctx(1, 1)

        def step(j):
            for u in range(4):
                b = 4 * j + u
                exps(b, u, (0, 1))
                if u == 0:
                    keep_self_values(j - 2)
                elif u == 2:
                    split_cross(j - 1)
                elif u == 3:
                    split_norm(j - 1)
                split_ctx(b + 2, u)
                if u == 0:
                    keep_self_keys(j - 2)
                elif u == 2:
                    spread_probs(j - 2)
                exps(b, u, (2, 3))
                if u == 1:
                    keep_logits(j - 3)
                elif u == 3:
                    split_self(j - 2)
                keep_keys(b + 1, (u + 1) % 4)
                if u == 0:
                    keep_router(j - 3)
                keep_probs(b - 1, (u - 1) % 4)
                keep_values(b + 1, (u + 1) % 4)
                if u == 1:
                    self_exp(j - 2)
                for i in late_weights(j, u):
                    split_weight(i)

        pipeline(step)(ac)

        def split(half_, n):
            if n >= NT:
                return
            e, t = EQ * half_ + n // HT, n % HT
            w = width(t)
            split_ready(ac, e, t)
            wait_freed(ac, "h_made", half_, n, RW)
            ac.activation(W01_hi[:, n % RW, :, :, 0:w].rearrange("p i k n -> p (i k) n"),
                          raw01[:, :, :, t * P:t * P + w].rearrange("p i k n -> p (i k) n"), ACT.Copy)\
              .then_inc(sm["split_act"], 1)

        def keep_expert(half_, q):
            ac.wait_ge(sm["y_made"], done(half_, HT * q + HT - 1))
            for g in range(2):
                dst = Y[q * CAP:(q + 1) * CAP, g::4, one(half_), :].rearrange("p h a n -> p (h a) n")
                last = ac.activation(dst, halves(bk[6 + q % 2][g * CAP:(g + 1) * CAP, :]), ACT.Copy)
            last.then_inc(sm["y_read_act"], 1)

        ac.sem_inc(sm["split_act"], 1)
        ac.sem_inc(sm["gelu_done"], 1)
        ac.sem_inc(sm["hhi_done"], 1)
        ac.sem_inc(sm["y_read_act"], 1)

        def router_exp(k):
            t0, t1 = BATCHES[k]
            ac.wait_ge(sm["r_shifted"], k + 1)
            ac.activation(eq_[:, t0:t1, :], rest[:, t0:t1, :], ACT.Exp).then_inc(sm["r_exp"], 1)

        def keep_inputs(t):
            ac.wait_ge(sm["r_x_made"], t + 1)
            for i, dst in enumerate((XT_hi, XT_lo)):
                last = ac.activation(dst[:, :, :, t * CAP:(t + 1) * CAP],
                                     bk[3 + i].rearrange("p (k e c) -> p k e c", k=KH, e=E), ACT.Copy)
            last.then_inc(sm["r_x_kept"], 1)

        def keep_weights_of(i):
            ac.wait_ge(sm["ct_made"], i + 1)
            ac.activation(CT[:, 2 * i:2 * i + 2, :, :], bk[7].rearrange("p (t k n) -> p t k n", t=2, k=2), ACT.Copy)\
              .then_inc(sm["ct_read"], 1)

        y_, z = TT - 2, TT - 1
        keep_probs(B - 1, (B - 1) % 4)
        keep_self_values(y_)
        keep_self_keys(y_)
        keep_router(y_ - 1)
        split_cross(z)
        keep_logits(y_ - 1)
        split_norm(z)
        self_exp(y_)
        router_exp(0)
        spread_probs(y_)
        keep_self_values(z)
        keep_self_keys(z)
        self_exp(z)
        split_self(y_)
        keep_inputs(0)
        spread_probs(z)
        keep_inputs(1)
        keep_router(y_)
        split_self(z)
        keep_logits(y_)
        keep_inputs(2)
        keep_inputs(3)
        keep_router(z)
        keep_logits(z)
        keep_inputs(4)
        keep_weights_of(0)
        keep_weights_of(1)
        router_exp(1)
        for n in range(3):
            split(0, n)
        keep_inputs(5)
        keep_weights_of(2)
        keep_inputs(y_)
        keep_inputs(z)
        keep_weights_of(3)

        with ac.Fori(0, E // EQ) as half_:
            for n in range(NT):
                w = width(n % HT)
                ac.wait_ge(sm["h_made"], done(half_, n))
                wait_freed(ac, "h_done", half_, n, RH)
                ac.activation(act[0:w, n % RH, :], bk[n % RH][0:w, 0:SL], ACT.Gelu_apprx_tanh).then_inc(sm["gelu_done"], 1)
                split(half_, n + 3)
                ac.wait_ge(sm["h_done"], done(half_, n))
                wait_freed(ac, "y_made", half_, n, RW)
                ac.activation(hid_hi[0:w, n % RW, :], hid[0:w, n % RH, :], ACT.Copy).then_inc(sm["hhi_done"], 1)
                if n % HT == 2 and n > HT:
                    keep_expert(half_, n // HT - 1)
            split(half_ + 1, 0)
            keep_expert(half_, EQ - 1)
            split(half_ + 1, 1)
            split(half_ + 1, 2)

    @block_.vector
    def _(ve):
        ve.memset(ones[:, :], 1.0)
        ve.memset(half[:, :], -0.5).then_inc(sm["ones_set"], 1)

        def low(n, kind, i):
            ve.wait_ge(sm["first_act"], n + 1)
            src = bk[n % 8]
            if kind == "w":
                hi, lo = WT_hi[:, i, :, :], WT_lo[:, i, :, :]
            elif kind == "xT":
                hi, lo = xnT_hi[:, :, i * D:(i + 1) * D], xnT_lo[:, :, i * D:(i + 1) * D]
            if kind == "lastT":
                hi, lo = (z[:, :, :, :].rearrange("p k b s -> p (k b) s") for z in (lastT_hi, lastT_lo))
                src = src[:, 0:KH * B].unsqueeze(2).broadcast_to([P, KH * B, S])
            else:
                src = halves(src)
            ve.tensor_tensor(lo, src, f(hi), ALU.subtract).then_inc(sm["first_dve"], 1)

        for n, (kind, i) in enumerate(slots):
            if kind in ("w", "lastT"):
                low(n, kind, i)
        ve.wait_ge(sm["x_in"], 16)
        for j in range(TT):
            ve.bn_stats(bn[:, j, :], x_sb[:, j, :]).then_inc(sm["ln1_stats"], 1)
        ve.wait_ge(sm["ln1_stats"], TT)
        for j in range(TT):
            ve.bn_aggr(mv[:, j, :], bn[:, j, :]).then_inc(sm["ln1_stats"], 1)
        ve.wait_ge(sm["ln1_stats"], 2 * TT)
        ve.tensor_scalar(mv[:, :, 1], mv[:, :, 1], EPS, None, ALU.add).then_inc(sm["ln1_var"], 1)
        ve.wait_ge(sm["ln1_rstd"], 1)
        for j in range(TT):
            ve.tensor_scalar(xn[:, j, :], x_sb[:, j, :], mv[:, j, 0:1], rstd[:, j:j + 1], ALU.subtract, ALU.mult)\
              .then_inc(sm["ln1_done"], 1)
        for n, (kind, i) in enumerate(slots):
            if kind == "xT":
                low(n, kind, i)
        ve.wait_ge(sm["mask_in"], 64)
        ve.tensor_scalar(mask_add[:, :], mask_i[:, :], 0.0, MASKED * 4.0, ALU.is_equal, ALU.mult).then_inc(sm["maskb_set"], 1)

        def split_weight(i):
            ve.wait_ge(sm["w_hi"], i - WF + 1)
            ve.tensor_tensor(WT_lo[:, i, :, :], halves(bk[(2, 6)[(i - WF) % 2]]), f(WT_hi[:, i, :, :]), ALU.subtract)\
              .then_inc(sm["w_lo"], 1)

        def split_ctx(b, r):
            if not exists(b, B):
                return
            ve.wait_ge(sm["ctx_hi"], b + 1)
            if beyond(b, 2):
                ve.wait_ge(sm["v_made"], b - 1)
            ve.tensor_tensor(ctxT_lo[:, r % 2, :, :], halves(bk[0]), f(ctxT_hi[:, r % 2, :, :]), ALU.subtract)\
              .then_inc(sm["ctx_lo"], 1)

        def maxima(b, r, pair):
            if not exists(b, B):
                return
            ve.wait_ge(sm["s_made"], 2 * b + pair + 1)
            for q in range(2):
                g = 2 * pair + q
                if beyond(b, 2):
                    ve.wait_ge(sm["p_ready"], 4 * b - 7 + g)
                ve.sem_inc(sm["turns_ve"], 1)
                ve.tensor_tensor_reduce(Sc[:, r % 2, g, 0:SC], bk[3 + q][:, 0:SC], mask_add[:, :], -0.25, 3e38,
                                        ALU.add, ALU.min, nmax[:, r % 2, g:g + 1]).then_inc(sm["s_read"], 1)

        def rows_of(array, b, r):
            t = b // BT if isinstance(b, int) else (b - r) // BT
            return array[r * S:(r + 1) * S, one(t)]

        def keep_outputs(b, r):
            if not exists(b, B):
                return
            ve.wait_ge(sm["o_made"], b + 1)
            rows = rows_of(O_all, b, r).rearrange("p a n -> p (a n)").rearrange("p (g h d) -> p g h d", g=G, h=HG)
            for h in range(HG):
                src = bk[7][h * S:(h + 1) * S, 0:D].rearrange("p (g h d) -> p g h d", g=G, h=HG)[:, :, h, :]
                last = ve.tensor_copy(rows[:, :, h, :], src)
            last.then_inc(sm["o_read"], 1)

        def move_stats(b, r):
            ve.wait_ge(sm["p_ready"], 4 * b + 4)
            rows = rows_of(stat_all, b, r).rearrange("p a h k -> p (a h) k").rearrange("p (g h) k -> p g h k", h=HG)
            for h in range(HG):
                last = ve.tensor_copy(rows[:, :, h, :], Pr[h * S:(h + 1) * S, r % 2, :, SC - 1:SC + 1])
            last.then_inc(sm["stats_moved"], 1)

        def keep_probs(b, r, part):
            if not exists(b, B):
                return
            if part == 0:
                move_stats(b, r)
                return
            ve.wait_ge(sm["pt_made"], 2 * b + 2)
            if beyond(b, 2):
                ve.wait_ge(sm["o_made"], b - 1)
            ve.tensor_copy(PT[:, r % 2, 1, :, :], bk[0].rearrange("p (g n) -> p g n", g=G)).then_inc(sm["pt1_ready"], 1)

        def invert_sums(t):
            if not exists(t, TT):
                return
            ve.wait_ge(sm["stats_moved"], BT * t + BT)
            if beyond(t, 1):
                ve.wait_ge(sm["a_norm"], t)
            ve.sem_inc(sm["turns_ve"], 1)
            ve.reciprocal(rinv[:, :], stat_all[:, one(t), :, 1].rearrange("p a h -> p (a h)")).then_inc(sm["a_inv"], 1)

        def split_cross(t):
            if not exists(t, TT):
                return
            ve.wait_ge(sm["a_oT_hi"], t + 1)
            for k in range(KH):
                last = ve.scalar_tensor_tensor(out=OT_lo[:, k, :], in0=front(t)[:, k * P:(k + 1) * P], scalar=bv_col[:, k:k + 1],
                                               in1=f(OT_hi[:, k, :]), op0=ALU.add, op1=ALU.subtract)
            last.then_inc(sm["a_oT_lo"], 1)

        def add_and_norm(t, who, part):
            if not exists(t, TT):
                return
            made, src, dst = ("a_wo_made", front(t), y1) if who == "b" else ("b_wo_made", back(t), y2)
            if part == 1:
                ve.wait_ge(sm[who + "_r"], t + 1)
                if beyond(t, 1):
                    ve.wait_ge(sm["b_yT_made" if who == "b" else "c_kept"], t)
                ve.tensor_scalar(dst[:, :], tile_of(x_sb, t), ln_mv[who][:, 0:1], ln_r[who][:, 0:1], ALU.subtract, ALU.mult)\
                  .then_inc(sm[who + "_y"], 1)
                return
            ve.wait_ge(sm[made], t + 1)
            added = ("a_x1", "b_x2")[who == "c"]
            ve.tensor_tensor(tile_of(x_sb, t), src[:, 0:D], tile_of(x_sb, t), ALU.add).then_inc(sm[added], 1)
            ve.wait_ge(sm[added], t + 1)
            if beyond(t, 1):
                ve.wait_ge(sm[who + "_y"], t)
            ve.sem_inc(sm["turns_ve"], 1)
            ve.bn_stats(ln_bn[who][:, :], tile_of(x_sb, t)).then_inc(sm[who + "_bn"], 1)
            ve.wait_ge(sm[who + "_bn"], t + 1)
            ve.sem_inc(sm["turns_ve"], 1)
            ve.bn_aggr(ln_mv[who][:, :], ln_bn[who][:, :]).then_inc(sm[who + "_mv"], 1)
            ve.wait_ge(sm[who + "_mv"], t + 1)
            ve.tensor_scalar(ln_mv[who][:, 1:2], ln_mv[who][:, 1:2], EPS, None, ALU.add).then_inc(sm[who + "_var"], 1)

        def low_parts(t, hi_done, lo, src, hi, ready):
            if not exists(t, TT):
                return
            ve.wait_ge(sm[hi_done], t + 1)
            ve.tensor_tensor(lo, src, f(hi), ALU.subtract).then_inc(sm[ready], 1)

        def split_norm(t):
            low_parts(t, "b_yT_hi", yT_lo[:, :, :], halves(front(t)[:, 0:D]), yT_hi[:, :, :], "b_yT_lo")

        def split_self(t):
            low_parts(t, "b_oT_hi", O2T_lo[:, :, :], halves(back(t)[:, 0:D]), O2T_hi[:, :, :], "b_oT_lo")

        def rotate(t):
            if not exists(t, TT):
                return
            ve.wait_ge(sm["b_qk_made"], t + 1)
            if beyond(t, 1):
                ve.wait_ge(sm["b_qkT_made"], t)
            pq = front(t).rearrange("p (h d) -> p h d", d=DH)
            turned = qk[:, :].rearrange("p (h d) -> p h d", d=DH)
            ve.tensor_tensor(turned, pq, cos16.unsqueeze(1).broadcast_to([P, 2 * NH, DH]), ALU.mult).then_inc(sm["b_cos"], 1)
            ve.tensor_tensor(qk_s[:, :, 0::2], pq[:, :, 1::2], nsin8.unsqueeze(1).broadcast_to([P, 2 * NH, DH // 2]),
                             ALU.mult)
            ve.tensor_tensor(qk_s[:, :, 1::2], pq[:, :, 0::2], sin8.unsqueeze(1).broadcast_to([P, 2 * NH, DH // 2]),
                             ALU.mult).then_inc(sm["b_sin"], 1)

        def spread_queries(t):
            if not exists(t, TT):
                return
            ve.wait_ge(sm["b_kT"], t + 1)
            if beyond(t, 1):
                ve.wait_ge(sm["b_s_made"], t)
            ve.tensor_tensor(qTb[:, :, :, :, :].rearrange("p k b h s -> p (k b) h s"),
                             front(t)[:, 0:D].rearrange("p (kb s) -> p kb s", s=S).unsqueeze(2).broadcast_to([P, KH * BT, HG, S]),
                             block.unsqueeze(1).unsqueeze(3).broadcast_to([P, KH * BT, HG, S]), ALU.mult)\
              .then_inc(sm["b_qT"], 1)

        flat = lambda t: t[:, :, :, :, :].rearrange("p a g b s -> p (a g b) s")

        def shift_scores(t):
            if not exists(t, TT):
                return
            ve.wait_ge(sm["b_s_made"], t + 1)
            if beyond(t, 1):
                ve.wait_ge(sm["b_exp"], t)
            ve.scalar_tensor_tensor(out=flat(sc2), in0=front(t).rearrange("p (q s) -> p q s", s=S), scalar=0.25,
                                    in1=causal.unsqueeze(1).broadcast_to([P, NH, S]), op0=ALU.mult, op1=ALU.add)\
              .then_inc(sm["b_scaled"], 1)
            ve.wait_ge(sm["b_scaled"], t + 1)
            ve.tensor_reduce(mx2[:, :], flat(sc2), X, ALU.max).then_inc(sm["b_max"], 1)
            ve.wait_ge(sm["b_max"], t + 1)
            ve.tensor_tensor(flat(sc2), flat(sc2), mx2[:, :].unsqueeze(2).broadcast_to([P, NH, S]), ALU.subtract)\
              .then_inc(sm["b_shift"], 1)

        def normalise(t):
            if not exists(t, TT):
                return
            ve.wait_ge(sm["b_o_made"], t + 1)
            sums = back(t)[:, 0:NH * (DH + 1)].rearrange("p (h d) -> p h d", d=DH + 1)
            ve.reciprocal(inv2[:, :], sums[:, :, DH]).then_inc(sm["b_inv"], 1)
            ve.wait_ge(sm["b_inv"], t + 1)
            ve.tensor_tensor(O2[:, :].rearrange("p (h d) -> p h d", d=DH), sums[:, :, 0:DH],
                             inv2[:, :].unsqueeze(2).broadcast_to([P, NH, DH]), ALU.mult).then_inc(sm["b_o"], 1)

        def spread_probs(t):
            if not exists(t, TT):
                return
            ve.wait_ge(sm["diag_zero"], 1)
            ve.wait_ge(sm["b_pT_made"], t + 1)
            if beyond(t, 1):
                ve.wait_ge(sm["b_o_made"], t)
            for b in range(2, BT):
                last = ve.tensor_copy(PTd[b * S:(b + 1) * S, :, :, b, :].rearrange("p g h s -> p (g h) s"),
                                      back(t)[b * S:(b + 1) * S, :].rearrange("p (gh s) -> p gh s", s=S))
            last.then_inc(sm["b_pT_dve"], 1)

        split_ctx(0, 0)
        split_ctx(1, 1)
        ve.wait_ge(sm["maskb_set"], 1)

        def step(j):
            for u in range(4):
                b = 4 * j + u
                maxima(b, u, 0)
                if u == 0:
                    add_and_norm(j - 3, "c", 0)
                elif u == 1:
                    invert_sums(j - 1)
                elif u == 2:
                    split_cross(j - 1)
                elif u == 3:
                    split_norm(j - 1)
                    normalise(j - 2)
                split_ctx(b + 2, u)
                keep_outputs(b - 2, (u - 2) % 4)
                if u == 0:
                    add_and_norm(j - 3, "c", 1)
                    spread_queries(j - 2)
                elif u == 2:
                    spread_probs(j - 2)
                maxima(b, u, 1)
                if u == 2:
                    add_and_norm(j - 1, "b", 0)
                elif u == 3:
                    rotate(j - 1)
                    split_self(j - 2)
                keep_probs(b - 1, (u - 1) % 4, 0)
                if u == 1:
                    shift_scores(j - 2)
                elif u == 2:
                    add_and_norm(j - 1, "b", 1)
                keep_probs(b - 1, (u - 1) % 4, 1)
                for i in late_weights(j, u):
                    split_weight(i)

        pipeline(step)(ve)

        count = [0]

        def chain(ins):
            ins.then_inc(sm["r_dve"], 1)
            count[0] += 1
            ve.wait_ge(sm["r_dve"], count[0])

        def batch(k):
            t = slice(*BATCHES[k])
            n = t.stop - t.start
            return t, n, (lambda a: a[:, t].unsqueeze(2).broadcast_to([P, n, E])), \
                (lambda a: a.unsqueeze(1).broadcast_to([P, n, E]))

        def shift_logits(k):
            t, n, per_expert, _ = batch(k)
            ve.wait_ge(sm["c_lg"], t.stop)
            chain(ve.tensor_reduce(rmax[:, t], lg[:, t, :], X, ALU.max))
            ve.tensor_tensor(rest[:, t, :], lg[:, t, :], per_expert(rmax), ALU.subtract).then_inc(sm["r_shifted"], 1)

        def gates_of(k):
            t, n, per_expert, _ = batch(k)
            ve.wait_ge(sm["r_exp"], k + 1)
            chain(ve.tensor_reduce(rsum[:, t], eq_[:, t, :], X, ALU.add))
            chain(ve.reciprocal(rinv_[:, t], rsum[:, t]))
            chain(ve.tensor_tensor(gates[:, t, :], eq_[:, t, :], per_expert(rinv_), ALU.mult))

        def choose(k, c):
            t, n, per_expert, per_tile = batch(k)
            src = (gates, rest)[c]
            chain(ve.tensor_reduce(gate[:, c, t], src[:, t, :], X, ALU.max))
            chain(ve.tensor_tensor(eq_[:, t, :], src[:, t, :], per_expert(gate[:, c, :]), ALU.is_equal))
            chain(ve.tensor_tensor(pick[:, t, :], eq_[:, t, :], per_tile(expert_no), ALU.mult))
            chain(ve.tensor_reduce(lowest[:, t], pick[:, t, :], X, ALU.min))
            chain(ve.tensor_tensor(chosen[:, c, t, :], per_tile(expert_no), per_expert(lowest), ALU.is_equal))
            if c == 0:
                chain(ve.tensor_tensor(weighted[:, t, :], chosen[:, 0, t, :], gates[:, t, :], ALU.mult))
                chain(ve.tensor_tensor(rest[:, t, :], gates[:, t, :], weighted[:, t, :], ALU.subtract))
            else:
                ve.sem_inc(sm["r_chosen"], 1)

        def slots_of(k):
            t, n, _, _ = batch(k)
            ve.wait_ge(sm["r_pos_made"], k + 1)
            bank_pos = bk[0][:, 0:3 * n * E].rearrange("p (w t e) -> p w t e", w=3, t=n)
            chain(ve.tensor_scalar(counted[:, t, :], bank_pos[:, 2], float(CAP), None, ALU.min))
            ve.tensor_copy(pos[:, 0, t, :], bank_pos[:, 0])
            chain(ve.tensor_tensor(pos[:, 1, t, :], bank_pos[:, 1], counted[:, t, :], ALU.add))
            chain(ve.tensor_scalar(over[:, :, t, :], pos[:, :, t, :], float(CAP), 1e4, ALU.is_ge, ALU.mult))
            chain(ve.tensor_tensor(over[:, :, t, :], over[:, :, t, :], pos[:, :, t, :], ALU.add))
            chain(ve.tensor_tensor(over[:, :, t, :], over[:, :, t, :],
                                   first_slot.unsqueeze(1).unsqueeze(1).broadcast_to([P, 2, n, E]), ALU.add))
            chain(ve.tensor_tensor(over[:, :, t, :], over[:, :, t, :], chosen[:, :, t, :], ALU.mult))
            chain(ve.tensor_reduce(slot_of[:, :, t], over[:, :, t, :], X, ALU.add))

        def weigh(t):
            ve.tensor_scalar(C_all[:, t, :], slot_no, slot_of[:, 0, t:t + 1], gate[:, 0, t:t + 1], ALU.is_equal, ALU.mult)
            if t >= 2:
                ve.wait_ge(sm["r_both"], t - 1)
            ve.tensor_scalar(second[:, t % 2, :], slot_no, slot_of[:, 1, t:t + 1], gate[:, 1, t:t + 1],
                             ALU.is_equal, ALU.mult).then_inc(sm["r_first"], 1)

        def tokens_of(t):
            ve.wait_ge(sm["r_both"], t + 1)
            if t >= 2:
                ve.wait_ge(sm["r_x_made"], t - 1)
            ve.tensor_scalar(disp[:, t % 2, :], C_all[:, t, :], 0.0, None, ALU.not_equal).then_inc(sm["r_disp"], 1)

        y_, z = TT - 2, TT - 1
        keep_probs(B - 1, (B - 1) % 4, 0)
        add_and_norm(y_ - 1, "c", 0)
        keep_probs(B - 1, (B - 1) % 4, 1)
        keep_outputs(B - 2, (B - 2) % 4)
        add_and_norm(y_ - 1, "c", 1)
        invert_sums(z)
        spread_queries(y_)
        keep_outputs(B - 1, (B - 1) % 4)
        split_cross(z)
        add_and_norm(z, "b", 0)
        add_and_norm(z, "b", 1)
        split_norm(z)
        shift_scores(y_)
        rotate(z)
        shift_logits(0)
        spread_probs(y_)
        gates_of(0)
        choose(0, 0)
        spread_queries(z)
        choose(0, 1)
        slots_of(0)
        shift_scores(z)
        weigh(0)
        weigh(1)
        tokens_of(0)
        normalise(y_)
        split_self(y_)
        tokens_of(1)
        spread_probs(z)
        weigh(2)
        add_and_norm(y_, "c", 0)
        add_and_norm(y_, "c", 1)
        tokens_of(2)
        weigh(3)
        tokens_of(3)
        weigh(4)
        normalise(z)
        split_self(z)
        add_and_norm(z, "c", 0)
        tokens_of(4)
        add_and_norm(z, "c", 1)
        weigh(5)
        tokens_of(5)
        shift_logits(1)
        gates_of(1)
        choose(1, 0)
        choose(1, 1)
        slots_of(1)
        weigh(y_)
        weigh(z)
        tokens_of(y_)
        tokens_of(z)

        def split(half_, n):
            if n >= NT:
                return
            e, t = EQ * half_ + n // HT, n % HT
            w = width(t)
            split_ready(ve, e, t)
            ve.wait_ge(sm["split_act"], done(half_, n))
            wait_freed(ve, "h_made", half_, n, RW)
            ve.tensor_tensor(W01_lo[:, n % RW, :, :, 0:w].rearrange("p i k n -> p (i k) n"),
                             raw01[:, :, :, t * P:t * P + w].rearrange("p i k n -> p (i k) n"),
                             f(W01_hi[:, n % RW, :, :, 0:w]).rearrange("p i k n -> p (i k) n"), ALU.subtract)\
              .then_inc(sm["split_dve"], 1)

        def keep_expert(half_, q):
            ve.wait_ge(sm["y_made"], done(half_, HT * q + HT - 1))
            for g in range(2, 4):
                dst = Y[q * CAP:(q + 1) * CAP, g::4, one(half_), :].rearrange("p h a n -> p (h a) n")
                last = ve.tensor_copy(dst, halves(bk[6 + q % 2][g * CAP:(g + 1) * CAP, :]))
            last.then_inc(sm["y_read_dve"], 1)

        ve.sem_inc(sm["split_dve"], 1)
        ve.sem_inc(sm["h_done"], 1)
        ve.sem_inc(sm["hlo_done"], 1)
        ve.sem_inc(sm["y_read_dve"], 1)
        for n in range(3):
            split(0, n)
        with ve.Fori(0, E // EQ) as half_:
            for n in range(NT):
                w = width(n % HT)
                ve.wait_ge(sm["gelu_done"], done(half_, n))
                wait_freed(ve, "hhi_done", half_, n, RH)
                wait_freed(ve, "hlo_done", half_, n, RH)
                ve.tensor_tensor(hid[0:w, n % RH, :], bk[3 + n % RH][0:w, 0:SL], act[0:w, n % RH, :], ALU.mult)\
                  .then_inc(sm["h_done"], 1)
                split(half_, n + 3)
                ve.wait_ge(sm["hhi_done"], done(half_, n))
                wait_freed(ve, "y_made", half_, n, RW)
                ve.tensor_tensor(hid_lo[0:w, n % RW, :], hid[0:w, n % RH, :], f(hid_hi[0:w, n % RW, :]), ALU.subtract)\
                  .then_inc(sm["hlo_done"], 1)
                if n % HT == 2 and n > HT:
                    keep_expert(half_, n // HT - 1)
            split(half_ + 1, 0)
            keep_expert(half_, EQ - 1)
            split(half_ + 1, 1)
            split(half_ + 1, 2)

        for j in range(TT):
            ve.wait_ge(sm["comb_made"], j + 1)
            if j >= 4:
                ve.wait_ge(sm["out_done"], 16 * 4)
            ve.tensor_tensor(fin[:, j % 4, :], bk[j][:, 0:D], x_sb[:, j, :], ALU.add).then_inc(sm["fin_done"], 1)

    @block_.gpsimd
    def _(po):
        po.wait_ge(sm["ones_set"], 1)
        po.wait_ge(sm["ln1_var"], 1)
        po.tensor_tensor(rstd[:, :], mv[:, :, 1], half[:, :], ALU.pow).then_inc(sm["ln1_rstd"], 1)
        po.wait_ge(sm["const_in"], 16)
        po.wait_ge(sm["bo_in"], 16)
        po.wait_ge(sm["ln1_done"], TT)
        for j in range(TT):
            po.tensor_tensor(x_sb[:, j, :], x_sb[:, j, :], bo_row[:, :], ALU.add).then_inc(sm["xbo_done"], 1)
        po.wait_ge(sm["first_act"], NS)
        po.wait_ge(sm["first_dve"], sum(by_dve))

        def spread(b, r):
            if not exists(b, B):
                return
            if beyond(b, 2):
                po.wait_ge(sm["s_made"], 2 * b - 2)
            for_b = slice(b * S, (b + 1) * S) if isinstance(b, int) else bass.ds(b * S, S)
            po.tensor_tensor(Qb[:, r % 2, :, :, :], QT[:, :, for_b].unsqueeze(2).broadcast_to([P, KH, HG, S]),
                             block.unsqueeze(1).unsqueeze(3).broadcast_to([P, KH, HG, S]), ALU.mult)\
              .then_inc(sm["qb_ready"], 1)
            po.tensor_copy(KT[:, r % 2, :, 2 * P:SC], KLT[:, :, one(b)]).then_inc(sm["kl_ready"], 1)

        def by_head(ap):
            return ap.rearrange("p (h d) -> p h d", d=DH)

        def finish_cross(t):
            if not exists(t, TT):
                return
            if beyond(t, 1):
                po.wait_ge(sm["a_oT_made"], t)
            po.wait_ge(sm["a_inv"], t + 1)
            prob = stat_all[:, one(t), :, 0].rearrange("p a h -> p (a h)")
            po.tensor_tensor(by_head(Ot[:, :]), by_head(tile_of(VL_all, t)), prob.unsqueeze(2).broadcast_to([P, NH, DH]),
                             ALU.mult).then_inc(sm["a_last"], 1)
            po.wait_ge(sm["o_read"], BT * t + BT)
            po.wait_ge(sm["a_last"], t + 1)
            po.tensor_tensor(Ot[:, :], Ot[:, :], tile_of(O_all, t), ALU.add).then_inc(sm["a_add"], 1)
            po.wait_ge(sm["a_add"], t + 1)
            po.tensor_tensor(by_head(Ot[:, :]), by_head(Ot[:, :]), rinv[:, :].unsqueeze(2).broadcast_to([P, NH, DH]),
                             ALU.mult).then_inc(sm["a_norm"], 1)

        def rotate(t):
            if not exists(t, TT):
                return
            po.wait_ge(sm["b_cos"], t + 1)
            po.wait_ge(sm["b_sin"], t + 1)
            po.tensor_tensor(qk[:, :], qk[:, :], qk_s[:, :, :].rearrange("p h d -> p (h d)"), ALU.add).then_inc(sm["b_rope"], 1)

        def power(t, who):
            if not exists(t, TT):
                return
            po.wait_ge(sm[who + "_var"], t + 1)
            po.tensor_tensor(ln_r[who][:, :], ln_mv[who][:, 1:2], half[:, 0:1], ALU.pow).then_inc(sm[who + "_r"], 1)

        def keep_normed(t):
            if not exists(t, TT):
                return
            po.wait_ge(sm["c_y"], t + 1)
            po.sem_inc(sm["turns_po"], 1)
            po.tensor_copy(tile_of(y_hi, t), y2[:, :]).then_inc(sm["c_rounded"], 1)
            po.wait_ge(sm["c_rounded"], t + 1)
            po.tensor_tensor(tile_of(y_lo, t), y2[:, :], f(tile_of(y_hi, t)), ALU.subtract).then_inc(sm["c_kept"], 1)

        spread(0, 0)
        po.wait_ge(sm["xbo_done"], TT)

        def step(j):
            if isinstance(j, int) and j == 1:
                po.wait_ge(sm["w_lo"], 8 - WF)
                po.memset(PTd[:, :, :, :, :], 0.0)
                po.memset(Vs[:, :, :, DH:DH + 1], 1.0).then_inc(sm["diag_zero"], 1)
            for u in range(4):
                spread(4 * j + u + 1, (u + 1) % 4)
                if u == 0:
                    power(j - 3, "c")
                    keep_normed(j - 3)
                elif u == 1:
                    finish_cross(j - 1)
                elif u == 2:
                    power(j - 1, "b")
                elif u == 3:
                    rotate(j - 1)

        pipeline(step)(po)

        def add_choices(t):
            po.wait_ge(sm["r_first"], t + 1)
            po.tensor_tensor(C_all[:, t, :], C_all[:, t, :], second[:, t % 2, :], ALU.add).then_inc(sm["r_both"], 1)

        y_, z = TT - 2, TT - 1
        power(y_ - 1, "c")
        keep_normed(y_ - 1)
        finish_cross(z)
        power(z, "b")
        rotate(z)
        add_choices(0)
        add_choices(1)
        add_choices(2)
        power(y_, "c")
        keep_normed(y_)
        add_choices(3)
        add_choices(4)
        power(z, "c")
        keep_normed(z)
        add_choices(5)
        add_choices(y_)
        add_choices(z)

        po.wait_ge(sm["r_x_kept"], TT)
        po.sem_inc(sm["split_pool"], 1)
        with po.Fori(0, E // EQ) as half_:
            for n in range(NT):
                e, t = EQ * half_ + n // HT, n % HT
                w = width(t)
                split_ready(po, e, t)
                wait_freed(po, "y_made", half_, n, RW)
                po.sem_inc(sm["turns_po"], 1)
                po.tensor_copy(W2_hi[0:w, n % RW, :], raw2[0:w, t, :]).then_inc(sm["hi2"], 1)
                po.wait_ge(sm["hi2"], NT * half_ + n + 1)
                po.tensor_tensor(W2_lo[0:w, n % RW, :], raw2[0:w, t, :], f(W2_hi[0:w, n % RW, :]), ALU.subtract)\
                  .then_inc(sm["split_pool"], 1)


_SQUARE = ["L0_xattn_Wq", "L0_xattn_Wk", "L0_xattn_Wv", "L0_xattn_Wo", "L0_attn_W_Q", "L0_attn_W_K", "L0_attn_W_V",
           "L0_attn_W_O"]
_INS = ["x", "ctx_1024", "mask_1x1xSxS2_ik1", *_SQUARE, "L0_xattn_bq", "L0_xattn_bk", "L0_xattn_bv", "L0_xattn_bo",
        "L0_ffn_router_w", "L0_ffn_w0_kernel", "L0_ffn_w1_kernel", "L0_ffn_wo_kernel"]


def make(nc, arrays):
    ap = {n: nc.dram_tensor(f"in_{n}", a.shape, mybir.dt.from_np(a.dtype), kind="ExternalInput").ap()
          for n, a in arrays.items()}
    out = nc.dram_tensor("out", (B, S, D), F32, kind="ExternalOutput").ap()
    build(nc, ap["x"], ap["ctx_1024"], ap["mask_1x1xSxS2_ik1"], [ap[n] for n in _SQUARE], ap["L0_xattn_bq"],
          ap["L0_xattn_bk"], ap["L0_xattn_bv"], ap["L0_xattn_bo"], ap["L0_ffn_router_w"], ap["L0_ffn_w0_kernel"],
          ap["L0_ffn_w1_kernel"], ap["L0_ffn_wo_kernel"], ap["table"], out)


def kernel(**inputs):
    import numpy as _np
    import concourse.bacc as _bacc
    from concourse.bass_utils import run_bass_kernel_spmd as _run

    nc = _bacc.Bacc("TRN2", target_bir_lowering=False, num_devices=1)
    arrays = {n: _np.ascontiguousarray(inputs[n]) for n in _INS}
    arrays["table"] = constants()
    make(nc, arrays)
    r = _run(nc, [{f"in_{n}": a for n, a in arrays.items()}], core_ids=[0])
    return r.results[0]["out"]
```
